# Optimizing a Trainium2 kernel written in Bass

```python
import numpy as np
import jax
import jax.numpy as jnp

def _softmax(x, axis=-1):
    return jax.nn.softmax(x, axis=axis)

def _gelu(x):
    return jax.nn.gelu(x, approximate=True)

def _silu(x):
    return jax.nn.silu(x)

def _sigmoid(x):
    return jax.nn.sigmoid(x)

def _layernorm(x, axis=-1, eps=1e-05):
    m = jnp.mean(x, axis=axis, keepdims=True)
    v = jnp.var(x, axis=axis, keepdims=True)
    return (x - m) / jnp.sqrt(v + eps)

def _scatter_add(tgt, idx, src, axis=0):
    return tgt.at[idx].add(src)

def _segment_sum(src, seg, n):
    return jax.ops.segment_sum(src, seg, n)
kernel_name = 'mk_decoder_preln_d4_seqx_r8_756765'

def setup_inputs(seed: int=0):
    np.random.seed(seed)
    _w = jnp.asarray

    def _rec_inputs():
        import jax
        import jax.numpy as jnp
        _rk = jax.random.key(seed)
        x = -0.0002928 + 1 * jax.random.normal(jax.random.fold_in(_rk, 1), (2, 512, 128), jnp.float32)
        _lenS = 512 - jax.random.randint(jax.random.fold_in(_rk, 7), (2,), 0, max(1, 512 // 4) + 1, jnp.int32)
        _lenS2 = 77 - jax.random.randint(jax.random.fold_in(_rk, 8), (2,), 0, max(1, 77 // 4) + 1, jnp.int32)
        _ctx_1024P = jax.random.normal(jax.random.fold_in(_rk, 11), (2, 16, 128), jnp.float32)
        _ctx_1024c = jax.random.dirichlet(jax.random.fold_in(_rk, 511), 0.3 * jnp.ones((16,), jnp.float32), (2, 77))
        _ctx_1024t = jnp.einsum('bsk,bkd->bsd', _ctx_1024c, _ctx_1024P)
        _ctx_1024t = _ctx_1024t * jax.lax.rsqrt(jnp.mean(jnp.square(_ctx_1024t)) + 1e-12) * 0.953939
        ctx_1024 = -1.39393e-06 + 0.999914 * (_ctx_1024t + 0.3 * jax.random.normal(jax.random.fold_in(_rk, 611), (2, 77, 128), jnp.float32))
        fside_BxSxS2_0 = -1.47943e-05 + 1.00017 * jax.random.normal(jax.random.fold_in(_rk, 13), (2, 512, 77), jnp.float32)
        _validS = jnp.arange(512)[None, :] < _lenS[:, None]
        _validS2 = jnp.arange(77)[None, :] < _lenS2[:, None]
        _causal = jnp.tril(jnp.ones((512, 512), dtype=bool))
        mask_1x1xSxS2_if1 = jnp.where(jnp.ones((1, 1, 512, 77), dtype=bool), 1, 0).astype(jnp.int32)
        mask_BxS2_bf0 = jnp.logical_not(jnp.ones((2, 77), dtype=bool))
        return (x, ctx_1024, fside_BxSxS2_0, mask_1x1xSxS2_if1, mask_BxS2_bf0)
    x, ctx_1024, fside_BxSxS2_0, mask_1x1xSxS2_if1, mask_BxS2_bf0 = _rec_inputs()

    def _L0_attn_setup():
        import jax, jax.numpy as jnp
        import numpy as np
        E = 128
        H = 16
        HD = E // H
        R = 8
        T, B = (256, 2)

        def _dora_linear(x, m, V, A, Bm, b):
            Vu = V + Bm @ A
            W = m / (jnp.linalg.norm(Vu) + 1e-08) * Vu
            return x @ W.T + b
        key = jax.random.key(seed)
        ks = jax.random.split(key, 16)
        query = jax.random.normal(ks[0], (T, B, E), dtype=jnp.float32)
        kk = jax.random.normal(ks[1], (T, B, E), dtype=jnp.float32)
        vv = jax.random.normal(ks[2], (T, B, E), dtype=jnp.float32)

        def make_dora(k1, k2, k3, k4):
            w = jax.random.normal(k1, (E, E), dtype=jnp.float32) * E ** (-0.5)
            m = jnp.linalg.norm(w)
            V = w / m
            A = jax.random.normal(k2, (R, E), dtype=jnp.float32) * E ** (-0.5)
            Bm = jax.random.normal(k3, (E, R), dtype=jnp.float32) * 0.01
            b = jax.random.normal(k4, (E,), dtype=jnp.float32) * 0.01
            return (m, V, A, Bm, b)
        mag_q, dir_q, A_q, B_q, bias_q = make_dora(ks[3], ks[4], ks[5], ks[6])
        mag_v, dir_v, A_v, B_v, bias_v = make_dora(ks[7], ks[8], ks[9], ks[10])
        k_w = jax.random.normal(ks[11], (E, E), dtype=jnp.float32) * E ** (-0.5)
        k_b = jax.random.normal(ks[12], (E,), dtype=jnp.float32) * 0.01
        out_w = jax.random.normal(ks[13], (E, E), dtype=jnp.float32) * E ** (-0.5)
        out_b = jax.random.normal(ks[14], (E,), dtype=jnp.float32) * 0.01
        return dict(query=query, key=kk, value=vv, mag_q=mag_q, dir_q=dir_q, A_q=A_q, B_q=B_q, bias_q=bias_q, mag_v=mag_v, dir_v=dir_v, A_v=A_v, B_v=B_v, bias_v=bias_v, k_w=k_w, k_b=k_b, out_w=out_w, out_b=out_b)
    _L0_attn_all = _L0_attn_setup()
    _L0_attn_in = {k: v for k, v in _L0_attn_all.items() if k in ('key', 'value', 'mag_q', 'dir_q', 'A_q', 'B_q', 'bias_q', 'mag_v', 'dir_v', 'A_v', 'B_v', 'bias_v', 'k_w', 'k_b', 'out_w', 'out_b')}
    del _L0_attn_all

    def _L0_xattn_setup():
        import jax, jax.numpy as jnp
        import numpy as np
        D_MODEL = 128
        HEADS = 16
        D_K = D_MODEL // HEADS
        B, S = (2, 256)
        NEG = -1000000000.0
        key = jax.random.key(seed)
        ks = jax.random.split(key, 7)
        Query = jax.random.normal(ks[0], (B, S, D_MODEL), dtype=jnp.float32)
        Key = jax.random.normal(ks[1], (B, S, D_MODEL), dtype=jnp.float32)
        Value = jax.random.normal(ks[2], (B, S, D_MODEL), dtype=jnp.float32)
        mask = jnp.ones((1, 1, S, S), dtype=jnp.int32)
        sc = 1.0 / np.sqrt(D_MODEL)
        W_q = jax.random.normal(ks[3], (D_MODEL, D_MODEL), dtype=jnp.float32) * sc
        W_k = jax.random.normal(ks[4], (D_MODEL, D_MODEL), dtype=jnp.float32) * sc
        W_v = jax.random.normal(ks[5], (D_MODEL, D_MODEL), dtype=jnp.float32) * sc
        W_o = jax.random.normal(ks[6], (D_MODEL, D_MODEL), dtype=jnp.float32) * sc
        return {'Query': Query, 'Key': Key, 'Value': Value, 'mask': mask, 'W_q': W_q, 'W_k': W_k, 'W_v': W_v, 'W_o': W_o}
    _L0_xattn_all = _L0_xattn_setup()
    _L0_xattn_in = {k: v for k, v in _L0_xattn_all.items() if k in ('W_q', 'W_k', 'W_v', 'W_o')}
    del _L0_xattn_all

    def _L0_ffn_setup():
        import jax, jax.numpy as jnp
        import numpy as np
        from jax import lax
        HIDDEN = 128
        INTER = 64
        E = 64
        K = 6
        G = 8
        TG = 4
        NSH = 2
        ISH = INTER * NSH

        def _moe_forward(hidden_states, gate_w, gate_bias, eg_w, eu_w, ed_w, sg_w, su_w, sd_w):
            B, S, H = hidden_states.shape
            x = hidden_states.reshape(-1, H)
            T = x.shape[0]
            shared = jax.nn.silu(x @ sg_w.T) * (x @ su_w.T) @ sd_w.T
            logits = x @ gate_w.T
            scores = jax.nn.sigmoid(logits) + gate_bias
            group_scores = scores.reshape(T, G, E // G).max(axis=-1)
            _, sel_groups = lax.top_k(group_scores, TG)
            group_mask = jnp.zeros((T, G), scores.dtype).at[jnp.arange(T)[:, None], sel_groups].set(1.0)
            mask = jnp.repeat(group_mask, E // G, axis=1)
            masked_scores = scores * mask
            topk_w, topk_i = lax.top_k(masked_scores, K)
            topk_w = topk_w / (topk_w.sum(axis=-1, keepdims=True) + 1e-08)
            comb = jnp.zeros((T, E), x.dtype).at[jnp.arange(T)[:, None], topk_i].add(topk_w)
            h = jax.nn.silu(jnp.einsum('th,eih->eti', x, eg_w)) * jnp.einsum('th,eih->eti', x, eu_w)
            routed = jnp.einsum('eti,ehi,te->th', h, ed_w, comb)
            return (shared + routed).reshape(B, S, H)
        key = jax.random.key(seed)
        ks = jax.random.split(key, 9)
        s = 0.02
        return {'hidden_states': jax.random.normal(ks[0], (1, 128, HIDDEN), jnp.float32), 'gate_w': jax.random.normal(ks[1], (E, HIDDEN), jnp.float32) * s, 'gate_bias': jnp.zeros((E,), jnp.float32), 'eg_w': jax.random.normal(ks[2], (E, INTER, HIDDEN), jnp.float32) * s, 'eu_w': jax.random.normal(ks[3], (E, INTER, HIDDEN), jnp.float32) * s, 'ed_w': jax.random.normal(ks[4], (E, HIDDEN, INTER), jnp.float32) * s, 'sg_w': jax.random.normal(ks[5], (ISH, HIDDEN), jnp.float32) * s, 'su_w': jax.random.normal(ks[6], (ISH, HIDDEN), jnp.float32) * s, 'sd_w': jax.random.normal(ks[7], (HIDDEN, ISH), jnp.float32) * s}
    _L0_ffn_all = _L0_ffn_setup()
    _L0_ffn_in = {k: v for k, v in _L0_ffn_all.items() if k in ('gate_w', 'gate_bias', 'eg_w', 'eu_w', 'ed_w', 'sg_w', 'su_w', 'sd_w')}
    del _L0_ffn_all

    def _L1_attn_setup():
        import jax, jax.numpy as jnp
        import numpy as np
        N_HEAD = 16
        EPS = 1e-06

        def _rotate_half(x):
            d = x.shape[-1] // 2
            return jnp.concatenate((-x[..., d:], x[..., :d]), axis=-1)

        def _rms_norm(x, w, eps=EPS):
            d = x.shape[-1]
            rms = jnp.linalg.norm(x, axis=-1, keepdims=True) * d ** (-0.5)
            return w * (x / (rms + eps))
        key = jax.random.key(seed)
        ks = jax.random.split(key, 3)
        B, T, C = (4, 256, 128)
        x = jax.random.normal(ks[0], (B, T, C), dtype=jnp.float32)
        W_kqv = jax.random.normal(ks[1], (3 * C, C), dtype=jnp.float32) * C ** (-0.5)
        W_proj = jax.random.normal(ks[2], (C, C), dtype=jnp.float32) * C ** (-0.5)
        D = C // N_HEAD
        q_norm_w = jnp.ones((D,), dtype=jnp.float32)
        k_norm_w = jnp.ones((D,), dtype=jnp.float32)
        return {'x': x, 'W_kqv': W_kqv, 'W_proj': W_proj, 'q_norm_w': q_norm_w, 'k_norm_w': k_norm_w}
    _L1_attn_all = _L1_attn_setup()
    _L1_attn_in = {k: v for k, v in _L1_attn_all.items() if k in ('W_kqv', 'W_proj', 'q_norm_w', 'k_norm_w')}
    del _L1_attn_all

    def _L1_xattn_setup():
        import jax, jax.numpy as jnp
        import numpy as np
        DIM = 128
        HEADS = 16
        HEAD_DIM = DIM // HEADS
        SCALE = HEAD_DIM ** (-0.5)
        key = jax.random.key(seed)
        ks = jax.random.split(key, 6)
        B, Nq, Nkv = (2, 128, 256)
        s = DIM ** (-0.5)
        return {'x': jax.random.normal(ks[0], (B, Nq, DIM), jnp.float32), 'mem': jax.random.normal(ks[1], (B, Nkv, DIM), jnp.float32), 'W_kv': jax.random.normal(ks[2], (DIM, 2 * DIM), jnp.float32) * s, 'W_q': jax.random.normal(ks[3], (DIM, DIM), jnp.float32) * s, 'W_proj': jax.random.normal(ks[4], (DIM, DIM), jnp.float32) * s, 'b_proj': jax.random.normal(ks[5], (DIM,), jnp.float32) * 0.01}
    _L1_xattn_all = _L1_xattn_setup()
    _L1_xattn_in = {k: v for k, v in _L1_xattn_all.items() if k in ('W_kv', 'W_q', 'W_proj', 'b_proj')}
    del _L1_xattn_all

    def _L1_ffn_setup():
        import jax, jax.numpy as jnp
        import numpy as np
        B, N, D, F, E, K = (4, 256, 128, 512, 16, 2)
        EPS = 1e-05
        key = jax.random.key(seed)
        ks = jax.random.split(key, 6)
        scaled = lambda k, shape, fan: jax.random.normal(k, shape, jnp.float32) / np.float32(np.sqrt(fan))
        return {'x': jax.random.normal(ks[0], (B, N, D), jnp.float32), 'Wr': scaled(ks[1], (D, E), D), 'br': jnp.zeros((E,), jnp.float32), 'W1': scaled(ks[2], (E, D, F), D), 'W3': scaled(ks[3], (E, D, F), D), 'W2': scaled(ks[4], (E, F, D), F), 'gamma': jnp.ones((E, D), jnp.float32), 'beta': jnp.zeros((E, D), jnp.float32)}
    _L1_ffn_all = _L1_ffn_setup()
    _L1_ffn_in = {k: v for k, v in _L1_ffn_all.items() if k in ('Wr', 'br', 'W1', 'W3', 'W2', 'gamma', 'beta')}
    del _L1_ffn_all

    def _L2_attn_setup():
        import jax, jax.numpy as jnp
        import numpy as np
        D_STATE = 16
        D_CONV = 4

        def silu(x):
            return x * jax.nn.sigmoid(x)

        def _reference_tuple_inner(x, in_w, in_b, conv_w, conv_b, xp_w, xp_b, out_w, out_b):
            B, S, D = x.shape
            h = x @ in_w.T + in_b
            hc = jax.lax.conv_general_dilated(h.transpose(0, 2, 1), conv_w, window_strides=(1,), padding=[(D_CONV - 1, 0)], feature_group_count=conv_w.shape[0], dimension_numbers=('NCH', 'OIH', 'NCH')) + conv_b[None, :, None]
            h = silu(hc.transpose(0, 2, 1))
            xp = h @ xp_w.T + xp_b
            a = jnp.exp(-jnp.exp(xp[..., :D_STATE]))
            b = silu(xp[..., D_STATE:]) * jnp.sum(h, axis=-1, keepdims=True)

            def step(state, ab):
                a_t, b_t = ab
                state = state * a_t + b_t
                return (state, state)
            init = jnp.zeros((B, D_STATE), x.dtype)
            final_state, ys = jax.lax.scan(step, init, (a.transpose(1, 0, 2), b.transpose(1, 0, 2)))
            out = ys.transpose(1, 0, 2) @ out_w.T + out_b
            return (out, final_state)
        key = jax.random.key(seed)
        ks = jax.random.split(key, 9)
        B, S, D = (8, 512, 128)
        DI = 2 * D

        def w(k, shape, fan_in):
            bound = 1.0 / np.sqrt(fan_in)
            return jax.random.uniform(k, shape, jnp.float32, -bound, bound)
        return {'x': jax.random.normal(ks[0], (B, S, D), jnp.float32), 'in_w': w(ks[1], (DI, D), D), 'in_b': w(ks[2], (DI,), D), 'conv_w': w(ks[3], (DI, 1, D_CONV), D_CONV), 'conv_b': w(ks[4], (DI,), D_CONV), 'xp_w': w(ks[5], (2 * D_STATE, DI), DI), 'xp_b': w(ks[6], (2 * D_STATE,), DI), 'out_w': w(ks[7], (D, D_STATE), D_STATE), 'out_b': w(ks[8], (D,), D_STATE)}
    _L2_attn_all = _L2_attn_setup()
    _L2_attn_in = {k: v for k, v in _L2_attn_all.items() if k in ('in_w', 'in_b', 'conv_w', 'conv_b', 'xp_w', 'xp_b', 'out_w', 'out_b')}
    del _L2_attn_all

    def _L2_xattn_setup():
        import jax, jax.numpy as jnp
        import numpy as np
        key = jax.random.key(seed)
        ks = jax.random.split(key, 8)
        B, T, D, H = (4, 256, 128, 16)
        s_in = float(np.sqrt(2.0 / (D + 3 * D)))
        s_out = float(np.sqrt(2.0 / (D + D)))
        return {'query': jax.random.normal(ks[0], (B, T, D), jnp.float32), 'key': jax.random.normal(ks[1], (B, T, D), jnp.float32), 'value': jax.random.normal(ks[2], (B, T, D), jnp.float32), 'attention_bias': jax.random.normal(ks[3], (B, T, T), jnp.float32), 'in_proj_weight': jax.random.normal(ks[4], (3 * D, D), jnp.float32) * s_in, 'in_proj_bias': jnp.zeros((3 * D,), jnp.float32), 'out_w': jax.random.normal(ks[5], (D, D), jnp.float32) * s_out, 'out_b': jnp.zeros((D,), jnp.float32), 'head_scales': jnp.ones((H,), jnp.float32) + 0.1 * jax.random.normal(ks[6], (H,), jnp.float32), 'key_padding_mask': jnp.zeros((B, T), bool)}
    _L2_xattn_all = _L2_xattn_setup()
    _L2_xattn_in = {k: v for k, v in _L2_xattn_all.items() if k in ('in_proj_weight', 'in_proj_bias', 'out_w', 'out_b', 'head_scales')}
    del _L2_xattn_all

    def _L2_ffn_setup():
        import jax, jax.numpy as jnp
        import numpy as np
        CAPACITY_FACTOR = 1.0

        def _top1_gate(x2d, wg):
            S, _ = x2d.shape
            E = wg.shape[1]
            C = int(CAPACITY_FACTOR * S / E)
            logits = x2d @ wg
            gates = jax.nn.softmax(logits, axis=-1)
            idx = jnp.argmax(gates, axis=-1)
            mask = jax.nn.one_hot(idx, E, dtype=jnp.int32)
            loc = jnp.cumsum(mask, axis=0) - 1
            me = jnp.mean(gates, axis=0)
            ce = jnp.mean(mask.astype(gates.dtype), axis=0)
            l_aux = E * jnp.sum(me * ce)
            mask = mask * (loc < C).astype(jnp.int32)
            gate_s = jnp.sum(gates * mask, axis=-1)
            loc_s = jnp.sum(loc * mask, axis=-1)
            loc_oh = jax.nn.one_hot(loc_s, C, dtype=gates.dtype)
            combine = (gate_s[:, None] * mask.astype(gates.dtype))[:, :, None] * loc_oh[:, None, :]
            dispatch = (combine > 0).astype(gates.dtype)
            return (l_aux, combine, dispatch)
        key = jax.random.key(seed)
        k1, k2, k3, k4 = jax.random.split(key, 4)
        s, b, m, E, ffn = (256, 4, 128, 8, 512)
        x = jax.random.normal(k1, (s, b, m), dtype=jnp.float32)
        wg = jax.random.normal(k2, (m, E), dtype=jnp.float32) * 0.02
        w1 = jax.random.normal(k3, (E, m, ffn), dtype=jnp.float32) * 0.02
        w2 = jax.random.normal(k4, (E, ffn, m), dtype=jnp.float32) * 0.02
        return {'x': x, 'wg': wg, 'w1': w1, 'w2': w2}
    _L2_ffn_all = _L2_ffn_setup()
    _L2_ffn_in = {k: v for k, v in _L2_ffn_all.items() if k in ('wg', 'w1', 'w2')}
    del _L2_ffn_all

    def _L3_attn_setup():
        import jax, jax.numpy as jnp
        import numpy as np
        D_MODEL = 128
        N_HEADS = 16
        HEAD_DIM = D_MODEL // N_HEADS
        MAX_SHIFT = HEAD_DIM // 2
        BATCH, SEQ = (2, 256)

        def _forward(x, Wq, bq, Wk, bk, Wv, bv, Wo, bo, W_cross, shift_weights, gate):
            b, s, _ = x.shape
            H, hd = (W_cross.shape[0], W_cross.shape[1])
            ms = shift_weights.shape[1]
            Q = (x @ Wq.T + bq).reshape(b, s, H, hd)
            K = (x @ Wk.T + bk).reshape(b, s, H, hd)
            V = (x @ Wv.T + bv).reshape(b, s, H, hd)
            Qt = jnp.einsum('bqhf,hfg->bqhg', Q, W_cross)
            scores_cross = jnp.einsum('bqhd,bkhd->bhqk', Qt, K)
            f = jnp.arange(hd)[:, None]
            g = jnp.arange(hd)[None, :]
            tau = g - f
            valid = (tau >= 0) & (tau < ms)
            M = jnp.where(valid[None], shift_weights[:, jnp.clip(tau, 0, ms - 1)], 0.0)
            K_mixed = jnp.einsum('hfg,bkhg->bkhf', M, K)
            scores_conv = jnp.einsum('bqhf,bkhf->bhqk', Q, K_mixed)
            gt = jax.nn.sigmoid(gate).reshape(1, H, 1, 1)
            scale = hd ** (-0.5)
            scores = (gt * scores_cross + (1.0 - gt) * scores_conv) * scale
            causal = jnp.tril(jnp.ones((s, s), dtype=bool))
            scores = jnp.where(causal[None, None], scores, -jnp.inf)
            attn = jax.nn.softmax(scores, axis=-1)
            out = jnp.einsum('bhqk,bkhd->bqhd', attn, V).reshape(b, s, H * hd)
            return out @ Wo.T + bo
        key = jax.random.key(seed)
        ks = jax.random.split(key, 12)
        s = 0.02
        x = jax.random.normal(ks[0], (BATCH, SEQ, D_MODEL), dtype=jnp.float32)
        Wq = jax.random.normal(ks[1], (D_MODEL, D_MODEL), dtype=jnp.float32) * s
        bq = jnp.zeros((D_MODEL,), jnp.float32)
        Wk = jax.random.normal(ks[2], (D_MODEL, D_MODEL), dtype=jnp.float32) * s
        bk = jnp.zeros((D_MODEL,), jnp.float32)
        Wv = jax.random.normal(ks[3], (D_MODEL, D_MODEL), dtype=jnp.float32) * s
        bv = jnp.zeros((D_MODEL,), jnp.float32)
        Wo = jax.random.normal(ks[4], (D_MODEL, D_MODEL), dtype=jnp.float32) * s
        bo = jnp.zeros((D_MODEL,), jnp.float32)
        eye = jnp.broadcast_to(jnp.eye(HEAD_DIM, dtype=jnp.float32), (N_HEADS, HEAD_DIM, HEAD_DIM))
        W_cross = eye + 0.01 * jax.random.normal(ks[5], (N_HEADS, HEAD_DIM, HEAD_DIM), dtype=jnp.float32)
        decay = jnp.exp(-jnp.arange(MAX_SHIFT, dtype=jnp.float32) / (MAX_SHIFT / 4.0))
        shift_weights = jnp.broadcast_to(decay, (N_HEADS, MAX_SHIFT)).copy()
        gate = jnp.zeros((N_HEADS,), jnp.float32)
        return {'x': x, 'Wq': Wq, 'bq': bq, 'Wk': Wk, 'bk': bk, 'Wv': Wv, 'bv': bv, 'Wo': Wo, 'bo': bo, 'W_cross': W_cross, 'shift_weights': shift_weights, 'gate': gate}
    _L3_attn_all = _L3_attn_setup()
    _L3_attn_in = {k: v for k, v in _L3_attn_all.items() if k in ('Wq', 'bq', 'Wk', 'bk', 'Wv', 'bv', 'Wo', 'bo', 'W_cross', 'shift_weights', 'gate')}
    del _L3_attn_all

    def _L3_xattn_setup():
        import jax, jax.numpy as jnp
        import numpy as np
        DIM = 128
        NUM_HEADS = 16
        HEAD_DIM = DIM // NUM_HEADS
        SCALE = HEAD_DIM ** (-0.5)
        EPS = 1e-05

        def layernorm(x, gamma, beta):
            mu = jnp.mean(x, axis=-1, keepdims=True)
            var = jnp.mean(jnp.square(x - mu), axis=-1, keepdims=True)
            return (x - mu) * jax.lax.rsqrt(var + EPS) * gamma + beta
        key = jax.random.key(seed)
        ks = jax.random.split(key, 12)
        B, Lq, Lk = (2, 256, 256)
        s = 0.02
        return {'q': jax.random.normal(ks[0], (B, Lq, DIM), jnp.float32), 'k': jax.random.normal(ks[1], (B, Lk, DIM), jnp.float32), 'v': jax.random.normal(ks[2], (B, Lk, DIM), jnp.float32), 'Wq': jax.random.normal(ks[3], (DIM, DIM), jnp.float32) * s, 'Wk': jax.random.normal(ks[4], (DIM, DIM), jnp.float32) * s, 'Wv': jax.random.normal(ks[5], (DIM, DIM), jnp.float32) * s, 'gq': jnp.ones((HEAD_DIM,), jnp.float32), 'bq': jnp.zeros((HEAD_DIM,), jnp.float32), 'gk': jnp.ones((HEAD_DIM,), jnp.float32), 'bk': jnp.zeros((HEAD_DIM,), jnp.float32), 'Wo': jax.random.normal(ks[6], (DIM, DIM), jnp.float32) * s, 'bo': jnp.zeros((DIM,), jnp.float32)}
    _L3_xattn_all = _L3_xattn_setup()
    _L3_xattn_in = {k: v for k, v in _L3_xattn_all.items() if k in ('Wq', 'Wk', 'Wv', 'gq', 'bq', 'gk', 'bk', 'Wo', 'bo')}
    del _L3_xattn_all

    def _L3_ffn_setup():
        import jax, jax.numpy as jnp
        import numpy as np
        key = jax.random.key(seed)
        k1, k2, k3, k4, k5 = jax.random.split(key, 5)
        d_in, d_out, r = (128, 128, 32)
        x = jax.random.normal(k1, (8, 1024, d_in), dtype=jnp.float32)
        W = jax.random.normal(k2, (d_out, d_in), dtype=jnp.float32) * (1.0 / np.sqrt(d_in))
        b = jax.random.normal(k3, (d_out,), dtype=jnp.float32) * 0.01
        V_r = jax.random.normal(k4, (d_in, r), dtype=jnp.float32) * (1.0 / np.sqrt(d_in))
        C = jax.random.normal(k5, (d_out, r), dtype=jnp.float32) * (1.0 / np.sqrt(r))
        return {'x': x, 'W': W, 'b': b, 'V_r': V_r, 'C': C}
    _L3_ffn_all = _L3_ffn_setup()
    _L3_ffn_in = {k: v for k, v in _L3_ffn_all.items() if k in ('W', 'b', 'V_r', 'C')}
    del _L3_ffn_all
    return {'x': x, 'ctx_1024': ctx_1024, 'fside_BxSxS2_0': fside_BxSxS2_0, 'mask_1x1xSxS2_if1': mask_1x1xSxS2_if1, 'mask_BxS2_bf0': mask_BxS2_bf0, 'L0_attn_key': _L0_attn_in['key'], 'L0_attn_value': _L0_attn_in['value'], 'L0_attn_mag_q': _L0_attn_in['mag_q'], 'L0_attn_dir_q': _L0_attn_in['dir_q'], 'L0_attn_A_q': _L0_attn_in['A_q'], 'L0_attn_B_q': _L0_attn_in['B_q'], 'L0_attn_bias_q': _L0_attn_in['bias_q'], 'L0_attn_mag_v': _L0_attn_in['mag_v'], 'L0_attn_dir_v': _L0_attn_in['dir_v'], 'L0_attn_A_v': _L0_attn_in['A_v'], 'L0_attn_B_v': _L0_attn_in['B_v'], 'L0_attn_bias_v': _L0_attn_in['bias_v'], 'L0_attn_k_w': _L0_attn_in['k_w'], 'L0_attn_k_b': _L0_attn_in['k_b'], 'L0_attn_out_w': _L0_attn_in['out_w'], 'L0_attn_out_b': _L0_attn_in['out_b'], 'L0_xattn_W_q': _L0_xattn_in['W_q'], 'L0_xattn_W_k': _L0_xattn_in['W_k'], 'L0_xattn_W_v': _L0_xattn_in['W_v'], 'L0_xattn_W_o': _L0_xattn_in['W_o'], 'L0_ffn_gate_w': _L0_ffn_in['gate_w'], 'L0_ffn_gate_bias': _L0_ffn_in['gate_bias'], 'L0_ffn_eg_w': _L0_ffn_in['eg_w'], 'L0_ffn_eu_w': _L0_ffn_in['eu_w'], 'L0_ffn_ed_w': _L0_ffn_in['ed_w'], 'L0_ffn_sg_w': _L0_ffn_in['sg_w'], 'L0_ffn_su_w': _L0_ffn_in['su_w'], 'L0_ffn_sd_w': _L0_ffn_in['sd_w'], 'L1_attn_W_kqv': _L1_attn_in['W_kqv'], 'L1_attn_W_proj': _L1_attn_in['W_proj'], 'L1_attn_q_norm_w': _L1_attn_in['q_norm_w'], 'L1_attn_k_norm_w': _L1_attn_in['k_norm_w'], 'L1_xattn_W_kv': _L1_xattn_in['W_kv'], 'L1_xattn_W_q': _L1_xattn_in['W_q'], 'L1_xattn_W_proj': _L1_xattn_in['W_proj'], 'L1_xattn_b_proj': _L1_xattn_in['b_proj'], 'L1_ffn_Wr': _L1_ffn_in['Wr'], 'L1_ffn_br': _L1_ffn_in['br'], 'L1_ffn_W1': _L1_ffn_in['W1'], 'L1_ffn_W3': _L1_ffn_in['W3'], 'L1_ffn_W2': _L1_ffn_in['W2'], 'L1_ffn_gamma': _L1_ffn_in['gamma'], 'L1_ffn_beta': _L1_ffn_in['beta'], 'L2_attn_in_w': _L2_attn_in['in_w'], 'L2_attn_in_b': _L2_attn_in['in_b'], 'L2_attn_conv_w': _L2_attn_in['conv_w'], 'L2_attn_conv_b': _L2_attn_in['conv_b'], 'L2_attn_xp_w': _L2_attn_in['xp_w'], 'L2_attn_xp_b': _L2_attn_in['xp_b'], 'L2_attn_out_w': _L2_attn_in['out_w'], 'L2_attn_out_b': _L2_attn_in['out_b'], 'L2_xattn_in_proj_weight': _L2_xattn_in['in_proj_weight'], 'L2_xattn_in_proj_bias': _L2_xattn_in['in_proj_bias'], 'L2_xattn_out_w': _L2_xattn_in['out_w'], 'L2_xattn_out_b': _L2_xattn_in['out_b'], 'L2_xattn_head_scales': _L2_xattn_in['head_scales'], 'L2_ffn_wg': _L2_ffn_in['wg'], 'L2_ffn_w1': _L2_ffn_in['w1'], 'L2_ffn_w2': _L2_ffn_in['w2'], 'L3_attn_Wq': _L3_attn_in['Wq'], 'L3_attn_bq': _L3_attn_in['bq'], 'L3_attn_Wk': _L3_attn_in['Wk'], 'L3_attn_bk': _L3_attn_in['bk'], 'L3_attn_Wv': _L3_attn_in['Wv'], 'L3_attn_bv': _L3_attn_in['bv'], 'L3_attn_Wo': _L3_attn_in['Wo'], 'L3_attn_bo': _L3_attn_in['bo'], 'L3_attn_W_cross': _L3_attn_in['W_cross'], 'L3_attn_shift_weights': _L3_attn_in['shift_weights'], 'L3_attn_gate': _L3_attn_in['gate'], 'L3_xattn_Wq': _L3_xattn_in['Wq'], 'L3_xattn_Wk': _L3_xattn_in['Wk'], 'L3_xattn_Wv': _L3_xattn_in['Wv'], 'L3_xattn_gq': _L3_xattn_in['gq'], 'L3_xattn_bq': _L3_xattn_in['bq'], 'L3_xattn_gk': _L3_xattn_in['gk'], 'L3_xattn_bk': _L3_xattn_in['bk'], 'L3_xattn_Wo': _L3_xattn_in['Wo'], 'L3_xattn_bo': _L3_xattn_in['bo'], 'L3_ffn_W': _L3_ffn_in['W'], 'L3_ffn_b': _L3_ffn_in['b'], 'L3_ffn_V_r': _L3_ffn_in['V_r'], 'L3_ffn_C': _L3_ffn_in['C']}

def reference(x, ctx_1024, fside_BxSxS2_0, mask_1x1xSxS2_if1, mask_BxS2_bf0, L0_attn_key, L0_attn_value, L0_attn_mag_q, L0_attn_dir_q, L0_attn_A_q, L0_attn_B_q, L0_attn_bias_q, L0_attn_mag_v, L0_attn_dir_v, L0_attn_A_v, L0_attn_B_v, L0_attn_bias_v, L0_attn_k_w, L0_attn_k_b, L0_attn_out_w, L0_attn_out_b, L0_xattn_W_q, L0_xattn_W_k, L0_xattn_W_v, L0_xattn_W_o, L0_ffn_gate_w, L0_ffn_gate_bias, L0_ffn_eg_w, L0_ffn_eu_w, L0_ffn_ed_w, L0_ffn_sg_w, L0_ffn_su_w, L0_ffn_sd_w, L1_attn_W_kqv, L1_attn_W_proj, L1_attn_q_norm_w, L1_attn_k_norm_w, L1_xattn_W_kv, L1_xattn_W_q, L1_xattn_W_proj, L1_xattn_b_proj, L1_ffn_Wr, L1_ffn_br, L1_ffn_W1, L1_ffn_W3, L1_ffn_W2, L1_ffn_gamma, L1_ffn_beta, L2_attn_in_w, L2_attn_in_b, L2_attn_conv_w, L2_attn_conv_b, L2_attn_xp_w, L2_attn_xp_b, L2_attn_out_w, L2_attn_out_b, L2_xattn_in_proj_weight, L2_xattn_in_proj_bias, L2_xattn_out_w, L2_xattn_out_b, L2_xattn_head_scales, L2_ffn_wg, L2_ffn_w1, L2_ffn_w2, L3_attn_Wq, L3_attn_bq, L3_attn_Wk, L3_attn_bk, L3_attn_Wv, L3_attn_bv, L3_attn_Wo, L3_attn_bo, L3_attn_W_cross, L3_attn_shift_weights, L3_attn_gate, L3_xattn_Wq, L3_xattn_Wk, L3_xattn_Wv, L3_xattn_gq, L3_xattn_bq, L3_xattn_gk, L3_xattn_bk, L3_xattn_Wo, L3_xattn_bo, L3_ffn_W, L3_ffn_b, L3_ffn_V_r, L3_ffn_C):
    import jax
    import jax.numpy as jnp

    def _L0_attn_ref(query, key, value, mag_q, dir_q, A_q, B_q, bias_q, mag_v, dir_v, A_v, B_v, bias_v, k_w, k_b, out_w, out_b):
        import jax, jax.numpy as jnp
        import numpy as np
        E = 128
        H = 16
        HD = E // H
        R = 8
        T, B = (256, 2)

        def _dora_linear(x, m, V, A, Bm, b):
            Vu = V + Bm @ A
            W = m / (jnp.linalg.norm(Vu) + 1e-08) * Vu
            return x @ W.T + b
        Tq, Bq, _ = query.shape
        q = _dora_linear(query, mag_q, dir_q, A_q, B_q, bias_q)
        k = query @ k_w.T + k_b
        v = _dora_linear(query, mag_v, dir_v, A_v, B_v, bias_v)
        q = q.reshape(Tq, Bq * H, HD).transpose(1, 0, 2)
        k = k.reshape(Tq, Bq * H, HD).transpose(1, 0, 2)
        v = v.reshape(Tq, Bq * H, HD).transpose(1, 0, 2)
        scale = HD ** (-0.5)
        attn = jnp.einsum('nqd,nkd->nqk', q, k) * scale
        attn = jax.nn.softmax(attn, axis=-1)
        out = jnp.einsum('nqk,nkd->nqd', attn, v)
        out = out.transpose(1, 0, 2).reshape(Tq, Bq, E)
        out = out @ out_w.T + out_b
        return out

    def _L0_xattn_ref(Query, Key, Value, mask, W_q, W_k, W_v, W_o):
        import jax, jax.numpy as jnp
        import numpy as np
        D_MODEL = 128
        HEADS = 16
        D_K = D_MODEL // HEADS
        B, S = (2, 256)
        NEG = -1000000000.0

        def split_heads(x):
            b, s, _ = x.shape
            return x.reshape(b, s, HEADS, D_K).transpose(0, 2, 1, 3)
        Q = split_heads(Query @ W_q.T)
        K = split_heads(Key @ W_k.T)
        V = split_heads(Value @ W_v.T)
        scores = jnp.einsum('bhqd,bhkd->bhqk', Q, K) / jnp.sqrt(jnp.asarray(D_K, dtype=Q.dtype))
        scores = jnp.where(mask == 0, jnp.asarray(NEG, dtype=scores.dtype), scores)
        attn = jax.nn.softmax(scores, axis=-1)
        X = jnp.einsum('bhqk,bhkd->bhqd', attn, V)
        X = X.transpose(0, 2, 1, 3).reshape(X.shape[0], -1, HEADS * D_K)
        return X @ W_o.T

    def _L0_ffn_ref(hidden_states, gate_w, gate_bias, eg_w, eu_w, ed_w, sg_w, su_w, sd_w):
        import jax, jax.numpy as jnp
        import numpy as np
        from jax import lax
        HIDDEN = 128
        INTER = 64
        E = 64
        K = 6
        G = 8
        TG = 4
        NSH = 2
        ISH = INTER * NSH

        def _moe_forward(hidden_states, gate_w, gate_bias, eg_w, eu_w, ed_w, sg_w, su_w, sd_w):
            B, S, H = hidden_states.shape
            x = hidden_states.reshape(-1, H)
            T = x.shape[0]
            shared = jax.nn.silu(x @ sg_w.T) * (x @ su_w.T) @ sd_w.T
            logits = x @ gate_w.T
            scores = jax.nn.sigmoid(logits) + gate_bias
            group_scores = scores.reshape(T, G, E // G).max(axis=-1)
            _, sel_groups = lax.top_k(group_scores, TG)
            group_mask = jnp.zeros((T, G), scores.dtype).at[jnp.arange(T)[:, None], sel_groups].set(1.0)
            mask = jnp.repeat(group_mask, E // G, axis=1)
            masked_scores = scores * mask
            topk_w, topk_i = lax.top_k(masked_scores, K)
            topk_w = topk_w / (topk_w.sum(axis=-1, keepdims=True) + 1e-08)
            comb = jnp.zeros((T, E), x.dtype).at[jnp.arange(T)[:, None], topk_i].add(topk_w)
            h = jax.nn.silu(jnp.einsum('th,eih->eti', x, eg_w)) * jnp.einsum('th,eih->eti', x, eu_w)
            routed = jnp.einsum('eti,ehi,te->th', h, ed_w, comb)
            return (shared + routed).reshape(B, S, H)
        return _moe_forward(hidden_states, gate_w, gate_bias, eg_w, eu_w, ed_w, sg_w, su_w, sd_w)

    def _L1_attn_ref(x, W_kqv, W_proj, q_norm_w, k_norm_w):
        import jax, jax.numpy as jnp
        import numpy as np
        N_HEAD = 16
        EPS = 1e-06

        def _rotate_half(x):
            d = x.shape[-1] // 2
            return jnp.concatenate((-x[..., d:], x[..., :d]), axis=-1)

        def _rms_norm(x, w, eps=EPS):
            d = x.shape[-1]
            rms = jnp.linalg.norm(x, axis=-1, keepdims=True) * d ** (-0.5)
            return w * (x / (rms + eps))
        B, T, C = x.shape
        H = N_HEAD
        D = C // H
        kqv = x @ W_kqv.T
        k, q, v = jnp.split(kqv, 3, axis=2)

        def to_heads(t):
            return t.reshape(B, T, H, D).transpose(0, 2, 1, 3)
        k, q, v = (to_heads(k), to_heads(q), to_heads(v))
        inv_freq = 1.0 / 10000.0 ** (jnp.arange(0, D, 2, dtype=jnp.float32) / D)
        t_pos = jnp.arange(T, dtype=jnp.float32)
        freqs = t_pos[:, None] * inv_freq[None, :]
        freqs = jnp.concatenate((freqs, freqs), axis=-1)
        cos = jnp.cos(freqs)[None, None]
        sin = jnp.sin(freqs)[None, None]
        q = q * cos + _rotate_half(q) * sin
        k = k * cos + _rotate_half(k) * sin
        q = _rms_norm(q, q_norm_w)
        k = _rms_norm(k, k_norm_w)
        scores = jnp.einsum('bhtd,bhsd->bhts', q, k) / jnp.sqrt(jnp.float32(D))
        causal = jnp.triu(jnp.ones((T, T), dtype=bool), k=1)
        scores = jnp.where(causal[None, None], -jnp.inf, scores)
        att = jax.nn.softmax(scores, axis=-1)
        y = jnp.einsum('bhts,bhsd->bhtd', att, v)
        y = y.transpose(0, 2, 1, 3).reshape(B, T, C)
        return y @ W_proj.T

    def _L1_xattn_ref(x, mem, W_kv, W_q, W_proj, b_proj):
        import jax, jax.numpy as jnp
        import numpy as np
        DIM = 128
        HEADS = 16
        HEAD_DIM = DIM // HEADS
        SCALE = HEAD_DIM ** (-0.5)
        B, Nkv, C = mem.shape
        Nq = x.shape[1]
        kv = (mem @ W_kv).reshape(B, Nkv, 2, HEADS, HEAD_DIM)
        k = kv[:, :, 0].transpose(0, 2, 1, 3)
        v = kv[:, :, 1].transpose(0, 2, 1, 3)
        q = (x @ W_q).reshape(B, Nq, HEADS, HEAD_DIM).transpose(0, 2, 1, 3)
        attn = jnp.einsum('bhqd,bhkd->bhqk', q, k) * SCALE
        attn = jax.nn.softmax(attn, axis=-1)
        out = jnp.einsum('bhqk,bhkd->bhqd', attn, v)
        out = out.transpose(0, 2, 1, 3).reshape(B, Nq, C)
        return out @ W_proj + b_proj

    def _L1_ffn_ref(x, Wr, br, W1, W3, W2, gamma, beta):
        import jax, jax.numpy as jnp
        import numpy as np
        B, N, D, F, E, K = (4, 256, 128, 512, 16, 2)
        EPS = 1e-05
        b, n, d = x.shape
        e = Wr.shape[1]
        xf = x.reshape(-1, d)
        logits = xf @ Wr + br
        probs = jax.nn.softmax(logits, axis=-1)
        vals, idx = jax.lax.top_k(probs, K)
        w = vals / vals.sum(axis=-1, keepdims=True)
        combine = jnp.zeros((xf.shape[0], e), x.dtype)
        for k in range(K):
            combine = combine + w[:, k:k + 1] * jax.nn.one_hot(idx[:, k], e, dtype=x.dtype)
        out = jnp.zeros_like(xf)
        for ei in range(e):
            h = jax.nn.silu(xf @ W1[ei]) * (xf @ W3[ei])
            y = h @ W2[ei]
            mu = y.mean(axis=-1, keepdims=True)
            var = ((y - mu) ** 2).mean(axis=-1, keepdims=True)
            y = (y - mu) * jax.lax.rsqrt(var + EPS) * gamma[ei] + beta[ei]
            out = out + combine[:, ei:ei + 1] * y
        return out.reshape(b, n, d)

    def _L2_attn_ref(x, in_w, in_b, conv_w, conv_b, xp_w, xp_b, out_w, out_b):
        import jax, jax.numpy as jnp
        import numpy as np
        D_STATE = 16
        D_CONV = 4

        def silu(x):
            return x * jax.nn.sigmoid(x)

        def _reference_tuple_inner(x, in_w, in_b, conv_w, conv_b, xp_w, xp_b, out_w, out_b):
            B, S, D = x.shape
            h = x @ in_w.T + in_b
            hc = jax.lax.conv_general_dilated(h.transpose(0, 2, 1), conv_w, window_strides=(1,), padding=[(D_CONV - 1, 0)], feature_group_count=conv_w.shape[0], dimension_numbers=('NCH', 'OIH', 'NCH')) + conv_b[None, :, None]
            h = silu(hc.transpose(0, 2, 1))
            xp = h @ xp_w.T + xp_b
            a = jnp.exp(-jnp.exp(xp[..., :D_STATE]))
            b = silu(xp[..., D_STATE:]) * jnp.sum(h, axis=-1, keepdims=True)

            def step(state, ab):
                a_t, b_t = ab
                state = state * a_t + b_t
                return (state, state)
            init = jnp.zeros((B, D_STATE), x.dtype)
            final_state, ys = jax.lax.scan(step, init, (a.transpose(1, 0, 2), b.transpose(1, 0, 2)))
            out = ys.transpose(1, 0, 2) @ out_w.T + out_b
            return (out, final_state)
        return _reference_tuple_inner(x, in_w, in_b, conv_w, conv_b, xp_w, xp_b, out_w, out_b)[0]

    def _L2_xattn_ref(query, key, value, attention_bias, in_proj_weight, in_proj_bias, out_w, out_b, head_scales, key_padding_mask):
        import jax, jax.numpy as jnp
        import numpy as np
        B, Tq, D = query.shape
        Tk = key.shape[1]
        H = head_scales.shape[0]
        hd = D // H
        scaling = 1.0 / np.sqrt(hd)
        qw, kw, vw = jnp.split(in_proj_weight, 3, axis=0)
        qb, kb, vb = jnp.split(in_proj_bias, 3)
        q = (query @ qw.T + qb).reshape(B, Tq, H, hd).transpose(0, 2, 1, 3)
        k = (key @ kw.T + kb).reshape(B, Tk, H, hd).transpose(0, 2, 1, 3)
        v = (value @ vw.T + vb).reshape(B, Tk, H, hd).transpose(0, 2, 1, 3)
        scores = jnp.einsum('bhqd,bhkd->bhqk', q, k) * scaling
        scores = scores + attention_bias[:, None, :, :]
        scores = jnp.where(key_padding_mask[:, None, None, :], -jnp.inf, scores)
        attn = jax.nn.softmax(scores, axis=-1)
        out = jnp.einsum('bhqk,bhkd->bhqd', attn, v)
        out = out * head_scales[None, :, None, None]
        out = out.transpose(0, 2, 1, 3).reshape(B, Tq, D)
        return out @ out_w.T + out_b

    def _L2_ffn_ref(x, wg, w1, w2):
        import jax, jax.numpy as jnp
        import numpy as np
        CAPACITY_FACTOR = 1.0

        def _top1_gate(x2d, wg):
            S, _ = x2d.shape
            E = wg.shape[1]
            C = int(CAPACITY_FACTOR * S / E)
            logits = x2d @ wg
            gates = jax.nn.softmax(logits, axis=-1)
            idx = jnp.argmax(gates, axis=-1)
            mask = jax.nn.one_hot(idx, E, dtype=jnp.int32)
            loc = jnp.cumsum(mask, axis=0) - 1
            me = jnp.mean(gates, axis=0)
            ce = jnp.mean(mask.astype(gates.dtype), axis=0)
            l_aux = E * jnp.sum(me * ce)
            mask = mask * (loc < C).astype(jnp.int32)
            gate_s = jnp.sum(gates * mask, axis=-1)
            loc_s = jnp.sum(loc * mask, axis=-1)
            loc_oh = jax.nn.one_hot(loc_s, C, dtype=gates.dtype)
            combine = (gate_s[:, None] * mask.astype(gates.dtype))[:, :, None] * loc_oh[:, None, :]
            dispatch = (combine > 0).astype(gates.dtype)
            return (l_aux, combine, dispatch)
        s, b, m = x.shape
        x2d = x.reshape(-1, m)
        l_aux, combine, dispatch = _top1_gate(x2d, wg)
        combine = combine[:, None]
        dispatch = dispatch[:, None]
        xr = x2d[:, None, :]
        dispatched = jnp.einsum('szfc,szm->zfcm', dispatch, xr)
        E = w1.shape[0]
        di = dispatched.reshape(E, -1, m)
        h = jax.nn.relu(jnp.einsum('ecm,emh->ech', di, w1))
        eo = jnp.einsum('ech,ehm->ecm', h, w2)
        eo = eo[None]
        out = jnp.einsum('szfc,zfcm->sm', combine, eo)
        return out.reshape(s, b, m)

    def _L3_attn_ref(x, Wq, bq, Wk, bk, Wv, bv, Wo, bo, W_cross, shift_weights, gate):
        import jax, jax.numpy as jnp
        import numpy as np
        D_MODEL = 128
        N_HEADS = 16
        HEAD_DIM = D_MODEL // N_HEADS
        MAX_SHIFT = HEAD_DIM // 2
        BATCH, SEQ = (2, 256)

        def _forward(x, Wq, bq, Wk, bk, Wv, bv, Wo, bo, W_cross, shift_weights, gate):
            b, s, _ = x.shape
            H, hd = (W_cross.shape[0], W_cross.shape[1])
            ms = shift_weights.shape[1]
            Q = (x @ Wq.T + bq).reshape(b, s, H, hd)
            K = (x @ Wk.T + bk).reshape(b, s, H, hd)
            V = (x @ Wv.T + bv).reshape(b, s, H, hd)
            Qt = jnp.einsum('bqhf,hfg->bqhg', Q, W_cross)
            scores_cross = jnp.einsum('bqhd,bkhd->bhqk', Qt, K)
            f = jnp.arange(hd)[:, None]
            g = jnp.arange(hd)[None, :]
            tau = g - f
            valid = (tau >= 0) & (tau < ms)
            M = jnp.where(valid[None], shift_weights[:, jnp.clip(tau, 0, ms - 1)], 0.0)
            K_mixed = jnp.einsum('hfg,bkhg->bkhf', M, K)
            scores_conv = jnp.einsum('bqhf,bkhf->bhqk', Q, K_mixed)
            gt = jax.nn.sigmoid(gate).reshape(1, H, 1, 1)
            scale = hd ** (-0.5)
            scores = (gt * scores_cross + (1.0 - gt) * scores_conv) * scale
            causal = jnp.tril(jnp.ones((s, s), dtype=bool))
            scores = jnp.where(causal[None, None], scores, -jnp.inf)
            attn = jax.nn.softmax(scores, axis=-1)
            out = jnp.einsum('bhqk,bkhd->bqhd', attn, V).reshape(b, s, H * hd)
            return out @ Wo.T + bo
        return _forward(x, Wq, bq, Wk, bk, Wv, bv, Wo, bo, W_cross, shift_weights, gate)

    def _L3_xattn_ref(q, k, v, Wq, Wk, Wv, gq, bq, gk, bk, Wo, bo):
        import jax, jax.numpy as jnp
        import numpy as np
        DIM = 128
        NUM_HEADS = 16
        HEAD_DIM = DIM // NUM_HEADS
        SCALE = HEAD_DIM ** (-0.5)
        EPS = 1e-05

        def layernorm(x, gamma, beta):
            mu = jnp.mean(x, axis=-1, keepdims=True)
            var = jnp.mean(jnp.square(x - mu), axis=-1, keepdims=True)
            return (x - mu) * jax.lax.rsqrt(var + EPS) * gamma + beta
        B, Lq, _ = q.shape
        Lk = k.shape[1]
        qh = (q @ Wq.T).reshape(B, Lq, NUM_HEADS, HEAD_DIM).transpose(0, 2, 1, 3)
        kh = (k @ Wk.T).reshape(B, Lk, NUM_HEADS, HEAD_DIM).transpose(0, 2, 1, 3)
        vh = (v @ Wv.T).reshape(B, Lk, NUM_HEADS, HEAD_DIM).transpose(0, 2, 1, 3)
        qh = layernorm(qh, gq, bq) * SCALE
        kh = layernorm(kh, gk, bk)
        attn = jax.nn.sigmoid(jnp.einsum('bhqd,bhkd->bhqk', qh, kh))
        x = jnp.einsum('bhqk,bhkd->bhqd', attn, vh)
        x = x.transpose(0, 2, 1, 3).reshape(B, Lq, DIM)
        return x @ Wo.T + bo

    def _L3_ffn_ref(x, W, b, V_r, C):
        import jax, jax.numpy as jnp
        import numpy as np
        base = jnp.einsum('bsd,od->bso', x, W) + b
        correction = jnp.einsum('bsr,or->bso', jnp.einsum('bsd,dr->bsr', x, V_r), C)
        return base + correction
    x = x + _L0_attn_ref(_layernorm(x, axis=-1), L0_attn_key, L0_attn_value, L0_attn_mag_q, L0_attn_dir_q, L0_attn_A_q, L0_attn_B_q, L0_attn_bias_q, L0_attn_mag_v, L0_attn_dir_v, L0_attn_A_v, L0_attn_B_v, L0_attn_bias_v, L0_attn_k_w, L0_attn_k_b, L0_attn_out_w, L0_attn_out_b)
    x = x + _L0_xattn_ref(_layernorm(x, axis=-1), ctx_1024, ctx_1024, mask_1x1xSxS2_if1, L0_xattn_W_q, L0_xattn_W_k, L0_xattn_W_v, L0_xattn_W_o)
    x = x + _L0_ffn_ref(_layernorm(x, axis=-1), L0_ffn_gate_w, L0_ffn_gate_bias, L0_ffn_eg_w, L0_ffn_eu_w, L0_ffn_ed_w, L0_ffn_sg_w, L0_ffn_su_w, L0_ffn_sd_w)
    x = x + _L1_attn_ref(_layernorm(x, axis=-1), L1_attn_W_kqv, L1_attn_W_proj, L1_attn_q_norm_w, L1_attn_k_norm_w)
    x = x + _L1_xattn_ref(_layernorm(x, axis=-1), ctx_1024, L1_xattn_W_kv, L1_xattn_W_q, L1_xattn_W_proj, L1_xattn_b_proj)
    x = x + _L1_ffn_ref(_layernorm(x, axis=-1), L1_ffn_Wr, L1_ffn_br, L1_ffn_W1, L1_ffn_W3, L1_ffn_W2, L1_ffn_gamma, L1_ffn_beta)
    x = x + _L2_attn_ref(_layernorm(x, axis=-1), L2_attn_in_w, L2_attn_in_b, L2_attn_conv_w, L2_attn_conv_b, L2_attn_xp_w, L2_attn_xp_b, L2_attn_out_w, L2_attn_out_b)
    x = x + _L2_xattn_ref(_layernorm(x, axis=-1), ctx_1024, ctx_1024, fside_BxSxS2_0, L2_xattn_in_proj_weight, L2_xattn_in_proj_bias, L2_xattn_out_w, L2_xattn_out_b, L2_xattn_head_scales, mask_BxS2_bf0)
    x = x + _L2_ffn_ref(_layernorm(x, axis=-1), L2_ffn_wg, L2_ffn_w1, L2_ffn_w2)
    x = x + _L3_attn_ref(_layernorm(x, axis=-1), L3_attn_Wq, L3_attn_bq, L3_attn_Wk, L3_attn_bk, L3_attn_Wv, L3_attn_bv, L3_attn_Wo, L3_attn_bo, L3_attn_W_cross, L3_attn_shift_weights, L3_attn_gate)
    x = x + _L3_xattn_ref(_layernorm(x, axis=-1), ctx_1024, ctx_1024, L3_xattn_Wq, L3_xattn_Wk, L3_xattn_Wv, L3_xattn_gq, L3_xattn_bq, L3_xattn_gk, L3_xattn_bk, L3_xattn_Wo, L3_xattn_bo)
    x = x + _L3_ffn_ref(_layernorm(x, axis=-1), L3_ffn_W, L3_ffn_b, L3_ffn_V_r, L3_ffn_C)
    return x

_drawn_inputs = setup_inputs


def setup_inputs(seed=0):
    import zlib

    import numpy as np

    out = dict(_drawn_inputs(seed))
    spreads = {'L0_ffn_gate_bias': (0.0, 0.369),
     'L1_attn_q_norm_w': (1.0, 0.2),
     'L1_attn_k_norm_w': (1.0, 0.2),
     'L1_ffn_br': (0.0, 0.1),
     'L1_ffn_gamma': (1.0, 0.2),
     'L1_ffn_beta': (0.0, 0.1),
     'L2_xattn_in_proj_bias': (0.0, 0.1),
     'L2_xattn_out_b': (0.0, 0.1),
     'L3_attn_bq': (0.0, 0.8),
     'L3_attn_bk': (0.0, 2.0),
     'L3_attn_bv': (0.0, 0.8),
     'L3_attn_bo': (0.0, 0.297),
     'L3_attn_gate': (0.0, 0.8),
     'L3_xattn_gq': (1.0, 0.6),
     'L3_xattn_bq': (0.0, 0.8),
     'L3_xattn_gk': (1.0, 0.6),
     'L3_xattn_bk': (0.0, 0.526),
     'L3_xattn_bo': (0.0, 0.286)}
    factors = {'L0_attn_bias_q': 3.497,
     'L0_attn_k_b': 64.0,
     'L0_ffn_gate_w': 3.888,
     'L0_ffn_eg_w': 4.21,
     'L0_ffn_eu_w': 4.343,
     'L0_ffn_ed_w': 4.345,
     'L0_ffn_sg_w': 2.931,
     'L0_ffn_sd_w': 2.788,
     'L2_xattn_head_scales': 4.225,
     'L2_ffn_wg': 8.0,
     'L2_ffn_w1': 8.0,
     'L2_ffn_w2': 8.0,
     'L3_attn_Wq': 8.0,
     'L3_attn_Wk': 8.0,
     'L3_attn_Wv': 4.69,
     'L3_attn_Wo': 3.501,
     'L3_attn_W_cross': 8.0,
     'L3_attn_shift_weights': 8.0,
     'L3_ffn_b': 21.743}
    for name, (base, spread) in spreads.items():
        noise = np.random.default_rng([zlib.crc32(name.encode()), seed]).standard_normal(out[name].shape)
        drawn = base * np.exp(spread * noise) if base else spread * noise
        out[name] = jnp.asarray(drawn.astype(out[name].dtype))
    for name, factor in factors.items():
        out[name] = (out[name] * factor).astype(out[name].dtype)
    return out
```

```python
from contextlib import ExitStack

import numpy as np

import concourse.bass as bass
from concourse import mybir

STAGES = 12

P = 128
B, SEQ, D = 2, 512, 128
TILES = B * SEQ // P
TPB = SEQ // P
H, HD = 16, 8
QUADS, PER = 4, 4
ROWS = 32
AUG = 24
NCTX, NCTXP = 77, 78
BIG = float(2 ** 100)
SCALE = float(np.float32(HD ** -0.5))
E0, PAIRS0, TOP0, GROUPS0, TOPG0 = 64, 32, 6, 8, 4
E1, F1 = 16, 512
E2, F2, CAP = 8, 512, 128
NSTATE, NCONV, CH = 16, 4, 2
LEFT = NCONV - 1

ALU = mybir.AluOpType
ACT = mybir.ActivationFunctionType
F32, F32R, BF16 = mybir.dt.float32, mybir.dt.float32r, mybir.dt.bfloat16
I32, U32, U8 = mybir.dt.int32, mybir.dt.uint32, mybir.dt.uint8
AX = mybir.AxisListType.X

ATTN = {
    1: dict(cross=True, add="mask"),
    3: dict(cross=False, heads="rope"),
    4: dict(cross=True, obias=True),
    7: dict(cross=True, add="bias", bias=True, obias=True, hscale=True),
    9: dict(cross=False, bias=True, obias=True, mixed=True),
    10: dict(cross=True, heads="norm", obias=True, sigmoid=True),
}

REUSES = {"wq_7": "wq_1", "wk_7": "wk_1", "cross_9": "wq_4", "shift_9": "wk_4"}
LATE = 7


def stack_columns(w):
    out = np.zeros((w.shape[0], QUADS, PER, ROWS), w.dtype)
    out[..., :3 * HD] = np.tile(w.reshape(w.shape[0], QUADS, PER, HD), (1, 1, 1, 3))
    return out.reshape(w.shape[0], QUADS, P)


def stack_bias(b):
    return np.ascontiguousarray(stack_columns(b.reshape(1, D))[0].T)


def head_blocks(m):
    out = np.zeros((H, HD, H, HD), m.dtype)
    for h in range(H):
        out[h, :, h, :] = m[h]
    return out.reshape(D, D)


def layout(i):
    t = {}

    def put(stage, name, a, rows=False):
        t[name] = (np.ascontiguousarray(a), stage, rows)

    row = lambda a: a.reshape(-1)
    f = np.float32
    lo = np.zeros((PER, ROWS, 2), f)
    lo[:, 2 * HD:3 * HD, 0] = 1.0
    lo[:, HD:2 * HD, 1] = 1.0
    put(-1, "lorows", lo.reshape(P, 2))
    kone = np.zeros((PER, ROWS, QUADS), f)
    kone[:, AUG] = 1.0
    kone = kone.reshape(P, QUADS)
    put(-1, "kone", kone)
    c = np.zeros((D, B, NCTXP), f)
    c[:, :, :NCTX] = i["ctx_1024"].transpose(2, 0, 1)
    put(-1, "ctxT", c)
    for n in "qv":
        put(0, f"dirT_{n}", i[f"L0_attn_dir_{n}"].T)
        put(0, f"A_{n}", i[f"L0_attn_A_{n}"])
        put(0, f"BT_{n}", i[f"L0_attn_B_{n}"].T)
        put(0, f"mag_{n}", i[f"L0_attn_mag_{n}"].reshape(1), True)
    put(0, "kwT_0", i["L0_attn_k_w"].T)
    for n, k in (("q", "bias_q"), ("k", "k_b"), ("v", "bias_v")):
        put(0, f"b{n}_0", i[f"L0_attn_{k}"], True)
    put(0, "wo_0", i["L0_attn_out_w"].T)
    put(0, "bo_0", i["L0_attn_out_b"].reshape(1, D))
    put(1, "wq_1", stack_columns(i["L0_xattn_W_q"].T))
    put(1, "wk_1", stack_columns(i["L0_xattn_W_k"].T))
    put(1, "wv_1", i["L0_xattn_W_v"].T)
    put(1, "wo_1", i["L0_xattn_W_o"].T)
    m = i["mask_1x1xSxS2_if1"].reshape(SEQ, NCTX)
    mq = np.zeros((SEQ, NCTXP), m.dtype)
    mq[:, :NCTX] = m
    put(1, "maskq", mq.reshape(TPB, P, NCTXP).transpose(1, 0, 2))
    put(1, "maskT", m.T)
    put(2, "gate0", i["L0_ffn_gate_w"].T)
    put(2, "gbias0", i["L0_ffn_gate_bias"], True)
    kqv = i["L1_attn_W_kqv"]
    put(3, "wk_3", kqv[0:D].T)
    put(3, "wq_3", kqv[D:2 * D].T)
    put(3, "wv_3", kqv[2 * D:].T)
    put(3, "wo_3", i["L1_attn_W_proj"].T)
    put(3, "nq_3", i["L1_attn_q_norm_w"], True)
    put(3, "nk_3", i["L1_attn_k_norm_w"], True)
    inv = (1.0 / (f(10000.0) ** (np.arange(0, HD, 2, dtype=f) / f(HD)))).astype(f)
    ang = (np.arange(SEQ, dtype=f)[:, None] * inv[None, :]).astype(f)
    ang = np.concatenate((ang, ang), -1).reshape(TPB, P, HD).transpose(1, 0, 2)
    sgn = np.ones(HD, f)
    sgn[:HD // 2] = -1.0
    put(3, "cos", np.cos(ang).astype(f))
    put(3, "sin", (np.sin(ang) * sgn).astype(f))
    put(4, "wq_4", stack_columns(i["L1_xattn_W_q"]))
    put(4, "wk_4", stack_columns(i["L1_xattn_W_kv"][:, :D]))
    put(4, "wv_4", i["L1_xattn_W_kv"][:, D:])
    put(4, "wo_4", i["L1_xattn_W_proj"])
    put(4, "bo_4", i["L1_xattn_b_proj"].reshape(1, D))
    put(5, "wr", i["L1_ffn_Wr"])
    put(5, "br", i["L1_ffn_br"], True)
    put(5, "beta", i["L1_ffn_beta"])
    put(6, "inw", i["L2_attn_in_w"].T)
    put(6, "inb", i["L2_attn_in_b"].reshape(CH, P).T)
    put(6, "convw", i["L2_attn_conv_w"].reshape(CH, P, NCONV).transpose(1, 0, 2))
    put(6, "convb", i["L2_attn_conv_b"].reshape(CH, P).T)
    put(6, "xpw", i["L2_attn_xp_w"].T.reshape(CH, P, 2 * NSTATE).transpose(1, 0, 2))
    xb = np.zeros((2, 2, NSTATE, 2), f)
    xb[:, 0] = i["L2_attn_xp_b"].reshape(2, NSTATE).T
    put(6, "xpb", xb.reshape(4 * NSTATE, 2))
    ow = np.zeros((2, 2, NSTATE, D), f)
    ow[:, 0] = i["L2_attn_out_w"].T
    put(6, "ssmo", ow.reshape(4 * NSTATE, D))
    ob = np.zeros((ROWS + 1, D), f)
    ob[0] = ob[ROWS] = i["L2_attn_out_b"]
    put(6, "bo_6", ob)
    ipw, ipb = i["L2_xattn_in_proj_weight"], i["L2_xattn_in_proj_bias"]
    put(7, "wq_7", stack_columns(ipw[:D].T))
    put(7, "wk_7", stack_columns(ipw[D:2 * D].T))
    put(7, "wv_7", ipw[2 * D:].T)
    put(7, "bq_7", stack_bias(ipb[:D]))
    put(7, "bk_7", np.where(kone > 0, kone, stack_bias(ipb[D:2 * D])))
    put(7, "bv_7", ipb[2 * D:], True)
    put(7, "wo_7", i["L2_xattn_out_w"].T)
    put(7, "bo_7", i["L2_xattn_out_b"].reshape(1, D))
    put(7, "hs_7", i["L2_xattn_head_scales"], True)
    fs = i["fside_BxSxS2_0"]
    fq = np.zeros((B, SEQ, NCTXP), fs.dtype)
    fq[:, :, :NCTX] = fs
    put(7, "biasq", fq.reshape(B, TPB, P, NCTXP).transpose(2, 0, 1, 3))
    put(7, "biasT", fs.transpose(2, 0, 1))
    kpp = np.zeros((B, NCTXP, 4), np.uint8)
    kpp[:, :NCTX, 0] = i["mask_BxS2_bf0"].view(np.uint8)
    kpp = kpp.view(np.int32)[..., 0]
    put(7, "padq", kpp.reshape(-1), True)
    put(7, "padT", kpp[:, :NCTX].T)
    put(8, "wg", i["L2_ffn_wg"])
    put(9, "wq_9", i["L3_attn_Wq"].T)
    put(9, "bqc_9", i["L3_attn_bq"].reshape(D, 1))
    put(9, "wk_9", stack_columns(i["L3_attn_Wk"].T))
    put(9, "bk_9", np.where(kone > 0, kone, stack_bias(i["L3_attn_bk"])))
    put(9, "wv_9", i["L3_attn_Wv"].T)
    put(9, "bv_9", i["L3_attn_bv"], True)
    put(9, "wo_9", i["L3_attn_Wo"].T)
    put(9, "bo_9", i["L3_attn_bo"].reshape(1, D))
    put(9, "cross_9", stack_columns(head_blocks(i["L3_attn_W_cross"])))
    sw = i["L3_attn_shift_weights"]
    toep = np.zeros((H, HD, HD), sw.dtype)
    for a in range(HD):
        for b in range(a, min(HD, a + sw.shape[1])):
            toep[:, a, b] = sw[:, b - a]
    put(9, "shift_9", stack_columns(head_blocks(toep)))
    put(9, "gate_9", np.repeat(i["L3_attn_gate"], HD).reshape(D, 1))
    for n in "qkv":
        put(10, f"w{n}_10", i[f"L3_xattn_W{n}"].T)
    for n in ("gq", "bq", "gk", "bk"):
        put(10, f"{n}_10", i[f"L3_xattn_{n}"], True)
    put(10, "wo_10", i["L3_xattn_Wo"].T)
    put(10, "bo_10", i["L3_xattn_bo"].reshape(1, D))
    put(11, "w_11", i["L3_ffn_W"].T)
    put(11, "b_11", i["L3_ffn_b"].reshape(1, D))
    put(11, "vr_11", i["L3_ffn_V_r"])
    put(11, "c_11", i["L3_ffn_C"].T)
    return {k: v for k, v in t.items() if v[1] < STAGES}


def streams(i):
    pair = lambda w: w.reshape(PAIRS0, P, D).transpose(0, 2, 1)
    s0 = np.empty((PAIRS0 + 1, P, 3, P), np.float32)
    s0[0, :, 0], s0[0, :, 1] = i["L0_ffn_sg_w"].T, i["L0_ffn_su_w"].T
    s0[0, :, 2] = i["L0_ffn_sd_w"].T
    s0[1:, :, 0], s0[1:, :, 1] = pair(i["L0_ffn_eg_w"]), pair(i["L0_ffn_eu_w"])
    s0[1:, :, 2] = i["L0_ffn_ed_w"].transpose(0, 2, 1).reshape(PAIRS0, P, D)
    s1 = np.empty((E1, P, 3, F1), np.float32)
    s1[:, :, 0], s1[:, :, 1] = i["L1_ffn_W1"], i["L1_ffn_W3"]
    s1[:, :, 2] = i["L1_ffn_W2"].reshape(E1, F1 // P, P, D).transpose(0, 2, 1, 3).reshape(E1, P, F1)
    s2 = np.empty((E2, P, 2, F2), np.float32)
    s2[:, :, 0] = i["L2_ffn_w1"]
    s2[:, :, 1] = i["L2_ffn_w2"].reshape(E2, F2 // P, P, D).transpose(0, 2, 1, 3).reshape(E2, P, F2)
    return {"stream0": s0, "stream1": s1, "gamma": i["L1_ffn_gamma"], "stream2": s2}


class Signal:

    def __init__(self, sem, planned):
        self.sem, self.planned, self.made = sem, planned, {}

    def tick(self, *step):
        assert step not in self.made, step
        self.made[step] = len(self.made) + 1
        return self.sem, 1

    def at(self, *step):
        assert not self.planned or step in self.planned, step
        return self.sem, self.planned.get(step, 1)


class Slots:

    def __init__(self, count, planned):
        self.count, self.planned, self.made = count, planned, {}
        self.readers = [None] * count

    def take(self, pe, reader, step, use):
        slot = len(self.made) % self.count
        self.made[use] = slot
        if self.readers[slot] is not None:
            before, then = self.readers[slot]
            pe.wait_ge(*before.at(*then))
        self.readers[slot] = (reader, step)
        return slot

    def of(self, *use):
        return self.planned.get(use, 0)


def positive_wait(eng, sem, value):
    if not (isinstance(value, int) and value <= 0):
        eng.wait_ge(sem, value)


def build(nc, tiles, shapes, dram, out, plan):
    made = {}
    ctx = ExitStack()
    with ctx:
        def sb(name, shape, dt=F32):
            return ctx.enter_context(nc.sbuf_tensor(name, list(shape), dt))

        def plain(name):
            return ctx.enter_context(nc.semaphore(name))

        def signal(name):
            s = Signal(plain(name), plan.get(name, {}))
            made[name] = s.made
            return s

        def slots(name, count):
            s = Slots(count, plan.get(name, {}))
            made[name] = s.made
            return s

        PAIR = ctx.enter_context(nc.psum_tensor("PAIR", [P, 6, 512], F32))
        BANK = ctx.enter_context(nc.psum_tensor("BANK", [P, 2, 512], F32))
        pairs, banks = slots("pairs", 3), slots("banks", 2)

        X = sb("X", [P, TILES, D])
        xn = sb("xn", [P, TILES, D])
        xnT = sb("xnT", [P, B * SEQ])
        stats = sb("stats", [P, TILES, 6])
        meanvar = sb("meanvar", [P, TILES, 2])
        vareps = sb("vareps", [P, TILES])
        rstd = sb("rstd", [P, TILES])
        ident = sb("ident", [P, P])
        identR = sb("identR", [P, P])
        identB = sb("identB", [P, P], BF16)
        above = sb("above", [P, P], BF16)
        below = sb("below", [P, P], BF16)
        ones = sb("ones", [P, P])
        minushalf = sb("minushalf", [P, 64])
        plushalf = sb("plushalf", [P, 64])
        qst = sb("qst", [P, B, QUADS, SEQ])
        kst = sb("kst", [P, B, QUADS, SEQ])
        lopart = sb("lopart", [P, 2, 2, 512])
        negmax = sb("negmax", [P, TPB, QUADS, P])
        probs = sb("probs", [P, 4, 2, 512])
        vaug = sb("vaug", [P, B, TPB, H * (HD + 1) + ROWS])
        pvT = sb("pvT", [P, 2, 512])
        rden = sb("rden", [P, TPB, PER])
        heads = sb("heads", [P, B, TPB, D])
        headsT = sb("headsT", [P, B, SEQ])
        addq = sb("addq", [P, B, TPB, NCTXP])
        addT = sb("addT", [NCTX, B, 2, SEQ])
        tokst = sb("tokst", [P, TPB, 512])
        tq = sb("tq", [P, 5, 512])
        small = sb("small", [P, 4, 64])
        blo = sb("blo", [P, 2, QUADS])
        W = {}
        for n, (a, _, rows) in tiles.items():
            W[n] = W[REUSES[n]] if n in REUSES else sb(
                "w_" + n, [P if rows else a.shape[0]] + ([a.size] if rows else list(a.shape[1:])),
                mybir.dt.from_np(a.dtype))
        stage_of = {n: s for n, (_, s, _) in tiles.items()}
        s_load = {s: plain(f"weights_loaded_{s + 1}") for s in range(-1, STAGES)}
        s_x = plain("x_loaded")
        s_out = plain("out_stored")

        def loaded(s):
            return s_load[s], 16 * sum(v == s for v in stage_of.values())

        names = ("consts", "vector_step", "scalar_step", "pool_step", "ln_var", "ln_rstd", "xn_ready", "xnT_psum",
                 "xnT_ready", "x_new", "proj_psum", "lo_ready", "stack_ready", "v_ready", "max_psum", "max_read",
                 "negmaxT_psum", "aug_ready", "score_psum", "probs_ready", "pv_done", "pvT_ready", "pv_psum", "heads_ready", "headsT_psum",
                 "headsT_ready", "out_psum", "tok_psum", "tok_read", "tok_square", "tok_power", "tok_stacked",
                 "add_ready", "mixed_ready", "qc_ready", "gate_psum", "gate_scored", "aside_psum", "aside_ready",
                 "aside_scalar", "aside_pool")
        S = {n: signal(n) for n in names}
        (consts, vector_step, scalar_step, pool_step, ln_var, ln_rstd, xn_ready, xnT_psum,
         xnT_ready, x_new, proj_psum, lo_ready, stack_ready, v_ready, max_psum, max_read,
         negmaxT_psum, aug_ready, score_psum, probs_ready, pv_done, pvT_ready, pv_psum, heads_ready, headsT_psum,
         headsT_ready, out_psum, tok_psum, tok_read, tok_square, tok_power, tok_stacked,
         add_ready, mixed_ready, qc_ready, gate_psum, gate_scored, aside_psum, aside_ready,
         aside_scalar, aside_pool) = [S[n] for n in names]

        def r32(ap):
            return ap.bitcast(F32R)

        def units(cfg):
            return [(g, kb, jp) for g in range(QUADS) for kb in range(1 if cfg["cross"] else TPB) for jp in range(2)]

        def half(b):
            return slice(b * SEQ, (b + 1) * SEQ)

        def col(t):
            return slice(t * P, (t + 1) * P)

        def chain(sig, eng):
            def then(ins):
                k = len(sig.made)
                ins.then_inc(*sig.tick(k))
                eng.wait_ge(sig.sem, k + 1)
            return then

        moe0 = STAGES > 2
        if moe0:
            ring0 = sb("ring0", [P, 4, 3, P])
            pick0 = sb("pick0", [P, PAIRS0, P], BF16)
            combA = sb("combA", [P, B * SEQ], BF16)
            combB = sb("combB", [P, B * SEQ], BF16)
            m0_load = [plain(f"experts0_loaded_{k}") for k in range(4)]
            m0_gu, m0_silu, m0_prod, m0_hidden, m0_down, m0_whigh, m0_wlow = [
                plain("experts0_" + n) for n in ("gate_up", "silu", "product", "hidden", "down", "weights_high",
                                                 "weights_low")]
            silu0, prod0, hidden0 = probs[:, 0], probs[:, 1], probs[:, 2]
        wide = probs[:, :, :, :].rearrange("p a b n -> p (a b) n")
        wide4 = lambda i: wide[:, 4 + i, :]
        tq4d = tq[:, 0:2, :].rearrange("p a (t n) -> p (a t) n", n=P)
        hpre = tq[:, :, :].rearrange("p a n -> p (a n)")[:, 0:CH * B * (SEQ + LEFT)]\
            .rearrange("p (c n) -> p c n", c=CH * B)
        high = qst[:, :, :, :].rearrange("p b g n -> p (b g n)")
        low = kst[:, :, :, :].rearrange("p b g n -> p (b g n)")
        X_AT = 3 * B * SEQ
        w_high = lambda k, a, c: high[:, (2 * k + a) * F1 + c.start:(2 * k + a) * F1 + c.stop]
        w_low = lambda k, a, c: low[:, (2 * k + a) * F1 + c.start:(2 * k + a) * F1 + c.stop]
        x_high, x_low = high[:, X_AT:X_AT + B * SEQ], low[:, X_AT:X_AT + B * SEQ]
        iota = sb("iota", [P, P])
        comb = sb("comb", [P, TILES, E0])
        moe1 = STAGES > 5
        if moe1:
            ring1 = sb("ring1", [P, 2, 3, F1])
            m1_load = [plain(f"experts1_loaded_{k}") for k in range(2)]
            (m1_gu, m1_silu, m1_prod, m1_down, m1_stat, m1_var, m1_rstd, m1_rescale, m1_scale, m1_norm,
             m1_scaled, m1_added, m1_whigh, m1_wlow) = [
                plain("experts1_" + n) for n in ("gate_up", "silu", "product", "down", "stat", "var",
                                                 "rstd", "rescale", "scale", "norm", "scaled", "added",
                                                 "weights_high", "weights_low")]
            m1_eps = plain("experts1_eps")
            m1_gamma = [plain(f"gamma_loaded_{k}") for k in range(2)]
            epsilon = sb("epsilon", [P, TPB])
            gammarow = sb("gammarow", [P, 2, D])
            hidden1, silu1, norm1 = wide[:, 0:4], wide[:, 4:6], wide[:, 6:8]
            shift1 = sb("shift1", [P, TILES])
            mv1 = sb("mv1", [P, TILES, 2])
            st1 = sb("st1", [P, TILES, 6])
            ve1 = sb("ve1", [P, TILES])
            rs1 = sb("rs1", [P, TILES])
            sc1 = sb("sc1", [P, TILES])
            combT1 = headsT[0:E1, :, :].rearrange("p b n -> p (b n)")

        moe2 = STAGES > 8
        if moe2:
            tri = sb("tri", [P, P], BF16)
            onesB = sb("onesB", [P, P], BF16)
            onehotB = sb("onehotB", [P, TILES, E2], BF16)
            own_slot = sb("own_slot", [P, E2])
            diag2 = heads[:, :, :, :].rearrange("p b t d -> p (b t) d")
            slot_rows = headsT[:, :, :].rearrange("p b n -> p (b n)")
            disp2 = [wide[:, 2 * k:2 * k + 2, :].rearrange("p a (t n) -> p (a t) n", n=CAP) for k in range(2)]
            combT2 = [wide[:, 4 + 2 * k:6 + 2 * k, :].rearrange("p a n -> p (a n)") for k in range(2)]
            hid2 = [pvT[:, k, :] for k in range(2)]
            ring2 = ring1
            m2_load = [plain(f"experts2_loaded_{k}") for k in range(2)]

        block = ctx.enter_context(nc.Block())

        @block.sync
        def _(sp):
            def load(s):
                for n, (_, stage, rows) in tiles.items():
                    if stage == s:
                        src = dram[n].partition_broadcast(P) if rows else dram[n]
                        sp.dma_start(W[n][:], src).then_inc(s_load[s], 16)
            sp.dma_start(X[:, :, :], dram["x"].rearrange("b (t p) d -> p (b t) d", p=P)).then_inc(s_x, 16)
            for s in range(-1, min(STAGES, LATE)):
                load(s)

            def load_pairs(i, first=False):
                for k in range(4):
                    positive_wait(sp, m0_down, 8 * i + 2 * k - 4 if not first else 2 * k - 4)
                    sp.dma_start(ring0[:, k, :, :], dram["stream0"][4 * i + k + 1]).then_inc(m0_load[k], 16)
            if moe0:
                sp.dma_start(ring0[:, 3, :, :], dram["stream0"][0]).then_inc(m0_load[3], 16)
                load_pairs(0, True)
                with sp.Fori(1, PAIRS0 // 4) as i:
                    load_pairs(i)

            def load_expert(e, k, first=False):
                positive_wait(sp, m1_down, 8 * e - 8 if not first else 0)
                sp.dma_start(ring1[:, k, :, :], dram["stream1"][e]).then_inc(m1_load[k], 16)
                positive_wait(sp, m1_scaled, 2 * e - 2 if not first else 0)
                sp.dma_start(gammarow[:, k, :], dram["gamma"][e].partition_broadcast(P)).then_inc(m1_gamma[k], 16)
            if moe1:
                load_expert(0, 0, True)
                load_expert(1, 1, True)
                with sp.Fori(1, E1 // 2) as i:
                    for k in range(2):
                        load_expert(2 * i + k, k)
            if STAGES > LATE:
                sp.wait_ge(*x_new.at(4, 1))
            for s in range(LATE, STAGES):
                load(s)
            if moe2:
                sp.wait_ge(*x_new.at(5, 1))
                for e in range(E2):
                    if e >= 2:
                        sp.wait_ge(*aside_psum.at(8, "expert", e - 2))
                    sp.dma_start(ring2[:, e % 2, 0:2, :], dram["stream2"][e]).then_inc(m2_load[e % 2], 16)
            for b in range(B):
                sp.wait_ge(*x_new.at(STAGES - 1, b))
                sp.dma_start(out.rearrange("b (t p) d -> p b t d", p=P)[:, b],
                             X[:, TPB * b:TPB * (b + 1), :]).then_inc(s_out, 16)
            sp.wait_ge(s_out, 16 * B)

        @block.tensor
        def _(pe):
            mm, tr = nc.tensor.matmul, nc.tensor.transpose

            def ln(s, b):
                slot = banks.take(pe, xnT_ready, (s, b), ("xnT", s, b))
                if (s, b) == (0, 0):
                    pe.wait_ge(*consts.at("ident"))
                pe.wait_ge(*xn_ready.at(s, b))
                for t in range(TPB):
                    last = tr(BANK[:, slot, col(t)], xn[:, TPB * b + t, :], ident[:, :])
                last.then_inc(*xnT_psum.tick(s, b))

            def tokens_by(dst, w, b, first=True, last=True, src=None):
                for t in range(TPB):
                    n = w.shape[-1]
                    ins = mm(dst[:, t * n:(t + 1) * n], xnT[:, b * SEQ + t * P:b * SEQ + (t + 1) * P], w,
                             start=True, stop=True)
                return ins

            def context_kv(s, b):
                cfg = ATTN[s]
                if cfg.get("heads") == "norm":
                    slot = pairs.take(pe, tok_read, (s, b, "k"), ("tok", s, b, "k"))
                    mm(PAIR[0:NCTX, 2 * slot, 0:D], W["ctxT"][:, b, 0:NCTX], W[f"wk_{s}"][:, :],
                       start=True, stop=True).then_inc(*tok_psum.tick(s, b, "k"))
                else:
                    slot = pairs.take(pe, stack_ready, (s, b, "k", 0), ("stack", s, b, "k", 0))
                    for g in range(QUADS):
                        last = mm(PAIR[:, 2 * slot, g * NCTXP:(g + 1) * NCTXP], W[f"wk_{s}"][:, g, :],
                                  W["ctxT"][:, b, :], start=True, stop=True)
                    last.then_inc(*proj_psum.tick(s, b, "k", 0))
                slot = banks.take(pe, v_ready, (s, b), ("v", s, b))
                mm(BANK[0:NCTX, slot, 0:D], W["ctxT"][:, b, 0:NCTX], W[f"wv_{s}"][:, :],
                   start=True, stop=True).then_inc(*proj_psum.tick(s, b, "v"))

            def stacked_product(s, b, which, w, rhs):
                for gp in range(2):
                    slot = pairs.take(pe, stack_ready, (s, b, which, gp), ("stack", s, b, which, gp))
                    for r in range(2):
                        last = mm(PAIR[:, 2 * slot + r, :], w[:, 2 * gp + r, :], rhs, start=True, stop=True)
                    last.then_inc(*proj_psum.tick(s, b, which, gp))

            def stacked_transpose(s, b, which):
                pe.wait_ge(*tok_stacked.at(s, b, which))
                cross = ATTN[s]["cross"] and which == "k"
                if cross:
                    slot = pairs.take(pe, stack_ready, (s, b, which, 0), ("stack", s, b, which, 0))
                    for g in range(QUADS):
                        last = tr(PAIR[:, 2 * slot, g * NCTXP:g * NCTXP + NCTX], tokst[0:NCTX, 0, col(g)],
                                  ident[0:NCTX, 0:NCTX])
                    last.then_inc(*proj_psum.tick(s, b, which, 0))
                    return
                for gp in range(2):
                    slot = pairs.take(pe, stack_ready, (s, b, which, gp), ("stack", s, b, which, gp))
                    for r in range(2):
                        for t in range(TPB):
                            last = tr(PAIR[:, 2 * slot + r, col(t)], tokst[:, t, col(2 * gp + r)], ident[:, :])
                    last.then_inc(*proj_psum.tick(s, b, which, gp))

            def project(s, b):
                cfg = ATTN[s]
                pe.wait_ge(*xnT_ready.at(s, b))
                x = xnT[:, half(b)]
                if cfg.get("heads"):
                    slot = pairs.take(pe, tok_read, (s, b, "k" if not cfg["cross"] else "q"), ("tok", s, b, "q"))
                    last = tokens_by(PAIR[:, 2 * slot, :], W[f"wq_{s}"][:, :], b)
                    if not cfg["cross"]:
                        last = tokens_by(PAIR[:, 2 * slot + 1, :], W[f"wk_{s}"][:, :], b)
                    last.then_inc(*tok_psum.tick(s, b, "q"))
                if not cfg["cross"]:
                    slot = banks.take(pe, v_ready, (s, b), ("v", s, b))
                    tokens_by(BANK[:, slot, :], W[f"wv_{s}"][:, :], b).then_inc(*proj_psum.tick(s, b, "v"))
                if cfg.get("heads"):
                    stacked_transpose(s, b, "q")
                    if not cfg["cross"]:
                        stacked_transpose(s, b, "k")
                    return
                if not cfg["cross"]:
                    stacked_product(s, b, "k", W[f"wk_{s}"], x)
                if cfg.get("mixed"):
                    slot = banks.take(pe, qc_ready, (s, b), ("qc", s, b))
                    mm(BANK[:, slot, :], W[f"wq_{s}"][:, :], x, start=True, stop=True)\
                        .then_inc(*proj_psum.tick(s, b, "qc"))
                    pe.wait_ge(*mixed_ready.at(s))
                    pe.wait_ge(*qc_ready.at(s, b))
                    x = tq[:, b, :]
                    stacked_product(s, b, "q", W[f"cross_{s}"], x)
                else:
                    stacked_product(s, b, "q", W[f"wq_{s}"], x)

            def maxima(s, b):
                cfg = ATTN[s]
                for which, n in (("q", 2), ("k", 1 if cfg["cross"] else 2)):
                    pe.wait_ge(*stack_ready.at(s, b, which, n - 1))
                if cfg["cross"]:
                    if cfg.get("add"):
                        pe.wait_ge(*add_ready.at(s))
                    for t in range(TPB):
                        for jp in range(2):
                            slot = pairs.take(pe, max_read, (s, b, t, jp), ("max", s, b, t, jp))
                            for r in range(2):
                                rows = slice(ROWS * (2 * jp + r), ROWS * (2 * jp + r + 1))
                                for g in range(QUADS):
                                    last = mm(PAIR[:, 2 * slot + r, g * NCTXP:(g + 1) * NCTXP],
                                              r32(qst[rows, b, g, col(t)]), r32(kst[rows, b, g, 0:NCTXP]),
                                              start=(g == 0), stop=not cfg.get("add"), skip_group_check=True)
                            if cfg.get("add"):
                                a = addq[:, b if cfg["add"] == "bias" else 0, t, :]
                                for r in range(2):
                                    last = mm(PAIR[:, 2 * slot + r, 0:QUADS * NCTXP], r32(identR[:, :]),
                                              r32(a.unsqueeze(1).to_broadcast([P, QUADS, NCTXP])),
                                              start=False, stop=True, skip_group_check=True)
                            last.then_inc(*max_psum.tick(s, b, t, jp))
                else:
                    for g in range(QUADS):
                        for t in range(TPB):
                            for jp in range(2):
                                slot = pairs.take(pe, max_read, (s, b, g, t, jp), ("max", s, b, g, t, jp))
                                for r in range(2):
                                    rows = slice(ROWS * (2 * jp + r), ROWS * (2 * jp + r + 1))
                                    mm(PAIR[:, 2 * slot + r, 0:(t + 1) * P], r32(qst[rows, b, g, col(t)]),
                                       r32(kst[rows, b, g, 0:(t + 1) * P]), start=True, stop=False,
                                       skip_group_check=True)
                                for r in range(2):
                                    last = mm(PAIR[:, 2 * slot + r, col(t)], identB[:, :], above[:, :],
                                              start=False, stop=True, skip_group_check=True)
                                last.then_inc(*max_psum.tick(s, b, g, t, jp))
                for g in range(QUADS):
                    slot = banks.take(pe, aug_ready, (s, b, g), ("aug", s, b, g))
                    pe.wait_ge(*(max_read.at(s, b, TPB - 1, 1) if cfg["cross"] else max_read.at(s, b, g, TPB - 1, 1)))
                    for t in range(TPB):
                        last = tr(BANK[:, slot, col(t)], negmax[:, t, g, :], ident[:, :])
                    last.then_inc(*negmaxT_psum.tick(s, b, g))

            def scores(s, b, u):
                cfg = ATTN[s]
                g, kb, jp = u
                slot = pairs.take(pe, probs_ready, (s, b, *u), ("score", s, b, *u))
                if kb == 0 and jp == 0:
                    if cfg.get("sigmoid"):
                        pe.wait_ge(*stack_ready.at(s, b, "q", 1))
                        pe.wait_ge(*stack_ready.at(s, b, "k", 0))
                    else:
                        pe.wait_ge(*aug_ready.at(s, b, g))
                keys = slice(0, NCTX) if cfg["cross"] else col(kb)
                n, m = SEQ - kb * P, NCTX if cfg["cross"] else P
                for r in range(2):
                    rows = slice(ROWS * (2 * jp + r), ROWS * (2 * jp + r + 1))
                    last = mm(PAIR[0:m, 2 * slot + r, 0:n], r32(kst[rows, b, g, keys]),
                              r32(qst[rows, b, g, kb * P:SEQ]), start=True,
                              stop=cfg["cross"] and not cfg.get("add"), skip_group_check=True)
                for r in range(2):
                    dst = PAIR[0:m, 2 * slot + r, 0:n]
                    if not cfg["cross"]:
                        last = mm(PAIR[:, 2 * slot + r, 0:P], identB[:, :], below[:, :], start=False, stop=True,
                                  skip_group_check=True)
                    elif cfg.get("add"):
                        ab = b if cfg["add"] == "bias" else 0
                        for part in range(2 if cfg["add"] == "bias" else 1):
                            last = mm(dst, r32(identR[0:NCTX, 0:NCTX]), r32(addT[:, ab, part, :]), start=False,
                                      stop=part == (cfg["add"] == "bias"), skip_group_check=True)
                last.then_inc(*score_psum.tick(s, b, *u))

            def weighted(s, b, u, n):
                cfg = ATTN[s]
                g, kb, jp = u
                if kb == 0 and jp == 0:
                    banks.take(pe, pvT_ready, (s, b, g), ("pv", s, b, g))
                slot = banks.made[("pv", s, b, g)]
                pe.wait_ge(*probs_ready.at(s, b, *u))
                if g == 0 and kb == 0 and jp == 0:
                    pe.wait_ge(*v_ready.at(s, b))
                m = NCTX if cfg["cross"] else P
                for r in range(2):
                    j = 2 * jp + r
                    c = (PER * g + j) * (HD + 1)
                    last = mm(BANK[ROWS * j:ROWS * (j + 1), slot, kb * P:SEQ], vaug[0:m, b, kb, c:c + ROWS],
                              probs[0:m, n % 4, r, 0:SEQ - kb * P], start=kb == 0,
                              stop=cfg["cross"] or kb == TPB - 1, skip_group_check=True)
                last.then_inc(*pv_done.tick(s, b, *u))

            def weighted_back(s, b, g):
                slot = pairs.take(pe, heads_ready, (s, b, g), ("pv", s, b, g))
                pe.wait_ge(*pvT_ready.at(s, b, g))
                for t in range(TPB):
                    last = tr(PAIR[:, 2 * slot, col(t)], pvT[:, g % 2, col(t)], ident[:, :])
                last.then_inc(*pv_psum.tick(s, b, g))

            count = [0]

            def attend(s, b):
                us = units(ATTN[s])
                scores(s, b, us[0])
                scores(s, b, us[1])
                for i, u in enumerate(us):
                    weighted(s, b, u, count[0])
                    count[0] += 1
                    if i + 2 < len(us):
                        scores(s, b, us[i + 2])
                    if i and us[i - 1][0] != u[0]:
                        weighted_back(s, b, us[i - 1][0])
                weighted_back(s, b, QUADS - 1)

            def output(s, b):
                slot = banks.take(pe, headsT_ready, (s, b), ("headsT", s, b))
                pe.wait_ge(*heads_ready.at(s, b, QUADS - 1))
                for t in range(TPB):
                    last = tr(BANK[:, slot, col(t)], heads[:, b, t, :], ident[:, :])
                last.then_inc(*headsT_psum.tick(s, b))
                slot = banks.take(pe, x_new, (s, b), ("out", s, b))
                pe.wait_ge(*headsT_ready.at(s, b))
                bias = f"bo_{s}" in W
                for t in range(TPB):
                    if bias:
                        mm(BANK[:, slot, col(t)], ones[0:1, :], W[f"bo_{s}"][:, :], start=True, stop=False)
                    last = mm(BANK[:, slot, col(t)], headsT[:, b, col(t)], W[f"wo_{s}"][:, :],
                              start=not bias, stop=True)
                last.then_inc(*out_psum.tick(s, b))

            def attention(s):
                cfg = ATTN[s]
                if s == 3 or s == 1:
                    pe.wait_ge(*consts.at("all"))
                pe.wait_ge(*loaded(s))
                if cfg["cross"]:
                    for b in range(B):
                        context_kv(s, b)
                    if cfg.get("heads"):
                        for b in range(B):
                            stacked_transpose(s, b, "k")
                for b in range(B):
                    ln(s, b)
                    project(s, b)
                    if not cfg.get("sigmoid"):
                        maxima(s, b)
                for b in range(B):
                    attend(s, b)
                    output(s, b)

            def pair_attention(s=0):
                pe.wait_ge(*loaded(-1))
                pe.wait_ge(*loaded(0))
                for w in "qv":
                    slot = banks.take(pe, aside_ready, (0, "V" + w), ("V", w))
                    mm(BANK[:, slot, 0:D], W[f"A_{w}"][:, :], W[f"BT_{w}"][:, :], start=True, stop=True)\
                        .then_inc(*aside_psum.tick(0, "V" + w))
                slot = banks.take(pe, aside_ready, (0, "norm"), ("norm",))
                pe.wait_ge(*consts.at("ident"))
                pe.wait_ge(*aside_ready.at(0, "squares"))
                mm(BANK[:, slot, 0:2], ones[:, :], small[:, 0, 0:2], start=True, stop=True)\
                    .then_inc(*aside_psum.tick(0, "norm"))
                for b in range(B):
                    ln(s, b)
                for b in range(B):
                    slot = pairs.take(pe, tok_read, (0, b, "k"), ("tok", 0, b, "q"))
                    pe.wait_ge(*xnT_ready.at(0, b))
                    pe.wait_ge(*aside_ready.at(0, "W"))
                    tokens_by(PAIR[:, 2 * slot, :], W["dirT_q"][:, :], b)
                    tokens_by(PAIR[:, 2 * slot + 1, :], W["kwT_0"][:, :], b).then_inc(*tok_psum.tick(0, b, "q"))
                    slot = banks.take(pe, v_ready, (0, b), ("v", 0, b))
                    tokens_by(BANK[:, slot, :], W["dirT_v"][:, :], b).then_inc(*proj_psum.tick(0, b, "v"))
                for b in range(B):
                    output(s, b)

            def three(dst, left, right, start, stop):
                for n, (i, j) in enumerate(((0, 0), (0, 1), (1, 0))):
                    last = mm(dst, r32(left[i]), r32(right[j]), start=start and n == 0, stop=stop and n == 2,
                              skip_group_check=True)
                return last

            def experts0(s=2):
                pe.wait_ge(*loaded(s))
                for b in range(B):
                    ln(s, b)
                slot = pairs.take(pe, gate_scored, (s,), ("gate", s))
                for b in range(B):
                    pe.wait_ge(*xnT_ready.at(s, b))
                    last = tokens_by(PAIR[:, 2 * slot, b * TPB * E0:(b + 1) * TPB * E0], W["gate0"][:, :], b)
                last.then_inc(*gate_psum.tick(s))
                slot = pairs.take(pe, aside_ready, (s, "comb"), ("combT", s))
                pe.wait_ge(*aside_ready.at(s, "doubled"))
                for t in range(TILES):
                    last = tr(PAIR[:, 2 * slot + t // TPB, col(t % TPB)], tq4d[:, t, :], ident[:, :])
                last.then_inc(*aside_psum.tick(s, "comb"))
                pe.wait_ge(*aside_ready.at(s, "comb"))
                pe.wait_ge(*aside_ready.at(s, "zeroed"))
                pe.wait_ge(*aside_pool.at(s, "pick", 1))
                pe.wait_ge(*aside_ready.at(s, "low"))

                def gate_up(i, k, h, shared=False):
                    positive_wait(pe, m0_hidden, 8 * i + 2 * k + h + 1)
                    for a in range(2):
                        w = slice((2 * k + a) * P, (2 * k + a + 1) * P)
                        last = three(PAIR[:, 3 * h + a, :], (high[:, w], low[:, w]),
                                     (x_high[:, half(h)], x_low[:, half(h)]), True, True)
                    if not shared:
                        pick = pick0[:, 4 * i + k, :]
                        mm(PAIR[:, 3 * h + 2, :], pick, combA[:, half(h)], start=True, stop=False)
                        last = mm(PAIR[:, 3 * h + 2, :], pick, combB[:, half(h)], start=False, stop=True)
                    last.then_inc(m0_gu, 1)

                def down(i, k, h):
                    pe.wait_ge(m0_hidden, 8 * i + 2 * k + h + 3)
                    for t in range(TPB):
                        last = mm(BANK[:, h, col(t)], hidden0[:, h, col(t)], ring0[:, k, 2, :],
                                  start=False, stop=False, skip_group_check=True)
                    last.then_inc(m0_down, 1)

                def four_pairs(i):
                    for k in range(4):
                        pe.wait_ge(m0_wlow, 4 * i + k + 2)
                        for h in range(2):
                            gate_up(i, k, h)
                            if k == 0:
                                down(i - 1, 3, h)
                            else:
                                down(i, k - 1, h)

                pe.wait_ge(m0_wlow, 1)
                gate_up(-1, 3, 0, shared=True)
                gate_up(-1, 3, 1, shared=True)
                four_pairs(0)
                with pe.Fori(1, PAIRS0 // 4) as i:
                    four_pairs(i)
                for h in range(2):
                    down(PAIRS0 // 4 - 1, 3, h)
                pairs.readers[:] = [(x_new, (s, 1))] * 3
                banks.readers[:] = [(x_new, (s, 1))] * 2

            def experts1(s=5):
                pe.wait_ge(*loaded(s))
                for b in range(B):
                    ln(s, b)
                slot = pairs.take(pe, gate_scored, (s,), ("gate", s))
                for b in range(B):
                    pe.wait_ge(*xnT_ready.at(s, b))
                    last = tokens_by(PAIR[:, 2 * slot, b * TPB * E1:(b + 1) * TPB * E1], W["wr"][:, :], b)
                last.then_inc(*gate_psum.tick(s))
                slot = pairs.take(pe, aside_ready, (s, "comb"), ("combT", s))
                pe.wait_ge(*aside_ready.at(s, "combined"))
                for t in range(TILES):
                    last = tr(PAIR[0:E1, 2 * slot + t // TPB, col(t % TPB)], comb[:, t, 0:E1], ident[:, :])
                last.then_inc(*aside_psum.tick(s, "comb"))
                slot = pairs.take(pe, aside_ready, (s, "beta"), ("beta", s))
                pe.wait_ge(*aside_ready.at(s, "comb"))
                for t in range(TILES):
                    last = mm(PAIR[:, 2 * slot + t // TPB, col(t % TPB)], combT1[:, col(t)], W["beta"][:, :],
                              start=True, stop=True)
                last.then_inc(*aside_psum.tick(s, "beta"))
                pe.wait_ge(*aside_ready.at(s, "beta"))

                pe.wait_ge(*aside_ready.at(s, "low"))

                def gate_up(e, k, h, fb):
                    positive_wait(pe, m1_prod, 8 * e + 4 * h + fb - 1)
                    if h == 0 and fb == 0:
                        pe.wait_ge(m1_wlow, 2 * e + 2)
                    for a in range(2):
                        last = three(PAIR[:, 2 * (fb % 2) + a, :], (w_high(k, a, col(fb)), w_low(k, a, col(fb))),
                                     (x_high[:, half(h)], x_low[:, half(h)]), True, True)
                    last.then_inc(m1_gu, 1)

                def down(e, k, h, fb):
                    pe.wait_ge(m1_prod, 8 * e + 4 * h + fb + 1)
                    if fb == 0:
                        positive_wait(pe, m1_norm, 2 * e + h - 1)
                    for t in range(TPB):
                        last = mm(BANK[:, h, col(t)], hidden1[:, fb, col(t)], ring1[:, k, 2, col(fb)],
                                  start=(fb == 0 and t == 0), stop=(fb == 3), skip_group_check=True)
                    last.then_inc(m1_down, 1)

                def expert(e, k, first=False):
                    for h in range(2):
                        for fb in range(4):
                            gate_up(e, k, h, fb)
                            if fb >= 2:
                                down(e, k, h, fb - 2)
                            elif h:
                                down(e, k, 0, fb + 2)
                            elif not first:
                                down(e - 1, 1 - k, 1, fb + 2)
                expert(0, 0, True)
                with pe.Fori(1, E1 // 2) as i:
                    expert(2 * i - 1, 1)
                    expert(2 * i, 0)
                expert(E1 - 1, 1)
                down(E1 - 1, 1, 1, 2)
                down(E1 - 1, 1, 1, 3)
                pairs.readers[:] = [(x_new, (s, 1))] * 3
                banks.readers[:] = [(x_new, (s, 1))] * 2

            def state_space(s=6):
                pe.wait_ge(*loaded(s))
                for b in range(B):
                    ln(s, b)
                for b in range(B):
                    pe.wait_ge(*xnT_ready.at(s, b))
                    slot = pairs.take(pe, aside_scalar, (s, "h", b), ("h", s, b))
                    for c in range(CH):
                        last = mm(PAIR[:, 2 * slot + c, :], W["inw"][:, col(c)], xnT[:, half(b)], start=True, stop=True)
                    last.then_inc(*aside_psum.tick(s, "h", b))
                slot = pairs.take(pe, aside_ready, (s, "scanned"), ("xp", s))
                slot2 = banks.take(pe, aside_ready, (s, "scanned"), ("hsum", s))
                for b in range(B):
                    pe.wait_ge(*aside_scalar.at(s, "silu", b))
                    rows = slice(ROWS * b, ROWS * b + NSTATE)
                    for c in range(CH):
                        hb = wide4(b * CH + c)
                        for a in range(2):
                            mm(PAIR[rows, 2 * slot + a, :], W["xpw"][:, c, a * NSTATE:(a + 1) * NSTATE], hb,
                               start=c == 0, stop=c == CH - 1, skip_group_check=True)
                        last = mm(BANK[rows, slot2, :], ones[:, 0:NSTATE], hb, start=c == 0, stop=c == CH - 1,
                                  skip_group_check=True)
                    last.then_inc(*aside_psum.tick(s, "xp", b))
                for b in range(B):
                    slot = banks.take(pe, x_new, (s, b), ("out", s, b))
                    if b == 0:
                        pe.wait_ge(*aside_ready.at(s, "scanned"))
                    rows = slice(ROWS * b, ROWS * b + NSTATE)
                    for t in range(TPB):
                        one = slice(ROWS * b, ROWS * b + 1)
                        mm(BANK[:, slot, col(t)], ones[one, :], W["bo_6"][one, :], start=True, stop=False)
                        last = mm(BANK[:, slot, col(t)], tokst[rows, 2, col(t)], W["ssmo"][rows, :],
                                  start=False, stop=True)
                    last.then_inc(*out_psum.tick(s, b))

            def dispatch_experts(s=8):
                pe.wait_ge(*loaded(s))
                for b in range(B):
                    ln(s, b)
                slot = pairs.take(pe, gate_scored, (s,), ("gate", s))
                for b in range(B):
                    pe.wait_ge(*xnT_ready.at(s, b))
                    last = tokens_by(PAIR[:, 2 * slot, b * TPB * E2:(b + 1) * TPB * E2], W["wg"][:, :], b)
                last.then_inc(*gate_psum.tick(s))
                slot = pairs.take(pe, aside_ready, (s, "slots"), ("cumsum", s))
                pe.wait_ge(*aside_ready.at(s, "onehot"))
                pe.wait_ge(*aside_pool.at(s, "triangle"))
                for t in range(TILES):
                    for u in range(t + 1):
                        last = mm(PAIR[:, 2 * slot, t * E2:(t + 1) * E2], (tri if u == t else onesB)[:, :], onehotB[:, u, :],
                                  start=u == 0, stop=u == t)
                last.then_inc(*aside_psum.tick(s, "cumsum"))
                slot = pairs.take(pe, aside_ready, (s, "rows"), ("rows", s))
                pe.wait_ge(*aside_ready.at(s, "diagonal"))
                for t in range(TILES):
                    last = mm(PAIR[:, 2 * slot + t // TPB, col(t % TPB)], ones[:, :], diag2[:, t, :],
                              start=True, stop=True)
                last.then_inc(*aside_psum.tick(s, "rows"))
                outs = [banks.take(pe, x_new, (s, 0), ("out", s, 0)), banks.take(pe, x_new, (s, 1), ("out", s, 1))]

                def gather(e):
                    slot = pairs.take(pe, aside_scalar, (s, "gathered", e), ("gather", s, e))
                    pe.wait_ge(*aside_ready.at(s, "dispatch", e))
                    for t in range(TILES):
                        last = mm(PAIR[:, 2 * slot, 0:CAP], xn[:, t, :], disp2[e % 2][:, t, :],
                                  start=t == 0, stop=t == TILES - 1)
                    last.then_inc(*aside_psum.tick(s, "gathered", e))

                def ffn_up(e):
                    slot = pairs.take(pe, aside_scalar, (s, "hidden", e), ("up", s, e))
                    pe.wait_ge(m2_load[e % 2], 16 * (e // 2 + 1))
                    pe.wait_ge(*aside_scalar.at(s, "gathered", e))
                    for fb in range(F2 // P):
                        last = mm(PAIR[:, 2 * slot, col(fb)], ring2[:, e % 2, 0, col(fb)], tokst[:, e % 2, 0:CAP],
                                  start=True, stop=True)
                    last.then_inc(*aside_psum.tick(s, "hidden", e))

                def ffn_down(e):
                    slot = pairs.take(pe, aside_scalar, (s, "expert", e), ("down", s, e))
                    pe.wait_ge(*aside_scalar.at(s, "hidden", e))
                    for fb in range(F2 // P):
                        last = mm(PAIR[:, 2 * slot, 0:D], hid2[e % 2][:, col(fb)], ring2[:, e % 2, 1, col(fb)],
                                  start=fb == 0, stop=fb == F2 // P - 1)
                    last.then_inc(*aside_psum.tick(s, "expert", e))

                def combine(e):
                    pe.wait_ge(*aside_scalar.at(s, "expert", e))
                    for t in range(TILES):
                        last = mm(BANK[:, outs[t // TPB], col(t % TPB)], combT2[e % 2][:, col(t)],
                                  tokst[:, e % 2, P:P + D],
                                  start=(e == 0 and t % TPB == 0), stop=e == E2 - 1, skip_group_check=True)
                    last.then_inc(*aside_psum.tick(s, "combined", e))

                gather(0)
                for e in range(E2):
                    ffn_up(e)
                    if e:
                        combine(e - 1)
                    if e + 1 < E2:
                        gather(e + 1)
                    ffn_down(e)
                combine(E2 - 1)

            def linear(s=11):
                pe.wait_ge(*loaded(s))
                for b in range(B):
                    ln(s, b)
                    pe.wait_ge(*xnT_ready.at(s, b))
                    slot = pairs.take(pe, aside_scalar, (s, "xv", b), ("xv", s, b))
                    mm(PAIR[0:32, 2 * slot, :], W["vr_11"][:, :], xnT[:, half(b)], start=True, stop=True)\
                        .then_inc(*aside_psum.tick(s, "xv", b))
                    slot = banks.take(pe, x_new, (s, b), ("out", s, b))
                    pe.wait_ge(*aside_scalar.at(s, "xv", b))
                    for t in range(TPB):
                        dst = BANK[:, slot, col(t)]
                        mm(dst, ones[0:1, :], W["b_11"][:, :], start=True, stop=False)
                        mm(dst, xnT[:, b * SEQ + t * P:b * SEQ + (t + 1) * P], W["w_11"][:, :], start=False, stop=False)
                        last = mm(dst, tokst[0:32, b, col(t)], W["c_11"][:, :], start=False, stop=True)
                    last.then_inc(*out_psum.tick(s, b))

            for s in range(STAGES):
                if s in ATTN:
                    attention(s)
                else:
                    {0: pair_attention, 2: experts0, 5: experts1, 6: state_space, 8: dispatch_experts, 11: linear}[s]()

        @block.scalar
        def _(act):
            def act_fn(out, in_, func, bias=0.0, scale=1.0):
                return nc.scalar.activation(out, in_, func, bias=bias, scale=scale)

            def ln_copy(s, b):
                act.wait_ge(*xnT_psum.at(s, b))
                act_fn(xnT[:, half(b)], BANK[:, banks.of("xnT", s, b), :], ACT.Copy).then_inc(*xnT_ready.tick(s, b))

            def low_parts(s, b, which, gp):
                n = len(lo_ready.made)
                if n >= 2:
                    act.wait_ge(*stack_ready.at(*list(lo_ready.made)[n - 2]))
                act.wait_ge(*proj_psum.at(s, b, which, gp))
                slot = pairs.of("stack", s, b, which, gp)
                i = 0 if which == "q" else 1
                scale = W["lorows"][:, i:i + 1]
                bias = ATTN[s].get("bias") and not (s == 9 and which == "q")
                if bias and (n == 0 or not any(k[0] == s for k in lo_ready.made)):
                    act.wait_ge(*aside_ready.at(s, "blo"))
                if ATTN[s]["cross"] and which == "k":
                    w = NCTX if ATTN[s].get("heads") else NCTXP
                    src = PAIR[:, 2 * slot, 0:QUADS * NCTXP].rearrange("p (g n) -> p g n", g=QUADS)[:, :, 0:w]
                    dst = lopart[:, n % 2, 0, 0:QUADS * NCTXP].rearrange("p (g n) -> p g n", g=QUADS)[:, :, 0:w]
                    gs = range(QUADS)
                else:
                    src, dst = PAIR[:, 2 * slot:2 * slot + 2, :], lopart[:, n % 2, :, :]
                    gs = range(2 * gp, 2 * gp + 2)
                if bias:
                    for k, g in enumerate(gs):
                        last = act_fn(r32(dst[:, k, :]), src[:, k, :], ACT.Identity, bias=blo[:, i, g:g + 1], scale=scale)
                else:
                    last = act_fn(r32(dst), src, ACT.Identity, scale=scale)
                last.then_inc(*lo_ready.tick(s, b, which, gp))

            def root(s, b, which):
                act.wait_ge(*tok_square.at(s, b, which))
                if ATTN[s]["cross"]:
                    m, n = (NCTX, H) if which == "k" else (P, TPB * H)
                    out, src = small[0:m, 1, 0:n], small[0:m, 2, 0:n]
                else:
                    out, src = small[:, 1, :], small[:, 0, :]
                act_fn(out, src, ACT.Sqrt).then_inc(*tok_power.tick(s, b, which))

            history = []
            copies = []

            def weighted_copy(s, b, g):
                act.wait_ge(*pv_done.at(s, b, *[u for u in units(ATTN[s]) if u[0] == g][-1]))
                if len(copies) >= 2:
                    act.wait_ge(*pv_psum.at(*copies[-2]))
                act_fn(pvT[:, g % 2, :], BANK[:, banks.of("pv", s, b, g), :], ACT.Copy)\
                    .then_inc(*pvT_ready.tick(s, b, g))
                copies.append((s, b, g))

            def attend(s, b):
                cfg = ATTN[s]
                m = NCTX if cfg["cross"] else P
                func, scale = (ACT.Sigmoid, SCALE) if cfg.get("sigmoid") else (ACT.Exp, SCALE)
                for u in units(cfg):
                    n = len(history)
                    if n >= 4:
                        act.wait_ge(*pv_done.at(*history[n - 4]))
                    act.wait_ge(*score_psum.at(s, b, *u))
                    slot = pairs.of("score", s, b, *u)
                    w = SEQ - u[1] * P
                    act_fn(probs[0:m, n % 4, :, 0:w], PAIR[0:m, 2 * slot:2 * slot + 2, 0:w], func, scale=scale)\
                        .then_inc(*probs_ready.tick(s, b, *u))
                    history.append((s, b, *u))
                    if u[0] and u[1:] == (0, 1):
                        weighted_copy(s, b, u[0] - 1)
                weighted_copy(s, b, QUADS - 1)

            def output(s, b):
                act.wait_ge(*headsT_psum.at(s, b))
                act_fn(headsT[:, b, :], BANK[:, banks.of("headsT", s, b), :], ACT.Copy)\
                    .then_inc(*headsT_ready.tick(s, b))

            def attention(s):
                cfg = ATTN[s]
                act.wait_ge(*loaded(-1))
                act.wait_ge(*loaded(s))
                if cfg.get("mixed"):
                    act_fn(small[:, 0, 0:1], W["gate_9"][:, :], ACT.Sigmoid).then_inc(*aside_scalar.tick(s, "gate"))
                if cfg["cross"]:
                    if cfg.get("heads"):
                        for b in range(B):
                            root(s, b, "k")
                    for b in range(B):
                        low_parts(s, b, "k", 0)
                for b in range(B):
                    ln_copy(s, b)
                    if not cfg["cross"] and not cfg.get("heads"):
                        low_parts(s, b, "k", 0)
                        low_parts(s, b, "k", 1)
                    if cfg.get("mixed"):
                        act.wait_ge(*proj_psum.at(s, b, "qc"))
                        act_fn(tq[:, b, :], BANK[:, banks.of("qc", s, b), :], ACT.Identity, bias=W["bqc_9"][:, 0:1])\
                            .then_inc(*qc_ready.tick(s, b))
                    if cfg.get("heads"):
                        root(s, b, "q")
                    low_parts(s, b, "q", 0)
                    low_parts(s, b, "q", 1)
                    if not cfg["cross"] and cfg.get("heads"):
                        root(s, b, "k")
                        low_parts(s, b, "k", 0)
                        low_parts(s, b, "k", 1)
                for b in range(B):
                    attend(s, b)
                    output(s, b)

            def pair_attention(s=0):
                for b in range(B):
                    ln_copy(s, b)
                act.wait_ge(*aside_ready.at(s, "centred"))
                act_fn(tq[:, 1, 0:256], tq[:, 0, 0:256], ACT.Exp, scale=SCALE).then_inc(*aside_scalar.tick(s, "exp"))
                for b in range(B):
                    output(s, b)

            def experts0(s=2):
                for b in range(B):
                    ln_copy(s, b)
                act.wait_ge(*gate_psum.at(s))
                act_fn(tq[:, 0, :], PAIR[:, 2 * pairs.of("gate", s), :], ACT.Sigmoid)\
                    .then_inc(*gate_scored.tick(s))

                def silu(i, k, h):
                    positive_wait(act, m0_hidden, 8 * i + 2 * k + h + 1)
                    act.wait_ge(m0_gu, 8 * i + 2 * k + h + 3)
                    act_fn(silu0[:, h, :], PAIR[:, 3 * h, :], ACT.Silu).then_inc(m0_silu, 1)

                act.wait_ge(*xnT_ready.at(s, 1))
                act_fn(r32(x_high), xnT[:, :], ACT.Copy).then_inc(*aside_scalar.tick(s, "high"))

                def weights_high(i, k):
                    act.wait_ge(m0_load[k], 16 * i + (32 if k == 3 else 16))
                    positive_wait(act, m0_gu, 8 * i + 2 * k - 4)
                    act_fn(r32(high[:, 2 * k * P:2 * (k + 1) * P]),
                           ring0[:, k, 0:2, :].rearrange("p a n -> p (a n)"), ACT.Copy).then_inc(m0_whigh, 1)

                def four_pairs(i, last=False):
                    for k in range(4):
                        silu(i, k, 0)
                        if k < 3:
                            weights_high(i, k + 1)
                        elif not last:
                            weights_high(i + 1, 0)
                        silu(i, k, 1)

                weights_high(-1, 3)
                weights_high(0, 0)
                silu(-1, 3, 0)
                silu(-1, 3, 1)
                four_pairs(0)
                with act.Fori(1, PAIRS0 // 4 - 1) as i:
                    four_pairs(i)
                four_pairs(PAIRS0 // 4 - 1, True)

            def experts1(s=5):
                for b in range(B):
                    ln_copy(s, b)
                act.wait_ge(*aside_ready.at(s, "centred"))
                act_fn(tq[:, 1, 0:TILES * E1], tq[:, 0, 0:TILES * E1], ACT.Exp)\
                    .then_inc(*aside_scalar.tick(s, "exp"))
                act.wait_ge(*xnT_ready.at(s, 1))
                act_fn(r32(x_high), xnT[:, :], ACT.Copy).then_inc(*aside_scalar.tick(s, "high"))

                def silu(e, h, fb):
                    u = 8 * e + 4 * h + fb
                    act.wait_ge(m1_gu, u + 1)
                    positive_wait(act, m1_prod, u - 1)
                    act_fn(silu1[:, fb % 2, :], PAIR[:, 2 * (fb % 2), :], ACT.Silu).then_inc(m1_silu, 1)

                def weights_high(e, k, a, loads, first=False):
                    if a == 0:
                        act.wait_ge(m1_load[k], loads)
                        positive_wait(act, m1_down, 8 * e - 8 if not first else 0)
                    act_fn(r32(w_high(k, a, slice(0, F1))), ring1[:, k, a, :], ACT.Copy).then_inc(m1_whigh, 1)

                def normed(n, h):
                    act.wait_ge(m1_scale, n + 1)
                    for t in range(TPB):
                        k = TPB * h + t
                        last = act_fn(norm1[:, h, col(t)], BANK[:, h, col(t)], ACT.Identity,
                                      bias=shift1[:, k:k + 1], scale=sc1[:, k:k + 1])
                    last.then_inc(m1_norm, 1)

                def expert(e, first=False, prepare=None):
                    for h in range(2):
                        for fb in range(4):
                            silu(e, h, fb)
                            if fb == 1 and not first:
                                normed(2 * e + h - 2, h)
                            if prepare and (h, fb) in ((0, 3), (1, 1)):
                                weights_high(e + 1, prepare[0], h, prepare[1])

                for a in range(2):
                    weights_high(0, 0, a, 16, True)
                expert(0, True, (1, 16))
                with act.Fori(1, E1 // 2) as i:
                    expert(2 * i - 1, prepare=(0, 16 * i + 16))
                    expert(2 * i, prepare=(1, 16 * i + 16))
                expert(E1 - 1)
                for h in range(2):
                    normed(2 * E1 - 2 + h, h)

            def state_space(s=6):
                act.wait_ge(*loaded(s))
                for b in range(B):
                    ln_copy(s, b)
                for b in range(B):
                    act.wait_ge(*aside_psum.at(s, "h", b))
                    slot = pairs.of("h", s, b)
                    for c in range(CH):
                        last = act_fn(hpre[:, b * CH + c, LEFT:LEFT + SEQ], PAIR[:, 2 * slot + c, :], ACT.Identity,
                                      bias=W["inb"][:, c:c + 1])
                    last.then_inc(*aside_scalar.tick(s, "h", b))
                for b in range(B):
                    act.wait_ge(*aside_ready.at(s, "conv", b))
                    for c in range(CH):
                        last = act_fn(wide4(b * CH + c), wide[:, b * CH + c, :], ACT.Silu, bias=W["convb"][:, c:c + 1])
                    last.then_inc(*aside_scalar.tick(s, "silu", b))
                for b in range(B):
                    act.wait_ge(*aside_psum.at(s, "xp", b))
                    rows = slice(ROWS * b, ROWS * b + NSTATE)
                    slot = pairs.of("xp", s)
                    last = act_fn(tokst[rows, 1, :], PAIR[rows, 2 * slot + 1, :], ACT.Silu, bias=W["xpb"][rows, 1:2])
                last.then_inc(*aside_scalar.tick(s, "input"))
                for b in range(B):
                    rows = slice(ROWS * b, ROWS * b + NSTATE)
                    last = act_fn(tokst[rows, 0, :], PAIR[rows, 2 * slot, :], ACT.Exp, bias=W["xpb"][rows, 0:1])
                last.then_inc(*aside_scalar.tick(s, "exp"))
                act.wait_ge(*aside_scalar.at(s, "exp"))
                for b in range(B):
                    rows = slice(ROWS * b, ROWS * b + NSTATE)
                    last = act_fn(tokst[rows, 3, :], tokst[rows, 0, :], ACT.Exp, scale=-1.0)
                last.then_inc(*aside_scalar.tick(s, "decay"))

            def dispatch_experts(s=8):
                for b in range(B):
                    ln_copy(s, b)
                act.wait_ge(*aside_ready.at(s, "centred"))
                act_fn(tq[:, 1, 0:TILES * E2], tq[:, 0, 0:TILES * E2], ACT.Exp)\
                    .then_inc(*aside_scalar.tick(s, "exp"))

                def gathered(e):
                    act.wait_ge(*aside_psum.at(s, "gathered", e))
                    act_fn(tokst[:, e % 2, 0:CAP], PAIR[:, 2 * pairs.of("gather", s, e), 0:CAP], ACT.Copy)\
                        .then_inc(*aside_scalar.tick(s, "gathered", e))

                gathered(0)
                for e in range(E2):
                    act.wait_ge(*aside_psum.at(s, "hidden", e))
                    act_fn(hid2[e % 2], PAIR[:, 2 * pairs.of("up", s, e), :], ACT.Relu)\
                        .then_inc(*aside_scalar.tick(s, "hidden", e))
                    if e + 1 < E2:
                        gathered(e + 1)
                    act.wait_ge(*aside_psum.at(s, "expert", e))
                    if e >= 2:
                        act.wait_ge(*aside_psum.at(s, "combined", e - 2))
                    act_fn(tokst[:, e % 2, P:P + D], PAIR[:, 2 * pairs.of("down", s, e), 0:D], ACT.Copy)\
                        .then_inc(*aside_scalar.tick(s, "expert", e))

            def linear(s=11):
                for b in range(B):
                    ln_copy(s, b)
                    act.wait_ge(*aside_psum.at(s, "xv", b))
                    act_fn(tokst[0:32, b, :], PAIR[0:32, 2 * pairs.of("xv", s, b), :], ACT.Copy)\
                        .then_inc(*aside_scalar.tick(s, "xv", b))

            for s in range(STAGES):
                if s in ATTN:
                    attention(s)
                else:
                    {0: pair_attention, 2: experts0, 5: experts1, 6: state_space, 8: dispatch_experts, 11: linear}[s]()

        @block.vector
        def _(v):
            V = nc.vector
            then = chain(vector_step, v)

            def ln(s, b):
                ts = range(TPB * b, TPB * (b + 1))
                if s == 0:
                    v.wait_ge(s_x, 16)
                else:
                    v.wait_ge(*x_new.at(s - 1, b))
                for t in ts:
                    last = V.bn_stats(stats[:, t, :], X[:, t, :])
                then(last)
                for t in ts:
                    last = V.bn_aggr(meanvar[:, t, :], stats[:, t, :])
                last.then_inc(*ln_var.tick(s, b))
                v.wait_ge(*ln_var.at(s, b))
                v.wait_ge(*ln_rstd.at(s, b))
                for t in ts:
                    last = V.tensor_scalar(xn[:, t, :], X[:, t, :], meanvar[:, t, 0:1], rstd[:, t:t + 1],
                                           ALU.subtract, ALU.mult)
                last.then_inc(*xn_ready.tick(s, b))

            def stack(s, b, which, gp):
                v.wait_ge(*lo_ready.at(s, b, which, gp))
                n = (lo_ready.at(s, b, which, gp)[1] - 1) % 2
                slot = pairs.of("stack", s, b, which, gp)
                cfg = ATTN[s]
                if cfg["cross"] and which == "k":
                    w = NCTX if cfg.get("heads") else NCTXP
                    src = PAIR[:, 2 * slot, 0:QUADS * NCTXP].rearrange("p (g n) -> p g n", g=QUADS)[:, :, 0:w]
                    lo = lopart[:, n, 0, 0:QUADS * NCTXP].rearrange("p (g n) -> p g n", g=QUADS)[:, :, 0:w]
                    dst, gs = kst[:, b, :, 0:w], range(QUADS)
                else:
                    src, lo = PAIR[:, 2 * slot:2 * slot + 2, :], lopart[:, n, :, :]
                    dst, gs = (qst if which == "q" else kst)[:, b, 2 * gp:2 * gp + 2, :], range(2 * gp, 2 * gp + 2)
                bias = cfg.get("bias") and not (s == 9 and which == "q")
                if bias:
                    for k, g in enumerate(gs):
                        last = V.scalar_tensor_tensor(r32(dst[:, k, :]), src[:, k, :], W[f"b{which}_{s}"][:, g:g + 1],
                                                      lo[:, k, :], ALU.add, ALU.subtract)
                elif which == "k":
                    last = V.scalar_tensor_tensor(r32(dst), src, W["kone"][:, 0:1], lo, ALU.add, ALU.subtract)
                else:
                    last = V.tensor_tensor(r32(dst), src, lo, ALU.subtract)
                last.then_inc(*stack_ready.tick(s, b, which, gp))

            def values(s, b):
                cfg = ATTN[s]
                v.wait_ge(*proj_psum.at(s, b, "v"))
                slot = banks.of("v", s, b)
                m, nt = (NCTX, 1) if cfg["cross"] else (P, TPB)
                src = BANK[0:m, slot, 0:nt * D].rearrange("p (t h d) -> p t h d", t=nt, h=H)
                dst = vaug[0:m, b, 0:nt, 0:H * (HD + 1)].rearrange("p t (h d) -> p t h d", h=H)[:, :, :, 0:HD]
                if cfg.get("bias"):
                    bv = W[f"bv_{s}"][0:m, :].rearrange("p (h d) -> p h d", h=H)
                    for t in range(nt):
                        last = V.tensor_tensor(dst[:, t], src[:, t], bv, ALU.add)
                else:
                    for t in range(nt):
                        last = V.tensor_copy(dst[:, t], src[:, t])
                last.then_inc(*v_ready.tick(s, b))

            def maxima(s, b):
                cfg = ATTN[s]
                if cfg["cross"]:
                    for t in range(TPB):
                        for jp in range(2):
                            v.wait_ge(*max_psum.at(s, b, t, jp))
                            slot = pairs.of("max", s, b, t, jp)
                            src = PAIR[:, 2 * slot:2 * slot + 2, 0:QUADS * NCTXP]\
                                .rearrange("p r (g n) -> p r g n", g=QUADS)[:, :, :, 0:NCTX]
                            c = 2 * jp * ROWS + AUG
                            V.tensor_reduce(negmax[:, t, :, c:c + ROWS + 1:ROWS].rearrange("p g r -> p r g"), src,
                                            AX, ALU.max, negate=True).then_inc(*max_read.tick(s, b, t, jp))
                else:
                    for g in range(QUADS):
                        for t in range(TPB):
                            for jp in range(2):
                                v.wait_ge(*max_psum.at(s, b, g, t, jp))
                                slot = pairs.of("max", s, b, g, t, jp)
                                c = 2 * jp * ROWS + AUG
                                V.tensor_reduce(negmax[:, t, g, c:c + ROWS + 1:ROWS],
                                                PAIR[:, 2 * slot:2 * slot + 2, 0:(t + 1) * P], AX, ALU.max,
                                                negate=True).then_inc(*max_read.tick(s, b, g, t, jp))
                for g in range(QUADS):
                    v.wait_ge(*negmaxT_psum.at(s, b, g))
                    V.tensor_tensor(r32(qst[:, b, g, :]), qst[:, b, g, :], BANK[:, banks.of("aug", s, b, g), :],
                                    ALU.add).then_inc(*aug_ready.tick(s, b, g))

            def normalise(s, b):
                cfg = ATTN[s]
                for g in range(QUADS):
                    v.wait_ge(*pv_psum.at(s, b, g))
                    O = PAIR[:, 2 * pairs.of("pv", s, b, g), :].rearrange("p (t j d) -> p t j d", t=TPB, j=PER)
                    dst = heads[:, b, :, g * PER * HD:(g + 1) * PER * HD].rearrange("p t (j d) -> p t j d", j=PER)
                    if cfg.get("sigmoid"):
                        V.tensor_copy(dst, O[:, :, :, 0:HD]).then_inc(*heads_ready.tick(s, b, g))
                        continue
                    if g or b:
                        v.wait_ge(*heads_ready.at(s, b if g else b - 1, (g or QUADS) - 1))
                    then(V.reciprocal(rden[:, :, :], O[:, :, :, HD:HD + 1].rearrange("p t j d -> p t (j d)")))
                    if cfg.get("hscale"):
                        hs = W[f"hs_{s}"][:, PER * g:PER * (g + 1)].unsqueeze(1).to_broadcast([P, TPB, PER])
                        then(V.tensor_tensor(rden[:, :, :], rden[:, :, :], hs, ALU.mult))
                    V.tensor_tensor(dst, O[:, :, :, 0:HD], rden[:, :, :].unsqueeze(3).to_broadcast([P, TPB, PER, HD]),
                                    ALU.mult).then_inc(*heads_ready.tick(s, b, g))

            def residual(s, b):
                v.wait_ge(*out_psum.at(s, b))
                xs = X[:, TPB * b:TPB * (b + 1), :]
                V.tensor_tensor(xs, xs, BANK[:, banks.of("out", s, b), :].rearrange("p (t d) -> p t d", d=D),
                                ALU.add).then_inc(*x_new.tick(s, b))

            def stack_tokens(dst, src, m):
                return dst.rearrange("p (h r) -> p h r", h=H)[0:m, :, 0:3 * HD].rearrange("p h (c d) -> p h c d", d=HD)

            def thrice(ap, m):
                return ap.unsqueeze(2).to_broadcast([m, H, 3, HD])

            def rope_and_norm(s, b, which):
                if which == "q":
                    v.wait_ge(*tok_psum.at(s, b, "q"))
                src = PAIR[:, 2 * pairs.of("tok", s, b, "q") + (which == "k"), :]\
                    .rearrange("p (t h d) -> p t h d", t=TPB, h=H)
                q4 = lambda i: tq[:, i, :].rearrange("p (t h d) -> p t h d", t=TPB, h=H)
                hh = HD // 2
                for t in range(TPB):
                    cs = W["cos"][:, t, :].unsqueeze(1).to_broadcast([P, H, HD])
                    sn = W["sin"][:, t, :].unsqueeze(1).to_broadcast([P, H, HD])
                    V.tensor_tensor(q4(0)[:, t], src[:, t], cs, ALU.mult)
                    V.tensor_tensor(q4(1)[:, t, :, 0:hh], src[:, t, :, hh:HD], sn[:, :, 0:hh], ALU.mult)
                    last = V.tensor_tensor(q4(1)[:, t, :, hh:HD], src[:, t, :, 0:hh], sn[:, :, hh:HD], ALU.mult)
                if which == "k":
                    last.then_inc(*tok_read.tick(s, b, which))
                    v.wait_ge(*tok_read.at(s, b, which))
                else:
                    then(last)
                then(V.tensor_tensor(tq[:, 2, :], tq[:, 0, :], tq[:, 1, :], ALU.add))
                then(V.tensor_tensor(tq[:, 3, :], tq[:, 2, :], tq[:, 2, :], ALU.mult))
                V.tensor_reduce(small[:, 0, :], tq[:, 3, :].rearrange("p (n d) -> p n d", d=HD), AX, ALU.add)\
                    .then_inc(*tok_square.tick(s, b, which))
                nw = W[f"n{which}_{s}"][:, :].unsqueeze(1).to_broadcast([P, TPB * H, HD])
                then(V.tensor_tensor(tq[:, 0, :].rearrange("p (n d) -> p n d", d=HD),
                                     tq[:, 2, :].rearrange("p (n d) -> p n d", d=HD), nw, ALU.mult))
                v.wait_ge(*tok_power.at(s, b, which))
                then(V.tensor_scalar(small[:, 2, :], small[:, 1, :], float(np.float32(HD ** -0.5)), 1e-6,
                                     ALU.mult, ALU.add))
                then(V.reciprocal(small[:, 3, :], small[:, 2, :]))
                if which == "k":
                    v.wait_ge(*proj_psum.at(s, b, "q", 1))
                elif b:
                    v.wait_ge(*proj_psum.at(s, b - 1, "k", 1))
                for t in range(TPB):
                    r = small[:, 3, t * H:(t + 1) * H].unsqueeze(2).unsqueeze(3).to_broadcast([P, H, 3, HD])
                    last = V.tensor_tensor(stack_tokens(tokst[:, t, :], None, P), thrice(q4(0)[:, t], P), r, ALU.mult)
                last.then_inc(*tok_stacked.tick(s, b, which))

            def head_norm(s, b, which):
                m, nt = (NCTX, 1) if which == "k" else (P, TPB)
                v.wait_ge(*tok_psum.at(s, b, which))
                n = nt * H
                src = PAIR[0:m, 2 * pairs.of("tok", s, b, which), 0:nt * D].rearrange("p (n d) -> p n d", d=HD)
                q = lambda i: tq[0:m, i, 0:nt * D].rearrange("p (n d) -> p n d", d=HD)
                over = lambda a: a.unsqueeze(2).to_broadcast([m, n, HD])
                then(V.tensor_reduce(small[0:m, 0, 0:n], src, AX, ALU.add))
                then(V.tensor_scalar(small[0:m, 1, 0:n], small[0:m, 0, 0:n], 1.0 / HD, None, ALU.mult))
                V.tensor_tensor(q(0), src, over(small[0:m, 1, 0:n]), ALU.subtract)\
                    .then_inc(*tok_read.tick(s, b, which))
                v.wait_ge(*tok_read.at(s, b, which))
                then(V.tensor_tensor(q(1), q(0), q(0), ALU.mult))
                then(V.tensor_reduce(small[0:m, 0, 0:n], q(1), AX, ALU.add))
                V.tensor_scalar(small[0:m, 2, 0:n], small[0:m, 0, 0:n], 1.0 / HD, 1e-5, ALU.mult, ALU.add)\
                    .then_inc(*tok_square.tick(s, b, which))
                v.wait_ge(*tok_power.at(s, b, which))
                then(V.reciprocal(small[0:m, 3, 0:n], small[0:m, 1, 0:n]))
                then(V.tensor_tensor(q(2), q(0), over(small[0:m, 3, 0:n]), ALU.mult))
                gm = W[f"g{which}_{s}"][0:m, :].unsqueeze(1).to_broadcast([m, n, HD])
                then(V.tensor_tensor(q(3), q(2), gm, ALU.mult))
                if which == "k" and b:
                    v.wait_ge(*proj_psum.at(s, b - 1, "k", 0))
                elif which == "q":
                    v.wait_ge(*(proj_psum.at(s, b - 1, "q", 1) if b else proj_psum.at(s, B - 1, "k", 0)))
                bt = W[f"b{which}_{s}"][0:m, :].unsqueeze(1).unsqueeze(2).to_broadcast([m, H, 3, HD])
                for t in range(nt):
                    last = V.tensor_tensor(stack_tokens(tokst[:, t, :], None, m),
                                           thrice(q(3)[:, t * H:(t + 1) * H, :], m), bt, ALU.add)
                last.then_inc(*tok_stacked.tick(s, b, which))

            def added(s):
                cfg = ATTN[s]
                v.wait_ge(*consts.at("all"))
                if cfg["add"] == "mask":
                    V.tensor_scalar(r32(addq[:, 0, :, :]), W["maskq"][:, :, :], 0.0, -BIG, ALU.is_equal, ALU.mult)
                    V.tensor_scalar(r32(addT[:, 0, 0, :]), W["maskT"][:, :], 0.0, -BIG, ALU.is_equal, ALU.mult)\
                        .then_inc(*add_ready.tick(s))
                    return
                root = float(np.float32(HD ** 0.5))
                padT, padq = small[0:NCTX, 0, 0:B], small[:, 1:4, :].rearrange("p a n -> p (a n)")[:, 0:B * NCTXP]
                V.tensor_scalar(padT, W["padT"][:, :], -BIG, None, ALU.mult)
                then(V.tensor_scalar(padq, W["padq"][:, :], -BIG, None, ALU.mult))
                for b in range(B):
                    V.scalar_tensor_tensor(r32(addq[:, b, :, :]), W["biasq"][:, b, :, :], root,
                                           padq[:, b * NCTXP:(b + 1) * NCTXP].unsqueeze(1)
                                           .to_broadcast([P, TPB, NCTXP]), ALU.mult, ALU.add)
                    then(V.tensor_scalar(tq[0:NCTX, 2 + b, :], W["biasT"][:, b, :], root, padT[:, b:b + 1],
                                         ALU.mult, ALU.add))
                    then(V.tensor_copy(r32(addT[:, b, 0, :]), tq[0:NCTX, 2 + b, :]))
                    last = V.tensor_tensor(r32(addT[:, b, 1, :]), tq[0:NCTX, 2 + b, :], addT[:, b, 0, :], ALU.subtract)
                last.then_inc(*add_ready.tick(s))

            def attention(s):
                cfg = ATTN[s]
                ln(s, 0)
                v.wait_ge(*loaded(-1))
                v.wait_ge(*loaded(s))
                if s == 1:
                    v.wait_ge(*consts.at("all"))
                    then(V.tensor_copy(r32(identR[:, :]), ident[:, :]))
                    then(V.tensor_copy(identB[:, :], ident[:, :]))
                if cfg.get("add"):
                    added(s)
                if cfg.get("bias"):
                    for i, n in enumerate("qk"):
                        if f"b{n}_{s}" in W:
                            last = V.tensor_scalar(blo[:, i, :], W[f"b{n}_{s}"][:, :], W["lorows"][:, i:i + 1], None,
                                                   ALU.mult)
                    last.then_inc(*aside_ready.tick(s, "blo"))
                if cfg.get("mixed"):
                    v.wait_ge(*aside_scalar.at(s, "gate"))
                    A, M = W[f"cross_{s}"], W[f"shift_{s}"]
                    then(V.tensor_tensor(A[:, :, :], A[:, :, :], M[:, :, :], ALU.subtract))
                    V.scalar_tensor_tensor(A[:, :, :].rearrange("p g n -> p (g n)"),
                                           A[:, :, :].rearrange("p g n -> p (g n)"), small[:, 0, 0:1],
                                           M[:, :, :].rearrange("p g n -> p (g n)"), ALU.mult, ALU.add)\
                        .then_inc(*mixed_ready.tick(s))
                if cfg["cross"]:
                    for b in range(B):
                        if cfg.get("heads"):
                            head_norm(s, b, "k")
                        values(s, b)
                    for b in range(B):
                        stack(s, b, "k", 0)
                for b in range(B):
                    if b:
                        ln(s, b)
                    if not cfg["cross"]:
                        if not cfg.get("heads"):
                            values(s, b)
                            stack(s, b, "k", 0)
                            stack(s, b, "k", 1)
                    if cfg.get("heads"):
                        (head_norm if cfg["cross"] else rope_and_norm)(s, b, "q")
                    if not cfg["cross"] and cfg.get("heads"):
                        values(s, b)
                    stack(s, b, "q", 0)
                    stack(s, b, "q", 1)
                    if not cfg["cross"] and cfg.get("heads"):
                        rope_and_norm(s, b, "k")
                        stack(s, b, "k", 0)
                        stack(s, b, "k", 1)
                    if not cfg.get("sigmoid"):
                        maxima(s, b)
                for b in range(B):
                    normalise(s, b)
                    residual(s, b)

            def pair_attention(s=0):
                v.wait_ge(*loaded(-1))
                v.wait_ge(*loaded(0))
                for i, w in enumerate("qv"):
                    v.wait_ge(*aside_psum.at(0, "V" + w))
                    V.tensor_tensor(W[f"dirT_{w}"][:, :], W[f"dirT_{w}"][:, :], BANK[:, banks.of("V", w), 0:D],
                                    ALU.add).then_inc(*aside_ready.tick(0, "V" + w))
                    v.wait_ge(*aside_ready.at(0, "V" + w))
                    V.tensor_tensor(tq[:, i, 0:D], W[f"dirT_{w}"][:, :], W[f"dirT_{w}"][:, :], ALU.mult)
                then(V.tensor_copy(tq[:, 2, 0:D], W["dirT_v"][:, :]))
                for i in range(2):
                    last = V.tensor_reduce(small[:, 0, i:i + 1], tq[:, i, 0:D], AX, ALU.add)
                last.then_inc(*aside_ready.tick(0, "squares"))
                v.wait_ge(*aside_psum.at(0, "norm"))
                V.tensor_copy(small[:, 1, 0:2], BANK[:, banks.of("norm"), 0:2]).then_inc(*aside_ready.tick(0, "norm"))
                v.wait_ge(*aside_pool.at(0, "norm"))
                then(V.tensor_scalar(small[:, 3, 0:2], small[:, 2, 0:2], 1e-8, None, ALU.add))
                then(V.reciprocal(small[:, 0, 2:4], small[:, 3, 0:2]))
                for i, w in enumerate("qv"):
                    last = V.tensor_tensor(small[:, 0, 4 + i:5 + i], small[:, 0, 2 + i:3 + i], W[f"mag_{w}"][:, :],
                                           ALU.mult)
                then(last)
                for i, w in enumerate("qv"):
                    last = V.tensor_scalar(W[f"dirT_{w}"][:, :], W[f"dirT_{w}"][:, :], small[:, 0, 4 + i:5 + i], None,
                                           ALU.mult)
                last.then_inc(*aside_ready.tick(0, "W"))
                for b in range(B):
                    ln(s, b)
                bias = lambda n: W[f"b{n}_0"][:, :].unsqueeze(1).to_broadcast([P, TPB, D])
                td = lambda ap: ap.rearrange("p (t d) -> p t d", d=D)
                for b in range(B):
                    v.wait_ge(*tok_psum.at(0, b, "q"))
                    slot = pairs.of("tok", 0, b, "q")
                    V.tensor_tensor(td(probs[:, 0, b, :]), td(PAIR[:, 2 * slot, :]), bias("q"), ALU.add)
                    V.tensor_tensor(td(probs[:, 1, b, :]), td(PAIR[:, 2 * slot + 1, :]), bias("k"), ALU.add)\
                        .then_inc(*tok_read.tick(0, b, "k"))
                    v.wait_ge(*proj_psum.at(0, b, "v"))
                    V.tensor_tensor(td(probs[:, 2, b, :]), td(BANK[:, banks.of("v", 0, b), :]), bias("v"), ALU.add)\
                        .then_inc(*v_ready.tick(0, b))
                v.wait_ge(*v_ready.at(0, 1))
                N = TPB * H
                for i in range(B):
                    for j in range(B):
                        then(V.tensor_tensor(tq[:, 2, :], probs[:, 0, i, :], probs[:, 1, j, :], ALU.mult))
                        last = V.tensor_reduce(tq[:, 3, (2 * i + j) * N:(2 * i + j + 1) * N],
                                               tq[:, 2, :].rearrange("p (n d) -> p n d", d=HD), AX, ALU.add)
                        then(last)
                for i in range(B):
                    last = V.tensor_tensor(small[:, i, :], tq[:, 3, 2 * i * N:(2 * i + 1) * N],
                                           tq[:, 3, (2 * i + 1) * N:(2 * i + 2) * N], ALU.max)
                then(last)
                for i in range(B):
                    for j in range(B):
                        c = slice((2 * i + j) * N, (2 * i + j + 1) * N)
                        last = V.tensor_tensor(tq[:, 0, c], tq[:, 3, c], small[:, i, :], ALU.subtract)
                last.then_inc(*aside_ready.tick(0, "centred"))
                v.wait_ge(*aside_scalar.at(0, "exp"))
                for i in range(B):
                    last = V.tensor_tensor(small[:, i, :], tq[:, 1, 2 * i * N:(2 * i + 1) * N],
                                           tq[:, 1, (2 * i + 1) * N:(2 * i + 2) * N], ALU.add)
                then(last)
                then(V.reciprocal(small[:, 2:4, :], small[:, 0:2, :]))
                for i in range(B):
                    for j in range(B):
                        c = slice((2 * i + j) * N, (2 * i + j + 1) * N)
                        last = V.tensor_tensor(tq[:, 2, c], tq[:, 1, c], small[:, 2 + i, :], ALU.mult)
                then(last)
                for i in range(B):
                    for j in range(B):
                        c = slice((2 * i + j) * N, (2 * i + j + 1) * N)
                        last = V.tensor_tensor(tq[:, 3 + j, :].rearrange("p (n d) -> p n d", d=HD),
                                               probs[:, 2, j, :].rearrange("p (n d) -> p n d", d=HD),
                                               tq[:, 2, c].unsqueeze(2).to_broadcast([P, N, HD]), ALU.mult)
                    then(last)
                    V.tensor_tensor(heads[:, i].rearrange("p t d -> p (t d)"), tq[:, 3, :], tq[:, 4, :], ALU.add)\
                        .then_inc(*heads_ready.tick(0, i, QUADS - 1))
                    v.wait_ge(*heads_ready.at(0, i, QUADS - 1))
                for b in range(B):
                    residual(s, b)

            def one_hots(idx, n, upto):
                acc = tq[:, 2, 0:TILES * n].rearrange("p (t e) -> p t e", e=n)
                eq = tq[:, 3, 0:TILES * n].rearrange("p (t e) -> p t e", e=n)
                io = iota[:, 0:n].unsqueeze(1).to_broadcast([P, TILES, n])
                for k in range(upto):
                    i = idx[:, :, k:k + 1].to_broadcast([P, TILES, n])
                    then(V.tensor_tensor(eq if k else acc, io, i, ALU.is_equal))
                    if k:
                        then(V.tensor_tensor(acc, acc, eq, ALU.add))
                return acc

            def best(values8, index8, as_float, src, n):
                for t in range(TILES):
                    last = V.max(values8[:, t, :], src[:, t * n:(t + 1) * n])
                then(last)
                for t in range(TILES):
                    last = V.max_index(index8[:, t, :], values8[:, t, :], src[:, t * n:(t + 1) * n])
                then(last)
                then(V.tensor_copy(as_float, index8))

            v8 = lambda i: small[:, i, :].rearrange("p (t k) -> p t k", k=8)
            u8 = lambda i: small[:, i, :].bitcast(U32).rearrange("p (t k) -> p t k", k=8)

            def softmax_rows(s, n):
                slot = pairs.of("gate", s)
                v.wait_ge(*gate_psum.at(s))
                g = lambda ap: ap.rearrange("p (t e) -> p t e", e=n)
                wide_n = TILES * n
                src = g(PAIR[:, 2 * slot, 0:wide_n])
                logits = g(tq[:, 3, 0:wide_n])
                if s == 5:
                    V.tensor_tensor(logits, src, W["br"][:, :].unsqueeze(1).to_broadcast([P, TILES, n]), ALU.add)\
                        .then_inc(*gate_scored.tick(s))
                else:
                    V.tensor_copy(logits, src).then_inc(*gate_scored.tick(s))
                v.wait_ge(*gate_scored.at(s))
                then(V.tensor_reduce(small[:, 0, 0:TILES], logits, AX, ALU.max))
                V.tensor_tensor(g(tq[:, 0, 0:wide_n]), logits,
                                small[:, 0, 0:TILES].unsqueeze(2).to_broadcast([P, TILES, n]), ALU.subtract)\
                    .then_inc(*aside_ready.tick(s, "centred"))
                v.wait_ge(*aside_scalar.at(s, "exp"))
                then(V.tensor_reduce(small[:, 0, 0:TILES], g(tq[:, 1, 0:wide_n]), AX, ALU.add))
                then(V.reciprocal(small[:, 0, 8:8 + TILES], small[:, 0, 0:TILES]))
                then(V.tensor_tensor(g(tq[:, 4, 0:wide_n]), g(tq[:, 1, 0:wide_n]),
                                     small[:, 0, 8:8 + TILES].unsqueeze(2).to_broadcast([P, TILES, n]), ALU.mult))

            def experts0(s=2):
                for b in range(B):
                    ln(s, b)
                v.wait_ge(*loaded(s))
                v.wait_ge(*gate_scored.at(s))
                te = lambda ap: ap.rearrange("p (t e) -> p t e", e=E0)
                then(V.tensor_tensor(te(tq[:, 4, :]), te(tq[:, 0, :]),
                                     W["gbias0"][:, :].unsqueeze(1).to_broadcast([P, TILES, E0]), ALU.add))
                then(V.tensor_reduce(small[:, 0, :], tq[:, 4, :].rearrange("p (g e) -> p g e", e=E0 // GROUPS0),
                                     AX, ALU.max))
                best(v8(1), u8(2), v8(3), small[:, 0, :], GROUPS0)
                groups = one_hots(v8(3), GROUPS0, TOPG0)
                masked = tq[:, 1, :]
                ge = lambda ap: ap.rearrange("p (g e) -> p g e", e=E0 // GROUPS0)
                then(V.tensor_tensor(ge(masked), ge(tq[:, 4, :]),
                                     tq[:, 2, 0:TILES * GROUPS0].unsqueeze(2)
                                     .to_broadcast([P, TILES * GROUPS0, E0 // GROUPS0]), ALU.mult))
                best(v8(1), u8(2), v8(3), masked, E0)
                chosen = one_hots(v8(3), E0, TOP0)
                then(V.tensor_reduce(small[:, 0, 0:TILES], v8(1)[:, :, 0:TOP0], AX, ALU.add))
                then(V.tensor_scalar(small[:, 0, 8:8 + TILES], small[:, 0, 0:TILES], 1e-8, None, ALU.add))
                then(V.reciprocal(small[:, 0, 16:16 + TILES], small[:, 0, 8:8 + TILES]))
                then(V.tensor_tensor(te(tq[:, 3, :]), chosen, te(masked), ALU.mult))
                weights = te(tq[:, 3, :])
                over = small[:, 0, 16:16 + TILES].unsqueeze(2).to_broadcast([P, TILES, E0])
                for c in range(2):
                    last = V.tensor_tensor(tq4d[:, :, c * E0:(c + 1) * E0], weights, over, ALU.mult)
                last.then_inc(*aside_ready.tick(s, "doubled"))
                v.wait_ge(*aside_psum.at(s, "comb"))
                slot = pairs.of("combT", s)
                src = PAIR[:, 2 * slot:2 * slot + 2, :]
                rest = tq[:, 2:4, :]
                h2 = lambda ap: ap.rearrange("p (a n) -> p a n", a=2)
                up = slice(P // 2, P)
                V.memset(combB[0:P // 2, :], 0.0)
                then(V.tensor_copy(h2(combA[:, :]), src))
                V.tensor_tensor(rest, src, h2(combA[:, :]), ALU.subtract).then_inc(*aside_ready.tick(s, "comb"))
                v.wait_ge(*aside_ready.at(s, "comb"))
                then(V.tensor_copy(h2(combA[up, :]), rest[up]))
                V.memset(BANK[:, 0, :], 0.0)
                V.memset(BANK[:, 1, :], 0.0)
                V.tensor_tensor(h2(combB[up, :]), rest[up], h2(combA[up, :]), ALU.subtract)\
                    .then_inc(*aside_ready.tick(s, "zeroed"))

                v.wait_ge(*aside_scalar.at(s, "high"))
                V.tensor_tensor(r32(x_low), xnT[:, :], x_high, ALU.subtract).then_inc(*aside_ready.tick(s, "low"))

                def unit(i, k, h, shared=False):
                    v.wait_ge(m0_silu, 8 * i + 2 * k + h + 3)
                    positive_wait(v, m0_down, 8 * i + 2 * k + h + 1)
                    if shared:
                        V.tensor_tensor(hidden0[:, h, :], silu0[:, h, :], PAIR[:, 3 * h + 1, :], ALU.mult)\
                            .then_inc(m0_hidden, 1)
                        return
                    V.tensor_tensor(prod0[:, h, :], silu0[:, h, :], PAIR[:, 3 * h + 1, :], ALU.mult)\
                        .then_inc(m0_prod, 1)
                    v.wait_ge(m0_prod, 8 * i + 2 * k + h + 1)
                    V.tensor_tensor(hidden0[:, h, :], prod0[:, h, :], PAIR[:, 3 * h + 2, :], ALU.mult)\
                        .then_inc(m0_hidden, 1)

                unit(-1, 3, 0, True)
                unit(-1, 3, 1, True)
                for k in range(4):
                    unit(0, k, 0)
                    unit(0, k, 1)
                with v.Fori(1, PAIRS0 // 4) as i:
                    for k in range(4):
                        unit(i, k, 0)
                        unit(i, k, 1)
                v.wait_ge(m0_down, 2 * PAIRS0 + 2)
                for b in range(B):
                    xs = X[:, TPB * b:TPB * (b + 1), :]
                    V.tensor_tensor(xs, xs, BANK[:, b, :].rearrange("p (t d) -> p t d", d=D), ALU.add)\
                        .then_inc(*x_new.tick(s, b))

            def experts1(s=5):
                for b in range(B):
                    ln(s, b)
                v.wait_ge(*loaded(s))
                softmax_rows(s, E1)
                gates = tq[:, 4, 0:TILES * E1]
                best(v8(1), u8(2), v8(3), gates, E1)
                then(V.tensor_tensor(small[:, 0, 0:TILES], v8(1)[:, :, 0], v8(1)[:, :, 1], ALU.add))
                then(V.reciprocal(small[:, 0, 8:8 + TILES], small[:, 0, 0:TILES]))
                chosen = one_hots(v8(3), E1, 2)
                te = lambda ap: ap.rearrange("p (t e) -> p t e", e=E1)
                then(V.tensor_tensor(te(tq[:, 3, 0:TILES * E1]), chosen, te(gates), ALU.mult))
                V.tensor_tensor(comb[:, :, 0:E1], te(tq[:, 3, 0:TILES * E1]),
                                small[:, 0, 8:8 + TILES].unsqueeze(2).to_broadcast([P, TILES, E1]), ALU.mult)\
                    .then_inc(*aside_ready.tick(s, "combined"))
                v.wait_ge(*aside_psum.at(s, "comb"))
                slot = pairs.of("combT", s)
                V.tensor_copy(combT1[:, :].rearrange("p (a n) -> p a n", a=2), PAIR[0:E1, 2 * slot:2 * slot + 2, :])\
                    .then_inc(*aside_ready.tick(s, "comb"))
                v.wait_ge(*aside_psum.at(s, "beta"))
                slot = pairs.of("beta", s)
                xs = X[:, :, :].rearrange("p (a t) d -> p a (t d)", a=2)
                V.tensor_tensor(xs, xs, PAIR[:, 2 * slot:2 * slot + 2, :], ALU.add)\
                    .then_inc(*aside_ready.tick(s, "beta"))
                v.wait_ge(*aside_ready.at(s, "beta"))

                v.wait_ge(*aside_scalar.at(s, "high"))
                V.tensor_tensor(r32(x_low), xnT[:, :], x_high, ALU.subtract).then_inc(*aside_ready.tick(s, "low"))

                def hidden(e, h, fb):
                    u = 8 * e + 4 * h + fb
                    v.wait_ge(m1_silu, u + 1)
                    positive_wait(v, m1_down, u - 3)
                    V.tensor_tensor(hidden1[:, fb, :], silu1[:, fb % 2, :], PAIR[:, 2 * (fb % 2) + 1, :], ALU.mult)\
                        .then_inc(m1_prod, 1)

                def moments(n, h):
                    v.wait_ge(m1_down, 4 * n + 4)
                    for t in range(TPB):
                        last = V.bn_stats(st1[:, TPB * h + t, :], BANK[:, h, col(t)])
                    last.then_inc(m1_stat, 1)

                def aggregate(n, h):
                    for t in range(TPB):
                        last = V.bn_aggr(mv1[:, TPB * h + t, :], st1[:, TPB * h + t, :])
                    last.then_inc(m1_var, 1)

                def scales(n, h, e):
                    hs = slice(TPB * h, TPB * (h + 1))
                    v.wait_ge(m1_rstd, n + 1)
                    V.tensor_tensor(sc1[:, hs], rs1[:, hs], comb[:, hs, e], ALU.mult).then_inc(m1_rescale, 1)
                    v.wait_ge(m1_rescale, n + 1)
                    V.scalar_tensor_tensor(shift1[:, hs], mv1[:, hs, 0], -1.0, sc1[:, hs], ALU.mult, ALU.mult)\
                        .then_inc(m1_scale, 1)

                def expert(e, first=False):
                    for h in range(2):
                        n = 2 * e + h
                        for fb in range(4):
                            if fb == 3 and not (first and h == 0):
                                v.wait_ge(m1_stat, n)
                            hidden(e, h, fb)
                            if fb == 0 and not first:
                                scales(n - 2, h, e - 1)
                            if fb == 2 and not (first and h == 0):
                                moments(n - 1, 1 - h)
                            if fb == 3 and not (first and h == 0):
                                aggregate(n - 1, 1 - h)

                expert(0, True)
                with v.Fori(1, E1 // 2) as i:
                    expert(2 * i - 1)
                    expert(2 * i)
                expert(E1 - 1)
                scales(2 * E1 - 2, 0, E1 - 1)
                moments(2 * E1 - 1, 1)
                v.wait_ge(m1_stat, 2 * E1)
                aggregate(2 * E1 - 1, 1)
                scales(2 * E1 - 1, 1, E1 - 1)
                v.wait_ge(m1_added, 2 * E1)
                for b in range(B):
                    V.memset(small[:, b, 0:1], 0.0).then_inc(*x_new.tick(s, b))

            def state_space(s=6):
                v.wait_ge(*x_new.at(s - 1, 1))
                V.memset(hpre[:, :, 0:LEFT], 0.0).then_inc(*aside_ready.tick(s, "padding"))
                for b in range(B):
                    ln(s, b)
                v.wait_ge(*loaded(s))
                v.wait_ge(*aside_ready.at(s, "padding"))
                for b in range(B):
                    v.wait_ge(*aside_scalar.at(s, "h", b))
                    for k in range(NCONV):
                        for c in range(CH):
                            src, dst, w = hpre[:, b * CH + c, k:k + SEQ], wide[:, b * CH + c, :], W["convw"][:, c, k:k + 1]
                            if k == 0:
                                last = V.tensor_scalar(dst, src, w, None, ALU.mult)
                            else:
                                last = V.scalar_tensor_tensor(dst, src, w, dst, ALU.mult, ALU.add)
                        if k < NCONV - 1:
                            then(last)
                    last.then_inc(*aside_ready.tick(s, "conv", b))
                v.wait_ge(*aside_psum.at(s, "xp", 1))
                v.wait_ge(*aside_scalar.at(s, "input"))
                slot = banks.of("hsum", s)
                for b in range(B):
                    rows = slice(ROWS * b, ROWS * b + NSTATE)
                    last = V.tensor_tensor(tokst[rows, 1, :], tokst[rows, 1, :], BANK[rows, slot, :], ALU.mult)
                then(last)
                v.wait_ge(*aside_scalar.at(s, "decay"))
                for b in range(B):
                    rows = slice(ROWS * b, ROWS * b + NSTATE)
                    last = V.tensor_tensor_scan(tokst[rows, 2, :], tokst[rows, 3, :], tokst[rows, 1, :], 0.0,
                                                ALU.mult, ALU.add)
                last.then_inc(*aside_ready.tick(s, "scanned"))
                for b in range(B):
                    residual(s, b)

            def dispatch_experts(s=8):
                for b in range(B):
                    ln(s, b)
                v.wait_ge(*loaded(s))
                softmax_rows(s, E2)
                gates = tq[:, 4, 0:TILES * E2]
                best(v8(1), u8(2), v8(3), gates, E2)
                onehot = one_hots(v8(3), E2, 1)
                V.tensor_copy(onehotB[:, :, :], onehot).then_inc(*aside_ready.tick(s, "onehot"))
                v.wait_ge(*aside_psum.at(s, "cumsum"))
                slot = pairs.of("cumsum", s)
                counts = PAIR[:, 2 * slot, 0:TILES * E2].rearrange("p (t e) -> p t e", e=E2)
                t3 = tq[:, 3, 0:TILES * E2].rearrange("p (t e) -> p t e", e=E2)
                then(V.tensor_tensor(t3, counts, onehot, ALU.mult))
                then(V.tensor_reduce(small[:, 0, 0:TILES], t3, AX, ALU.add))
                then(V.tensor_scalar(small[:, 0, 8:16], small[:, 0, 0:8], float(CAP), None, ALU.is_le))
                then(V.scalar_tensor_tensor(small[:, 0, 16:24], v8(3)[:, :, 0], float(CAP), small[:, 0, 0:8],
                                            ALU.mult, ALU.add))
                then(V.tensor_tensor(small[:, 0, 24:32], small[:, 0, 16:24], small[:, 0, 8:16], ALU.mult))
                V.tensor_copy(small[:, 0, 40:48], v8(1)[:, :, 0])
                V.tensor_scalar(small[:, 0, 32:40], small[:, 0, 24:32], -1.0, None, ALU.add)\
                    .then_inc(*aside_ready.tick(s, "slots"))
                v.wait_ge(*aside_ready.at(s, "slots"))
                token_slot = small[:, 0, 32:40]
                for t in range(TILES):
                    last = V.tensor_scalar(diag2[:, t, :], ident[:, :], token_slot[:, t:t + 1], None, ALU.mult)
                last.then_inc(*aside_ready.tick(s, "diagonal"))
                places = small[:, 1, :].rearrange("p (e t) -> p e t", e=E2)
                for e in range(E2):
                    last = V.tensor_scalar(places[:, e, :], token_slot, float(CAP * e), None, ALU.subtract)
                then(last)
                v.wait_ge(*aside_pool.at(s, "own"))
                v.wait_ge(*aside_psum.at(s, "rows"))
                slot = pairs.of("rows", s)
                V.tensor_copy(slot_rows.rearrange("p (a n) -> p a n", a=2), PAIR[:, 2 * slot:2 * slot + 2, :])\
                    .then_inc(*aside_ready.tick(s, "rows"))
                v.wait_ge(*aside_ready.at(s, "rows"))
                for e in range(E2):
                    if e >= 2:
                        v.wait_ge(*aside_psum.at(s, "combined", e - 2))
                    V.tensor_tensor(disp2[e % 2], iota[:, :].unsqueeze(1).to_broadcast([P, TILES, CAP]),
                                    places[:, e, :].unsqueeze(2).to_broadcast([P, TILES, CAP]), ALU.is_equal)
                    V.tensor_scalar(combT2[e % 2], slot_rows, own_slot[:, e:e + 1], None, ALU.is_equal)\
                        .then_inc(*aside_ready.tick(s, "dispatch", e))
                v.wait_ge(*aside_psum.at(s, "combined", E2 - 1))
                for b in range(B):
                    slot = banks.of("out", s, b)
                    for t in range(TPB):
                        k = TPB * b + t
                        last = V.scalar_tensor_tensor(X[:, k, :], BANK[:, slot, col(t)], small[:, 0, 40 + k:41 + k],
                                                      X[:, k, :], ALU.mult, ALU.add)
                    last.then_inc(*x_new.tick(s, b))

            def linear(s=11):
                for b in range(B):
                    ln(s, b)
                for b in range(B):
                    residual(s, b)

            for s in range(STAGES):
                if s in ATTN:
                    attention(s)
                else:
                    {0: pair_attention, 2: experts0, 5: experts1, 6: state_space, 8: dispatch_experts, 11: linear}[s]()

        @block.gpsimd
        def _(pool):
            G = nc.gpsimd
            then = chain(pool_step, pool)
            G.memset(ident[:, :], 0.0)
            G.memset(ones[:, :], 1.0)
            G.memset(plushalf[:, :], 0.5)
            then(G.memset(minushalf[:, :], -0.5))
            G.affine_select(out=ident[:, :], in_=ident[:, :], compare_op=ALU.not_equal, fill=1.0, base=0,
                            pattern=[[-1, P]], channel_multiplier=1).then_inc(*consts.tick("ident"))

            def power(out, in_, exponent, tick):
                G.tensor_tensor(out, in_, exponent, ALU.pow).then_inc(*tick)

            def ln(s, b):
                ts = slice(TPB * b, TPB * (b + 1))
                pool.wait_ge(*ln_var.at(s, b))
                then(G.tensor_scalar(vareps[:, ts], meanvar[:, ts, 1], 1e-5, None, ALU.add))
                power(rstd[:, ts], vareps[:, ts], minushalf[:, 0:TPB], ln_rstd.tick(s, b))

            def other_constants():
                if moe1:
                    G.memset(epsilon[:, :], 1e-5)
                G.memset(above[:, :], 0.0)
                G.memset(below[:, :], 0.0)
                G.memset(negmax[:, :, :, :], 0.0)
                G.memset(vaug[:, :, :, :], 1.0)
                then(G.memset(tokst[:, :, :], 0.0))
                G.affine_select(out=above[:, :], in_=above[:, :], compare_op=ALU.is_ge, fill=-BIG, base=0,
                                pattern=[[-1, P]], channel_multiplier=1)
                G.affine_select(out=below[:, :], in_=below[:, :], compare_op=ALU.is_ge, fill=-BIG, base=0,
                                pattern=[[1, P]], channel_multiplier=-1)
                G.iota(iota[:, :], pattern=[[1, P]], base=0, channel_multiplier=0,
                       allow_small_or_imprecise_dtypes=True).then_inc(*consts.tick("all"))

            for s in range(STAGES):
                cfg = ATTN.get(s)
                if s == 0:
                    pool.wait_ge(*aside_ready.at(0, "norm"))
                    power(small[:, 2, 0:2], small[:, 1, 0:2], plushalf[:, 0:2], aside_pool.tick(0, "norm"))
                    for b in range(B):
                        ln(s, b)
                    other_constants()
                    if moe0:
                        then(G.memset(pick0[:, :, :], 0.0))
                        for r in range(2):
                            v4 = pick0[r * E0:(r + 1) * E0, :, :].rearrange("p n (a m) -> p n a m", a=2)
                            G.affine_select(out=v4, in_=v4, compare_op=ALU.not_equal, fill=1.0, base=0,
                                            pattern=[[-2, PAIRS0], [-1, 2], [0, P // 2]], channel_multiplier=1)\
                                .then_inc(*aside_pool.tick(2, "pick", r))
                            pool.wait_ge(*aside_pool.at(2, "pick", r))
                    if STAGES > 8:
                        G.memset(onesB[:, :], 1.0)
                        then(G.memset(tri[:, :], 1.0))
                        G.affine_select(out=tri[:, :], in_=tri[:, :], compare_op=ALU.is_ge, fill=0.0, base=0,
                                        pattern=[[1, P]], channel_multiplier=-1).then_inc(*aside_pool.tick(8, "triangle"))
                        G.iota(own_slot[:, :], pattern=[[CAP, E2]], base=0, channel_multiplier=1,
                               allow_small_or_imprecise_dtypes=True).then_inc(*aside_pool.tick(8, "own"))
                    continue
                if s == 10:
                    pool.wait_ge(*x_new.at(s - 1, 0))
                    G.memset(tokst[:, :, :], 0.0).then_inc(*aside_pool.tick(s, "cleared"))
                for b in range(B):
                    ln(s, b)
                if s == 2:
                    def weights_low(i, k):
                        pool.wait_ge(m0_whigh, 4 * i + k + 2)
                        w = slice(2 * k * P, 2 * (k + 1) * P)
                        G.tensor_tensor(r32(low[:, w]), ring0[:, k, 0:2, :].rearrange("p a n -> p (a n)"), high[:, w],
                                        ALU.subtract).then_inc(m0_wlow, 1)

                    weights_low(-1, 3)
                    with pool.Fori(0, PAIRS0 // 4) as i:
                        for k in range(4):
                            weights_low(i, k)
                if s == 5:
                    pool.wait_ge(*aside_ready.at(s, "beta"))
                    pool.wait_ge(*loaded(s))

                    def weights_low(e, k, a):
                        G.tensor_tensor(r32(w_low(k, a, slice(0, F1))), ring1[:, k, a, :],
                                        w_high(k, a, slice(0, F1)), ALU.subtract).then_inc(m1_wlow, 1)

                    def rstd1(n, h):
                        hs = slice(TPB * h, TPB * (h + 1))
                        pool.wait_ge(m1_var, n + 1)
                        positive_wait(pool, m1_added, n)
                        G.tensor_tensor(ve1[:, hs], mv1[:, hs, 1], epsilon[:, 0:TPB], ALU.add).then_inc(m1_eps, 1)
                        pool.wait_ge(m1_eps, n + 1)
                        G.tensor_tensor(rs1[:, hs], ve1[:, hs], minushalf[:, 0:TPB], ALU.pow).then_inc(m1_rstd, 1)

                    def add1(n, k, h, loads):
                        pool.wait_ge(m1_gamma[k], loads)
                        pool.wait_ge(m1_norm, n + 1)
                        y = norm1[:, h, :].rearrange("p (t d) -> p t d", d=D)
                        gm = gammarow[:, k, :].unsqueeze(1).to_broadcast([P, TPB, D])
                        G.tensor_tensor(y, y, gm, ALU.mult).then_inc(m1_scaled, 1)
                        pool.wait_ge(m1_scaled, n + 1)
                        xs = X[:, TPB * h:TPB * (h + 1), :]
                        G.tensor_tensor(xs, xs, y, ALU.add).then_inc(m1_added, 1)

                    def expert(e, k, loads, first=False, last=False):
                        for h in range(2):
                            n = 2 * e + h
                            if not first:
                                add1(n - 2, 1 - k, h, loads)
                            if not last:
                                pool.wait_ge(m1_whigh, 2 * e + h + 3)
                                weights_low(e + 1, 1 - k, h)
                            if not (first and h == 0):
                                rstd1(n - 1, 1 - h)

                    for a in range(2):
                        pool.wait_ge(m1_whigh, a + 1)
                        weights_low(0, 0, a)
                    expert(0, 0, 0, first=True)
                    with pool.Fori(1, E1 // 2) as i:
                        expert(2 * i - 1, 1, 16 * i)
                        expert(2 * i, 0, 16 * i)
                    expert(E1 - 1, 1, 16 * (E1 // 2), last=True)
                    add1(2 * E1 - 2, 1, 0, 16 * (E1 // 2))
                    rstd1(2 * E1 - 1, 1)
                    add1(2 * E1 - 1, 1, 1, 16 * (E1 // 2))
    return made


def kernel(**inputs):
    import concourse.bacc as _bacc
    from concourse.bass_utils import run_bass_kernel_spmd as _run

    given = {k: np.asarray(v) for k, v in inputs.items()}
    tiles = layout(given)
    more = {k: v for k, v in streams(given).items() if STAGES > {"stream0": 2, "stream1": 5, "gamma": 5, "stream2": 8}[k]}

    def program(plan):
        nc = _bacc.Bacc("TRN2", target_bir_lowering=False, num_devices=1)
        arrays = {"x": np.ascontiguousarray(given["x"])}
        arrays.update({k: a for k, (a, _, _) in tiles.items()})
        arrays.update(more)
        dram = {k: nc.dram_tensor("in_" + k, a.shape, mybir.dt.from_np(a.dtype), kind="ExternalInput").ap()
                for k, a in arrays.items()}
        out = nc.dram_tensor("out_0", (B, SEQ, D), F32, kind="ExternalOutput").ap()
        made = build(nc, tiles, None, dram, out, plan)
        return nc, made, {"in_" + k: np.ascontiguousarray(a) for k, a in arrays.items()}

    _, plan, _ = program({})
    nc, _, arrays = program(plan)
    r = _run(nc, [arrays], core_ids=[0])
    return r.results[0]["out_0"]
```

```python
from contextlib import ExitStack

import numpy as np

import concourse.bass as bass
from concourse import mybir

STAGES = 12

P = 128
B, SEQ, D = 2, 512, 128
TILES = B * SEQ // P
TPB = SEQ // P
H, HD = 16, 8
QUADS, PER = 4, 4
ROWS = 32
AUG = 24
NCTX, NCTXP = 77, 78
BIG = float(2 ** 100)
SCALE = float(np.float32(HD ** -0.5))
E0, PAIRS0, TOP0, GROUPS0, TOPG0 = 64, 32, 6, 8, 4
E1, F1 = 16, 512
E2, F2, CAP = 8, 512, 128
NSTATE, NCONV, CH = 16, 4, 2
LEFT = NCONV - 1
SPREAD = P

ALU = mybir.AluOpType
ACT = mybir.ActivationFunctionType
F32, F32R, BF16 = mybir.dt.float32, mybir.dt.float32r, mybir.dt.bfloat16
I32, U32, U8 = mybir.dt.int32, mybir.dt.uint32, mybir.dt.uint8
AX = mybir.AxisListType.X

ATTN = {
    1: dict(cross=True, add="mask"),
    3: dict(cross=False, heads="rope"),
    4: dict(cross=True, obias=True),
    7: dict(cross=True, add="bias", bias=True, obias=True, hscale=True),
    9: dict(cross=False, bias=True, obias=True, mixed=True),
    10: dict(cross=True, heads="norm", obias=True, sigmoid=True),
}

REUSES = {"wq_7": "wq_1", "wk_7": "wk_1", "cross_9": "wq_4", "shift_9": "wk_4"}
LATE = 7
LINEAR = 11


def stack_columns(w):
    out = np.zeros((w.shape[0], QUADS, PER, ROWS), w.dtype)
    out[..., :3 * HD] = np.tile(w.reshape(w.shape[0], QUADS, PER, HD), (1, 1, 1, 3))
    return out.reshape(w.shape[0], QUADS, P)


def stack_bias(b):
    return np.ascontiguousarray(stack_columns(b.reshape(1, D))[0].T)


def head_blocks(m):
    out = np.zeros((H, HD, H, HD), m.dtype)
    for h in range(H):
        out[h, :, h, :] = m[h]
    return out.reshape(D, D)


def layout(i):
    t = {}

    def put(stage, name, a, rows=False):
        t[name] = (np.ascontiguousarray(a), stage, rows)

    row = lambda a: a.reshape(-1)
    f = np.float32
    lo = np.zeros((PER, ROWS, 2), f)
    lo[:, 2 * HD:3 * HD, 0] = 1.0
    lo[:, HD:2 * HD, 1] = 1.0
    put(-1, "lorows", lo.reshape(P, 2))
    kone = np.zeros((PER, ROWS, QUADS), f)
    kone[:, AUG] = 1.0
    kone = kone.reshape(P, QUADS)
    put(-1, "kone", kone)
    rows = np.zeros((PER, ROWS, PER), f)
    for j in range(PER):
        rows[j, :, j] = 1.0
    put(-1, "headrows", rows.reshape(P, PER))
    c = np.zeros((D, B, NCTXP), f)
    c[:, :, :NCTX] = i["ctx_1024"].transpose(2, 0, 1)
    put(-1, "ctxT", c)
    for n in "qv":
        put(0, f"dirT_{n}", i[f"L0_attn_dir_{n}"].T)
        put(0, f"A_{n}", i[f"L0_attn_A_{n}"])
        put(0, f"BT_{n}", i[f"L0_attn_B_{n}"].T)
        put(0, f"mag_{n}", i[f"L0_attn_mag_{n}"].reshape(1), True)
    put(0, "kwT_0", i["L0_attn_k_w"].T)
    for n, k in (("q", "bias_q"), ("k", "k_b"), ("v", "bias_v")):
        put(0, f"b{n}_0", i[f"L0_attn_{k}"], True)
    put(0, "wo_0", i["L0_attn_out_w"].T)
    put(0, "bo_0", i["L0_attn_out_b"].reshape(1, D))
    put(1, "wq_1", stack_columns(i["L0_xattn_W_q"].T))
    put(1, "wk_1", stack_columns(i["L0_xattn_W_k"].T))
    put(1, "wv_1", i["L0_xattn_W_v"].T)
    put(1, "wo_1", i["L0_xattn_W_o"].T)
    m = i["mask_1x1xSxS2_if1"].reshape(SEQ, NCTX)
    mq = np.zeros((SEQ, NCTXP), m.dtype)
    mq[:, :NCTX] = m
    put(1, "maskq", mq.reshape(TPB, P, NCTXP).transpose(1, 0, 2))
    put(1, "maskT", m.T)
    put(2, "gate0", i["L0_ffn_gate_w"].T)
    put(2, "gbias0", i["L0_ffn_gate_bias"], True)
    kqv = i["L1_attn_W_kqv"]
    put(3, "wk_3", kqv[0:D].T)
    put(3, "wq_3", kqv[D:2 * D].T)
    put(3, "wv_3", kqv[2 * D:].T)
    put(3, "wo_3", i["L1_attn_W_proj"].T)
    put(3, "nq_3", i["L1_attn_q_norm_w"], True)
    put(3, "nk_3", i["L1_attn_k_norm_w"], True)
    inv = (1.0 / (f(10000.0) ** (np.arange(0, HD, 2, dtype=f) / f(HD)))).astype(f)
    ang = (np.arange(SEQ, dtype=f)[:, None] * inv[None, :]).astype(f)
    ang = np.concatenate((ang, ang), -1).reshape(TPB, P, HD).transpose(1, 0, 2)
    sgn = np.ones(HD, f)
    sgn[:HD // 2] = -1.0
    put(3, "cos", np.cos(ang).astype(f))
    put(3, "sin", (np.sin(ang) * sgn).astype(f))
    put(4, "wq_4", stack_columns(i["L1_xattn_W_q"]))
    put(4, "wk_4", stack_columns(i["L1_xattn_W_kv"][:, :D]))
    put(4, "wv_4", i["L1_xattn_W_kv"][:, D:])
    put(4, "wo_4", i["L1_xattn_W_proj"])
    put(4, "bo_4", i["L1_xattn_b_proj"].reshape(1, D))
    put(5, "wr", i["L1_ffn_Wr"])
    put(5, "br", i["L1_ffn_br"], True)
    put(5, "beta", i["L1_ffn_beta"])
    put(6, "inw", i["L2_attn_in_w"].T)
    put(6, "inb", i["L2_attn_in_b"].reshape(CH, P).T)
    put(6, "convw", i["L2_attn_conv_w"].reshape(CH, P, NCONV).transpose(1, 0, 2))
    put(6, "convb", i["L2_attn_conv_b"].reshape(CH, P).T)
    put(6, "xpw", i["L2_attn_xp_w"].T.reshape(CH, P, 2 * NSTATE).transpose(1, 0, 2))
    xb = np.zeros((2, 2, NSTATE, 2), f)
    xb[:, 0] = i["L2_attn_xp_b"].reshape(2, NSTATE).T
    put(6, "xpb", xb.reshape(4 * NSTATE, 2))
    ow = np.zeros((2, 2, NSTATE, D), f)
    ow[:, 0] = i["L2_attn_out_w"].T
    put(6, "ssmo", ow.reshape(4 * NSTATE, D))
    ob = np.zeros((ROWS + 1, D), f)
    ob[0] = ob[ROWS] = i["L2_attn_out_b"]
    put(6, "bo_6", ob)
    ipw, ipb = i["L2_xattn_in_proj_weight"], i["L2_xattn_in_proj_bias"]
    put(7, "wq_7", stack_columns(ipw[:D].T))
    put(7, "wk_7", stack_columns(ipw[D:2 * D].T))
    put(7, "wv_7", ipw[2 * D:].T)
    put(7, "bq_7", stack_bias(ipb[:D]))
    put(7, "bk_7", np.where(kone > 0, kone, stack_bias(ipb[D:2 * D])))
    put(7, "bv_7", ipb[2 * D:], True)
    put(7, "wo_7", i["L2_xattn_out_w"].T)
    put(7, "bo_7", i["L2_xattn_out_b"].reshape(1, D))
    put(7, "hs_7", i["L2_xattn_head_scales"], True)
    fs = i["fside_BxSxS2_0"]
    fq = np.zeros((B, SEQ, NCTXP), fs.dtype)
    fq[:, :, :NCTX] = fs
    put(7, "biasq", fq.reshape(B, TPB, P, NCTXP).transpose(2, 0, 1, 3))
    put(7, "biasT", fs.transpose(2, 0, 1))
    kpp = np.zeros((B, NCTXP, 4), np.uint8)
    kpp[:, :NCTX, 0] = i["mask_BxS2_bf0"].view(np.uint8)
    kpp = kpp.view(np.int32)[..., 0]
    put(7, "padq", kpp.reshape(-1), True)
    put(7, "padT", kpp[:, :NCTX].T)
    put(8, "wg", i["L2_ffn_wg"])
    put(9, "wq_9", i["L3_attn_Wq"].T)
    put(9, "bqc_9", i["L3_attn_bq"].reshape(D, 1))
    put(9, "wk_9", stack_columns(i["L3_attn_Wk"].T))
    put(9, "bk_9", np.where(kone > 0, kone, stack_bias(i["L3_attn_bk"])))
    put(9, "wv_9", i["L3_attn_Wv"].T)
    put(9, "bv_9", i["L3_attn_bv"], True)
    put(9, "wo_9", i["L3_attn_Wo"].T)
    put(9, "bo_9", i["L3_attn_bo"].reshape(1, D))
    put(9, "cross_9", stack_columns(head_blocks(i["L3_attn_W_cross"])))
    sw = i["L3_attn_shift_weights"]
    toep = np.zeros((H, HD, HD), sw.dtype)
    for a in range(HD):
        for b in range(a, min(HD, a + sw.shape[1])):
            toep[:, a, b] = sw[:, b - a]
    put(9, "shift_9", stack_columns(head_blocks(toep)))
    put(9, "gate_9", np.repeat(i["L3_attn_gate"], HD).reshape(D, 1))
    for n in "qkv":
        put(10, f"w{n}_10", i[f"L3_xattn_W{n}"].T)
    for n in ("gq", "bq", "gk", "bk"):
        put(10, f"{n}_10", i[f"L3_xattn_{n}"], True)
    put(10, "wo_10", i["L3_xattn_Wo"].T)
    put(10, "bo_10", i["L3_xattn_bo"].reshape(1, D))
    put(11, "w_11", i["L3_ffn_W"].T)
    put(11, "b_11", i["L3_ffn_b"].reshape(1, D))
    put(11, "vr_11", i["L3_ffn_V_r"])
    put(11, "c_11", i["L3_ffn_C"].T)
    return {k: v for k, v in t.items() if v[1] < STAGES}


def streams(i):
    pair = lambda w: w.reshape(PAIRS0, P, D).transpose(0, 2, 1)
    s0 = np.empty((PAIRS0 + 1, P, 3, P), np.float32)
    s0[0, :, 0], s0[0, :, 1] = i["L0_ffn_sg_w"].T, i["L0_ffn_su_w"].T
    s0[0, :, 2] = i["L0_ffn_sd_w"].T
    s0[1:, :, 0], s0[1:, :, 1] = pair(i["L0_ffn_eg_w"]), pair(i["L0_ffn_eu_w"])
    s0[1:, :, 2] = i["L0_ffn_ed_w"].transpose(0, 2, 1).reshape(PAIRS0, P, D)
    s1 = np.empty((E1, P, 3, F1), np.float32)
    s1[:, :, 0], s1[:, :, 1] = i["L1_ffn_W1"], i["L1_ffn_W3"]
    s1[:, :, 2] = i["L1_ffn_W2"].reshape(E1, F1 // P, P, D).transpose(0, 2, 1, 3).reshape(E1, P, F1)
    s2 = np.empty((E2, P, 2, F2), np.float32)
    s2[:, :, 0] = i["L2_ffn_w1"]
    s2[:, :, 1] = i["L2_ffn_w2"].reshape(E2, F2 // P, P, D).transpose(0, 2, 1, 3).reshape(E2, P, F2)
    return {"stream0": s0, "stream1": s1, "gamma": i["L1_ffn_gamma"], "stream2": s2}


class Signal:

    def __init__(self, sem, planned):
        self.sem, self.planned, self.made = sem, planned, {}

    def tick(self, *step):
        assert step not in self.made, step
        self.made[step] = len(self.made) + 1
        return self.sem, 1

    def at(self, *step):
        assert not self.planned or step in self.planned, step
        return self.sem, self.planned.get(step, 1)


class Slots:

    def __init__(self, count, base, planned):
        self.count, self.base, self.planned, self.made = count, base, planned, {}
        self.readers = [None] * count

    def take(self, pe, reader, step, use):
        n = len(self.made) % self.count
        self.made[use] = slot = self.base + n
        if self.readers[n] is not None:
            before, then = self.readers[n]
            pe.wait_ge(*before.at(*then))
        self.readers[n] = (reader, step)
        return slot

    def of(self, *use):
        return self.planned.get(use, 0)


def prepare_steps(s):
    cfg = ATTN[s]
    steps = [("ln",)]
    if cfg["cross"]:
        steps += [("context",)]
        if cfg.get("heads"):
            steps += [("root", "k"), ("stack", "k", 0)]
    elif cfg.get("heads"):
        steps += [("values",)]
    else:
        steps += [("values",), ("stack", "k", 0), ("stack", "k", 1)]
    if cfg.get("mixed"):
        steps += [("mix",)]
    if cfg.get("heads"):
        steps += [("tokens", "q"), ("root", "q")]
        if cfg["cross"]:
            steps += [("stack", "q", 0), ("stack", "q", 1)]
        else:
            steps += [("tokens", "k"), ("stack", "q", 0), ("stack", "q", 1), ("root", "k"), ("stack", "k", 0),
                      ("stack", "k", 1)]
    else:
        steps += [("stack", "q", 0), ("stack", "q", 1)]
    if cfg.get("sigmoid"):
        return steps
    if cfg["cross"]:
        steps += [("spread",)]
        groups = [[("max", t, gp) for t in range(TPB)] for gp in range(2)]
        augs = [[("aug", 2 * gp), ("aug", 2 * gp + 1)] for gp in range(2)]
    else:
        groups = [[("max", g, t, jp) for t in range(TPB) for jp in range(2)] for g in range(QUADS)]
        augs = [[("aug", g)] for g in range(QUADS)]
    before = []
    for group, aug in zip(groups, augs):
        for n, step in enumerate(group):
            steps += [step] + (before[:1] if n else [])
            before = before[1:] if n else before
        before = aug
    return steps + before


def units(s):
    return [(g, kb, jp) for g in range(QUADS) for kb in range(1 if ATTN[s]["cross"] else TPB) for jp in range(2)]


WEIGHT = dict(ln=2.0, context=1.0, values=1.0, mix=1.0, tokens=4.0, root=3.0, stack=1.0, spread=1.0, max=0.8, aug=0.8,
              product=2.0)


def interleave(prepared, attended):
    weigh = lambda step: WEIGHT[step[3][0]]
    total = sum(map(weigh, prepared))
    order, k, done = [], 0, 0.0
    cost = lambda step: 0 if step[3][0] in ("ln", "root", "values", "mix", "aug", "spread") else 1
    for n, unit in enumerate(attended):
        order.append(unit)
        room = 1 if unit[3] != ("finish",) and unit[3][0] and unit[3][1:] == (0, 1) else 2
        while k < len(prepared) and done * len(attended) < total * (n - 0.5) and cost(prepared[k]) <= room:
            room -= cost(prepared[k])
            done += weigh(prepared[k])
            order.append(prepared[k])
            k += 1
    return order + prepared[k:]


def schedule(stages):
    order, attending = [], []
    for s in range(stages):
        if s == LINEAR:
            for b in range(B):
                order += interleave([("linear", s, b, ("ln",)), ("linear", s, b, ("product",))], attending)
                attending = []
            continue
        if s not in ATTN:
            if s:
                for b in range(B):
                    order += interleave([("ln", s, b, ("ln",))], attending)
                    attending = []
            order.append(("stage", s, 0, ()))
            continue
        for b in range(B):
            order += interleave([("prepare", s, b, step) for step in prepare_steps(s)], attending)
            attending = [("attend", s, b, u) for u in units(s) + [("finish",)]]
    return order + attending


def positive_wait(eng, sem, value):
    if not (isinstance(value, int) and value <= 0):
        eng.wait_ge(sem, value)


def build(nc, tiles, shapes, dram, out, plan):
    made = {}
    ctx = ExitStack()
    with ctx:
        def sb(name, shape, dt=F32):
            return ctx.enter_context(nc.sbuf_tensor(name, list(shape), dt))

        def plain(name):
            return ctx.enter_context(nc.semaphore(name))

        def signal(name):
            s = Signal(plain(name), plan.get(name, {}))
            made[name] = s.made
            return s

        def slots(name, count, base=0):
            s = Slots(count, base, plan.get(name, {}))
            made[name] = s.made
            return s

        PAIR = ctx.enter_context(nc.psum_tensor("PAIR", [P, 6, 512], F32))
        BANK = ctx.enter_context(nc.psum_tensor("BANK", [P, 2, 512], F32))
        pairs, banks, sums = slots("pairs", 3), slots("banks", 1), slots("sums", 1, 1)
        order = schedule(STAGES)

        X = sb("X", [P, TILES, D])
        xn = sb("xn", [P, TILES, D])
        xnT = sb("xnT", [P, B * SEQ])
        stats = sb("stats", [P, TILES, 6])
        meanvar = sb("meanvar", [P, TILES, 2])
        vareps = sb("vareps", [P, TILES])
        rstd = sb("rstd", [P, TILES])
        ident = sb("ident", [P, P])
        identR = sb("identR", [P, P])
        identB = sb("identB", [P, P], BF16)
        above = sb("above", [P, P], BF16)
        below = sb("below", [P, P], BF16)
        ones = sb("ones", [P, P])
        minushalf = sb("minushalf", [P, 64])
        plushalf = sb("plushalf", [P, 64])
        qst = sb("qst", [P, B, QUADS, SEQ])
        kst = sb("kst", [P, B, QUADS, SEQ])
        lopart = sb("lopart", [P, 2, 2, 512])
        negmax = sb("negmax", [P, TPB, QUADS, P])
        probs = sb("probs", [P, 4, 2, 512])
        vaug = sb("vaug", [P, B, TPB, H * (HD + 1) + ROWS])
        pvT = sb("pvT", [P, 2, 512])
        rden = sb("rden", [P, TPB, PER])
        heads = sb("heads", [P, B, TPB, D])
        headsT = sb("headsT", [P, B, SEQ])
        addq = sb("addq", [P, B, TPB, NCTXP])
        addT = sb("addT", [NCTX, B, 2, SEQ])
        tokst = sb("tokst", [P, TPB, 512])
        tq = sb("tq", [P, 5, 512])
        small = sb("small", [P, 4, 64])
        blo = sb("blo", [P, 2, QUADS])
        W = {}
        for n, (a, _, rows) in tiles.items():
            W[n] = W[REUSES[n]] if n in REUSES else sb(
                "w_" + n, [P if rows else a.shape[0]] + ([a.size] if rows else list(a.shape[1:])),
                mybir.dt.from_np(a.dtype))
        stage_of = {n: s for n, (_, s, _) in tiles.items()}
        s_load = {s: plain(f"weights_loaded_{s + 1}") for s in range(-1, STAGES)}
        s_x = plain("x_loaded")
        s_out = plain("out_stored")

        def loaded(s):
            return s_load[s], 16 * sum(v == s for v in stage_of.values())

        names = ("consts", "vector_step", "scalar_step", "pool_step", "ln_var", "ln_rstd", "xn_ready", "xnT_psum",
                 "xnT_ready", "x_new", "proj_psum", "lo_ready", "stack_ready", "v_ready", "max_psum", "max_read",
                 "negmaxT_psum", "aug_ready", "score_psum", "probs_ready", "pv_done",
                 "pvT_ready", "pv_psum", "spread_ready", "heads_ready", "headsT_psum",
                 "headsT_ready", "out_psum", "tok_psum", "tok_read", "tok_square", "tok_power", "tok_stacked",
                 "add_ready", "mixed_ready", "qc_ready", "gate_psum", "gate_scored", "aside_psum", "aside_ready",
                 "aside_scalar", "aside_pool")
        S = {n: signal(n) for n in names}
        (consts, vector_step, scalar_step, pool_step, ln_var, ln_rstd, xn_ready, xnT_psum,
         xnT_ready, x_new, proj_psum, lo_ready, stack_ready, v_ready, max_psum, max_read,
         negmaxT_psum, aug_ready, score_psum, probs_ready, pv_done,
         pvT_ready, pv_psum, spread_ready, heads_ready, headsT_psum,
         headsT_ready, out_psum, tok_psum, tok_read, tok_square, tok_power, tok_stacked,
         add_ready, mixed_ready, qc_ready, gate_psum, gate_scored, aside_psum, aside_ready,
         aside_scalar, aside_pool) = [S[n] for n in names]

        def r32(ap):
            return ap.bitcast(F32R)

        def half(b):
            return slice(b * SEQ, (b + 1) * SEQ)

        def col(t):
            return slice(t * P, (t + 1) * P)

        def chain(sig, eng):
            def then(ins):
                k = len(sig.made)
                ins.then_inc(*sig.tick(k))
                eng.wait_ge(sig.sem, k + 1)
            return then

        moe0 = STAGES > 2
        if moe0:
            ring0 = sb("ring0", [P, 4, 3, P])
            pick0 = sb("pick0", [P, PAIRS0, P], BF16)
            combA = sb("combA", [P, B * SEQ], BF16)
            combB = sb("combB", [P, B * SEQ], BF16)
            m0_load = [plain(f"experts0_loaded_{k}") for k in range(4)]
            m0_gu, m0_silu, m0_prod, m0_hidden, m0_down, m0_whigh, m0_wlow = [
                plain("experts0_" + n) for n in ("gate_up", "silu", "product", "hidden", "down", "weights_high",
                                                 "weights_low")]
            silu0, prod0, hidden0 = probs[:, 0], probs[:, 1], probs[:, 2]
        wide = probs[:, :, :, :].rearrange("p a b n -> p (a b) n")
        wide4 = lambda i: wide[:, 4 + i, :]
        tq4d = tq[:, 0:2, :].rearrange("p a (t n) -> p (a t) n", n=P)
        hpre = tq[:, :, :].rearrange("p a n -> p (a n)")[:, 0:CH * B * (SEQ + LEFT)]\
            .rearrange("p (c n) -> p c n", c=CH * B)
        high = qst[:, :, :, :].rearrange("p b g n -> p (b g n)")
        low = kst[:, :, :, :].rearrange("p b g n -> p (b g n)")
        X_AT = 3 * B * SEQ
        w_high = lambda k, a, c: high[:, (2 * k + a) * F1 + c.start:(2 * k + a) * F1 + c.stop]
        w_low = lambda k, a, c: low[:, (2 * k + a) * F1 + c.start:(2 * k + a) * F1 + c.stop]
        x_high, x_low = high[:, X_AT:X_AT + B * SEQ], low[:, X_AT:X_AT + B * SEQ]
        iota = sb("iota", [P, P])
        comb = sb("comb", [P, TILES, E0])
        moe1 = STAGES > 5
        if moe1:
            ring1 = sb("ring1", [P, 2, 3, F1])
            m1_load = [plain(f"experts1_loaded_{k}") for k in range(2)]
            (m1_gu, m1_silu, m1_prod, m1_down, m1_stat, m1_var, m1_rstd, m1_rescale, m1_scale, m1_norm,
             m1_scaled, m1_added, m1_whigh, m1_wlow) = [
                plain("experts1_" + n) for n in ("gate_up", "silu", "product", "down", "stat", "var",
                                                 "rstd", "rescale", "scale", "norm", "scaled", "added",
                                                 "weights_high", "weights_low")]
            m1_eps = plain("experts1_eps")
            m1_gamma = [plain(f"gamma_loaded_{k}") for k in range(2)]
            epsilon = sb("epsilon", [P, TPB])
            gammarow = sb("gammarow", [P, 2, D])
            hidden1, silu1, norm1 = wide[:, 0:4], wide[:, 4:6], wide[:, 6:8]
            shift1 = sb("shift1", [P, TILES])
            mv1 = sb("mv1", [P, TILES, 2])
            st1 = sb("st1", [P, TILES, 6])
            ve1 = sb("ve1", [P, TILES])
            rs1 = sb("rs1", [P, TILES])
            sc1 = sb("sc1", [P, TILES])
            combT1 = headsT[0:E1, :, :].rearrange("p b n -> p (b n)")

        moe2 = STAGES > 8
        if moe2:
            tri = sb("tri", [P, P], BF16)
            onesB = sb("onesB", [P, P], BF16)
            onehotB = sb("onehotB", [P, TILES, E2], BF16)
            own_slot = sb("own_slot", [P, E2])
            diag2 = heads[:, :, :, :].rearrange("p b t d -> p (b t) d")
            slot_rows = headsT[:, :, :].rearrange("p b n -> p (b n)")
            disp2 = [wide[:, 2 * k:2 * k + 2, :].rearrange("p a (t n) -> p (a t) n", n=CAP) for k in range(2)]
            combT2 = [wide[:, 4 + 2 * k:6 + 2 * k, :].rearrange("p a n -> p (a n)") for k in range(2)]
            hid2 = [pvT[:, k, :] for k in range(2)]
            ring2 = ring1
            m2_load = [plain(f"experts2_loaded_{k}") for k in range(2)]

        block = ctx.enter_context(nc.Block())

        @block.sync
        def _(sp):
            def load(s):
                for n, (_, stage, rows) in tiles.items():
                    if stage == s:
                        src = dram[n].partition_broadcast(P) if rows else dram[n]
                        sp.dma_start(W[n][:], src).then_inc(s_load[s], 16)
            sp.dma_start(X[:, :, :], dram["x"].rearrange("b (t p) d -> p (b t) d", p=P)).then_inc(s_x, 16)
            for s in range(-1, min(STAGES, LATE)):
                load(s)

            def load_pairs(i, first=False):
                for k in range(4):
                    positive_wait(sp, m0_down, 8 * i + 2 * k - 4 if not first else 2 * k - 4)
                    sp.dma_start(ring0[:, k, :, :], dram["stream0"][4 * i + k + 1]).then_inc(m0_load[k], 16)
            if moe0:
                sp.dma_start(ring0[:, 3, :, :], dram["stream0"][0]).then_inc(m0_load[3], 16)
                load_pairs(0, True)
                with sp.Fori(1, PAIRS0 // 4) as i:
                    load_pairs(i)

            def load_expert(e, k, first=False):
                positive_wait(sp, m1_down, 8 * e - 8 if not first else 0)
                sp.dma_start(ring1[:, k, :, :], dram["stream1"][e]).then_inc(m1_load[k], 16)
                positive_wait(sp, m1_scaled, 2 * e - 2 if not first else 0)
                sp.dma_start(gammarow[:, k, :], dram["gamma"][e].partition_broadcast(P)).then_inc(m1_gamma[k], 16)
            if moe1:
                load_expert(0, 0, True)
                load_expert(1, 1, True)
                with sp.Fori(1, E1 // 2) as i:
                    for k in range(2):
                        load_expert(2 * i + k, k)
            if STAGES > LATE:
                sp.wait_ge(*x_new.at(4, 1))
            for s in range(LATE, STAGES):
                load(s)
            if moe2:
                sp.wait_ge(*x_new.at(5, 1))
                for e in range(E2):
                    if e >= 2:
                        sp.wait_ge(*aside_psum.at(8, "expert", e - 2))
                    sp.dma_start(ring2[:, e % 2, 0:2, :], dram["stream2"][e]).then_inc(m2_load[e % 2], 16)
            for b in range(B):
                sp.wait_ge(*x_new.at(STAGES - 1, b))
                sp.dma_start(out.rearrange("b (t p) d -> p b t d", p=P)[:, b],
                             X[:, TPB * b:TPB * (b + 1), :]).then_inc(s_out, 16)
            sp.wait_ge(s_out, 16 * B)

        @block.tensor
        def _(pe):
            mm, tr = nc.tensor.matmul, nc.tensor.transpose

            def ln(s, b):
                slot = banks.take(pe, xnT_ready, (s, b), ("xnT", s, b))
                if (s, b) == (0, 0):
                    pe.wait_ge(*consts.at("ident"))
                pe.wait_ge(*xn_ready.at(s, b))
                for t in range(TPB):
                    last = tr(BANK[:, slot, col(t)], xn[:, TPB * b + t, :], ident[:, :])
                last.then_inc(*xnT_psum.tick(s, b))

            def tokens_by(dst, w, b, first=True, last=True, src=None):
                for t in range(TPB):
                    n = w.shape[-1]
                    ins = mm(dst[:, t * n:(t + 1) * n], xnT[:, b * SEQ + t * P:b * SEQ + (t + 1) * P], w,
                             start=True, stop=True)
                return ins

            def context_kv(s, b):
                cfg = ATTN[s]
                if cfg.get("heads") == "norm":
                    slot = pairs.take(pe, tok_read, (s, b, "k"), ("tok", s, b, "k"))
                    mm(PAIR[0:NCTX, 2 * slot, 0:D], W["ctxT"][:, b, 0:NCTX], W[f"wk_{s}"][:, :],
                       start=True, stop=True).then_inc(*tok_psum.tick(s, b, "k"))
                else:
                    slot = pairs.take(pe, stack_ready, (s, b, "k", 0), ("stack", s, b, "k", 0))
                    for g in range(QUADS):
                        last = mm(PAIR[:, 2 * slot, g * NCTXP:(g + 1) * NCTXP], W[f"wk_{s}"][:, g, :],
                                  W["ctxT"][:, b, :], start=True, stop=True)
                    last.then_inc(*proj_psum.tick(s, b, "k", 0))
                slot = banks.take(pe, v_ready, (s, b), ("v", s, b))
                mm(BANK[0:NCTX, slot, 0:D], W["ctxT"][:, b, 0:NCTX], W[f"wv_{s}"][:, :],
                   start=True, stop=True).then_inc(*proj_psum.tick(s, b, "v"))

            def stack(s, b, which, gp):
                slot = pairs.take(pe, stack_ready, (s, b, which, gp), ("stack", s, b, which, gp))
                cfg = ATTN[s]
                if cfg.get("heads"):
                    pe.wait_ge(*tok_stacked.at(s, b, which))
                    if cfg["cross"] and which == "k":
                        for g in range(QUADS):
                            last = tr(PAIR[:, 2 * slot, g * NCTXP:g * NCTXP + NCTX], tokst[0:NCTX, 0, col(g)],
                                      ident[0:NCTX, 0:NCTX])
                    else:
                        for r in range(2):
                            for t in range(TPB):
                                last = tr(PAIR[:, 2 * slot + r, col(t)], tokst[:, t, col(2 * gp + r)], ident[:, :])
                else:
                    w, x = W[f"w{which}_{s}"], xnT[:, half(b)]
                    if cfg.get("mixed") and which == "q":
                        pe.wait_ge(*mixed_ready.at(s))
                        pe.wait_ge(*qc_ready.at(s, b))
                        w, x = W[f"cross_{s}"], tq[:, b, :]
                    for r in range(2):
                        last = mm(PAIR[:, 2 * slot + r, :], w[:, 2 * gp + r, :], x, start=True, stop=True)
                last.then_inc(*proj_psum.tick(s, b, which, gp))

            def prepare(s, b, step):
                kind = step[0]
                if kind == "ln":
                    pe.wait_ge(*loaded(s))
                    pe.wait_ge(*consts.at("all"))
                    ln(s, b)
                    pe.wait_ge(*xnT_ready.at(s, b))
                elif kind == "context":
                    context_kv(s, b)
                elif kind == "values":
                    slot = banks.take(pe, v_ready, (s, b), ("v", s, b))
                    tokens_by(BANK[:, slot, :], W[f"wv_{s}"][:, :], b).then_inc(*proj_psum.tick(s, b, "v"))
                elif kind == "mix":
                    slot = banks.take(pe, qc_ready, (s, b), ("qc", s, b))
                    mm(BANK[:, slot, :], W[f"wq_{s}"][:, :], xnT[:, half(b)], start=True, stop=True)\
                        .then_inc(*proj_psum.tick(s, b, "qc"))
                elif kind == "tokens":
                    slot = pairs.take(pe, tok_read, (s, b, step[1]), ("tok", s, b, step[1]))
                    tokens_by(PAIR[:, 2 * slot, :], W[f"w{step[1]}_{s}"][:, :], b)\
                        .then_inc(*tok_psum.tick(s, b, step[1]))
                elif kind == "stack":
                    stack(s, b, step[1], step[2])
                elif kind == "max":
                    maxima(s, b, *step[1:])
                elif kind == "aug":
                    maxima_back(s, b, step[1])

            def maxima(s, b, *at):
                cfg = ATTN[s]
                t, jp = at[-2:]
                slot = pairs.take(pe, max_read, (s, b, *at), ("max", s, b, *at))
                if at == (0, 0) or at == (0, 0, 0):
                    pe.wait_ge(*stack_ready.at(s, b, "q", 1))
                    pe.wait_ge(*(spread_ready.at(s, b) if cfg["cross"] else stack_ready.at(s, b, "k", 1)))
                    if cfg.get("add"):
                        pe.wait_ge(*add_ready.at(s))
                for r in range(2):
                    rows = slice(ROWS * (2 * jp + r), ROWS * (2 * jp + r + 1))
                    if cfg["cross"]:
                        g = 2 * jp + r
                        last = mm(PAIR[:, 2 * slot + r, 0:PER * NCTXP], r32(qst[:, b, g, col(t)]),
                                  r32(kst[:, b, g, SPREAD:SPREAD + PER * NCTXP]),
                                  start=True, stop=not cfg.get("add"), skip_group_check=True)
                    else:
                        mm(PAIR[:, 2 * slot + r, 0:(t + 1) * P], r32(qst[rows, b, at[0], col(t)]),
                           r32(kst[rows, b, at[0], 0:(t + 1) * P]), start=True, stop=False, skip_group_check=True)
                for r in range(2):
                    if cfg.get("add"):
                        a = addq[:, b if cfg["add"] == "bias" else 0, t, :]
                        last = mm(PAIR[:, 2 * slot + r, 0:PER * NCTXP], r32(identR[:, :]),
                                  r32(a.unsqueeze(1).to_broadcast([P, PER, NCTXP])),
                                  start=False, stop=True, skip_group_check=True)
                    elif not cfg["cross"]:
                        last = mm(PAIR[:, 2 * slot + r, col(t)], identB[:, :], above[:, :],
                                  start=False, stop=True, skip_group_check=True)
                last.then_inc(*max_psum.tick(s, b, *at))

            def maxima_back(s, b, g):
                slot = banks.take(pe, aug_ready, (s, b, g), ("aug", s, b, g))
                pe.wait_ge(*max_read.at(s, b, *((TPB - 1, g // 2) if ATTN[s]["cross"] else (g, TPB - 1, 1))))
                for t in range(TPB):
                    last = tr(BANK[:, slot, col(t)], negmax[:, t, g, :], ident[:, :])
                last.then_inc(*negmaxT_psum.tick(s, b, g))

            def scores(s, b, u):
                cfg = ATTN[s]
                g, kb, jp = u
                slot = pairs.take(pe, probs_ready, (s, b, *u), ("score", s, b, *u))
                if kb == 0 and jp == 0:
                    if cfg.get("sigmoid"):
                        pe.wait_ge(*stack_ready.at(s, b, "q", 1))
                        pe.wait_ge(*stack_ready.at(s, b, "k", 0))
                    else:
                        pe.wait_ge(*aug_ready.at(s, b, g))
                keys = slice(0, NCTX) if cfg["cross"] else col(kb)
                n, m = SEQ - kb * P, NCTX if cfg["cross"] else P
                for r in range(2):
                    rows = slice(ROWS * (2 * jp + r), ROWS * (2 * jp + r + 1))
                    last = mm(PAIR[0:m, 2 * slot + r, 0:n], r32(kst[rows, b, g, keys]),
                              r32(qst[rows, b, g, kb * P:SEQ]), start=True,
                              stop=cfg["cross"] and not cfg.get("add"), skip_group_check=True)
                for r in range(2):
                    dst = PAIR[0:m, 2 * slot + r, 0:n]
                    if not cfg["cross"]:
                        last = mm(PAIR[:, 2 * slot + r, 0:P], identB[:, :], below[:, :], start=False, stop=True,
                                  skip_group_check=True)
                    elif cfg.get("add"):
                        ab = b if cfg["add"] == "bias" else 0
                        for part in range(2 if cfg["add"] == "bias" else 1):
                            last = mm(dst, r32(identR[0:NCTX, 0:NCTX]), r32(addT[:, ab, part, :]), start=False,
                                      stop=part == (cfg["add"] == "bias"), skip_group_check=True)
                last.then_inc(*score_psum.tick(s, b, *u))

            def weighted(s, b, u, n):
                cfg = ATTN[s]
                g, kb, jp = u
                if kb == 0 and jp == 0:
                    sums.take(pe, pvT_ready, (s, b, g), ("pv", s, b, g))
                slot = sums.made[("pv", s, b, g)]
                pe.wait_ge(*probs_ready.at(s, b, *u))
                if g == 0 and kb == 0 and jp == 0:
                    pe.wait_ge(*v_ready.at(s, b))
                m = NCTX if cfg["cross"] else P
                for r in range(2):
                    j = 2 * jp + r
                    c = (PER * g + j) * (HD + 1)
                    last = mm(BANK[ROWS * j:ROWS * (j + 1), slot, kb * P:SEQ], vaug[0:m, b, kb, c:c + ROWS],
                              probs[0:m, n % 4, r, 0:SEQ - kb * P], start=kb == 0,
                              stop=cfg["cross"] or kb == TPB - 1, skip_group_check=True)
                last.then_inc(*pv_done.tick(s, b, *u))

            def weighted_back(s, b, g):
                slot = pairs.take(pe, heads_ready, (s, b, g), ("pv", s, b, g))
                pe.wait_ge(*pvT_ready.at(s, b, g))
                for t in range(TPB):
                    last = tr(PAIR[:, 2 * slot, col(t)], pvT[:, g % 2, col(t)], ident[:, :])
                last.then_inc(*pv_psum.tick(s, b, g))

            count = [0]

            def attend(s, b, step):
                us = units(s)
                i = len(us) if step == ("finish",) else us.index(step)
                if i == 0:
                    scores(s, b, us[0])
                if i + 1 < len(us):
                    scores(s, b, us[i + 1])
                if i:
                    weighted(s, b, us[i - 1], count[0])
                    count[0] += 1
                if i == len(us):
                    weighted_back(s, b, QUADS - 1)
                    output(s, b)
                elif step[0] and step[1:] == (0, 1):
                    weighted_back(s, b, step[0] - 1)

            def output(s, b):
                slot = banks.take(pe, headsT_ready, (s, b), ("headsT", s, b))
                pe.wait_ge(*heads_ready.at(s, b, QUADS - 1))
                for t in range(TPB):
                    last = tr(BANK[:, slot, col(t)], heads[:, b, t, :], ident[:, :])
                last.then_inc(*headsT_psum.tick(s, b))
                slot = banks.take(pe, x_new, (s, b), ("out", s, b))
                pe.wait_ge(*headsT_ready.at(s, b))
                bias = f"bo_{s}" in W
                for t in range(TPB):
                    if bias:
                        mm(BANK[:, slot, col(t)], ones[0:1, :], W[f"bo_{s}"][:, :], start=True, stop=False)
                    last = mm(BANK[:, slot, col(t)], headsT[:, b, col(t)], W[f"wo_{s}"][:, :],
                              start=not bias, stop=True)
                last.then_inc(*out_psum.tick(s, b))

            def pair_attention(s=0):
                pe.wait_ge(*loaded(-1))
                pe.wait_ge(*loaded(0))
                for w in "qv":
                    slot = banks.take(pe, aside_ready, (0, "V" + w), ("V", w))
                    mm(BANK[:, slot, 0:D], W[f"A_{w}"][:, :], W[f"BT_{w}"][:, :], start=True, stop=True)\
                        .then_inc(*aside_psum.tick(0, "V" + w))
                slot = banks.take(pe, aside_ready, (0, "norm"), ("norm",))
                pe.wait_ge(*consts.at("ident"))
                pe.wait_ge(*aside_ready.at(0, "squares"))
                mm(BANK[:, slot, 0:2], ones[:, :], small[:, 0, 0:2], start=True, stop=True)\
                    .then_inc(*aside_psum.tick(0, "norm"))
                for b in range(B):
                    ln(s, b)
                for b in range(B):
                    slot = pairs.take(pe, tok_read, (0, b, "k"), ("tok", 0, b, "q"))
                    pe.wait_ge(*xnT_ready.at(0, b))
                    pe.wait_ge(*aside_ready.at(0, "W"))
                    tokens_by(PAIR[:, 2 * slot, :], W["dirT_q"][:, :], b)
                    tokens_by(PAIR[:, 2 * slot + 1, :], W["kwT_0"][:, :], b).then_inc(*tok_psum.tick(0, b, "q"))
                    slot = banks.take(pe, v_ready, (0, b), ("v", 0, b))
                    tokens_by(BANK[:, slot, :], W["dirT_v"][:, :], b).then_inc(*proj_psum.tick(0, b, "v"))
                for b in range(B):
                    output(s, b)

            def three(dst, left, right, start, stop):
                for n, (i, j) in enumerate(((0, 0), (0, 1), (1, 0))):
                    last = mm(dst, r32(left[i]), r32(right[j]), start=start and n == 0, stop=stop and n == 2,
                              skip_group_check=True)
                return last

            def experts0(s=2):
                for reader, step in pairs.readers:
                    pe.wait_ge(*reader.at(*step))
                for b in range(B):
                    pe.wait_ge(*xnT_ready.at(s, b))
                    last = tokens_by(PAIR[:, 2, b * TPB * E0:(b + 1) * TPB * E0], W["gate0"][:, :], b)
                last.then_inc(*gate_psum.tick(s))
                pe.wait_ge(*aside_ready.at(s, "low"))

                def gate_up(i, k, h, shared=False):
                    positive_wait(pe, m0_hidden, 8 * i + 2 * k + h + 1)
                    for a in range(2):
                        w = slice((2 * k + a) * P, (2 * k + a + 1) * P)
                        last = three(PAIR[:, 3 * h + a, :], (high[:, w], low[:, w]),
                                     (x_high[:, half(h)], x_low[:, half(h)]), True, True)
                    if not shared:
                        pick = pick0[:, 4 * i + k, :]
                        mm(PAIR[:, 3 * h + 2, :], pick, combA[:, half(h)], start=True, stop=False)
                        last = mm(PAIR[:, 3 * h + 2, :], pick, combB[:, half(h)], start=False, stop=True)
                    last.then_inc(m0_gu, 1)

                def down(i, k, h, shared=False):
                    pe.wait_ge(m0_hidden, 8 * i + 2 * k + h + 3)
                    for t in range(TPB):
                        last = mm(BANK[:, h, col(t)], hidden0[:, h, col(t)], ring0[:, k, 2, :],
                                  start=shared and t == 0, stop=False, skip_group_check=True)
                    last.then_inc(m0_down, 1)

                def four_pairs(i, first=False):
                    for k in range(4):
                        pe.wait_ge(m0_wlow, 4 * i + k + 2)
                        for h in range(2):
                            gate_up(i, k, h)
                            if k == 0:
                                down(i - 1, 3, h, shared=first)
                            else:
                                down(i, k - 1, h)

                pe.wait_ge(m0_wlow, 1)
                gate_up(-1, 3, 0, shared=True)
                gate_up(-1, 3, 1, shared=True)
                pe.wait_ge(*aside_ready.at(s, "doubled"))
                for t in range(TILES):
                    last = tr(PAIR[:, 2 + 3 * (t // TPB), col(t % TPB)], tq4d[:, t, :], ident[:, :])
                last.then_inc(*aside_psum.tick(s, "comb"))
                pe.wait_ge(*aside_ready.at(s, "comb"))
                pe.wait_ge(*aside_ready.at(s, "parts"))
                pe.wait_ge(*aside_pool.at(s, "pick", 1))
                four_pairs(0, True)
                with pe.Fori(1, PAIRS0 // 4) as i:
                    four_pairs(i)
                for h in range(2):
                    down(PAIRS0 // 4 - 1, 3, h)
                pairs.readers[:] = [(x_new, (s, 1))] * 3
                banks.readers[:] = sums.readers[:] = [(x_new, (s, 1))]

            def experts1(s=5):
                for reader, step in pairs.readers:
                    pe.wait_ge(*reader.at(*step))
                for b in range(B):
                    pe.wait_ge(*xnT_ready.at(s, b))
                    last = tokens_by(PAIR[:, 4, b * TPB * E1:(b + 1) * TPB * E1], W["wr"][:, :], b)
                last.then_inc(*gate_psum.tick(s))
                pe.wait_ge(*aside_ready.at(s, "low"))

                def gate_up(e, k, h, fb):
                    positive_wait(pe, m1_prod, 8 * e + 4 * h + fb - 1)
                    if h == 0 and fb == 0:
                        pe.wait_ge(m1_wlow, 2 * e + 2)
                    for a in range(2):
                        last = three(PAIR[:, 2 * (fb % 2) + a, :], (w_high(k, a, col(fb)), w_low(k, a, col(fb))),
                                     (x_high[:, half(h)], x_low[:, half(h)]), True, True)
                    last.then_inc(m1_gu, 1)

                def down(e, k, h, fb):
                    pe.wait_ge(m1_prod, 8 * e + 4 * h + fb + 1)
                    if fb == 0:
                        positive_wait(pe, m1_norm, 2 * e + h - 1)
                    for t in range(TPB):
                        last = mm(BANK[:, h, col(t)], hidden1[:, fb, col(t)], ring1[:, k, 2, col(fb)],
                                  start=(fb == 0 and t == 0), stop=(fb == 3), skip_group_check=True)
                    last.then_inc(m1_down, 1)

                def expert(e, k, first=False):
                    for h in range(2):
                        for fb in range(4):
                            gate_up(e, k, h, fb)
                            if fb >= 2:
                                down(e, k, h, fb - 2)
                            elif h:
                                down(e, k, 0, fb + 2)
                            elif not first:
                                down(e - 1, 1 - k, 1, fb + 2)
                expert(0, 0, True)
                with pe.Fori(1, E1 // 2) as i:
                    expert(2 * i - 1, 1)
                    expert(2 * i, 0)
                pe.wait_ge(*aside_ready.at(s, "combined"))
                for t in range(TILES):
                    last = tr(PAIR[0:E1, 4 + t // TPB, col(t % TPB)], comb[:, t, 0:E1], ident[:, :])
                last.then_inc(*aside_psum.tick(s, "comb"))
                expert(E1 - 1, 1)
                pe.wait_ge(*aside_ready.at(s, "comb"))
                for t in range(TILES):
                    last = mm(PAIR[:, 4 + t // TPB, col(t % TPB)], combT1[:, col(t)], W["beta"][:, :],
                              start=True, stop=True)
                last.then_inc(*aside_psum.tick(s, "beta"))
                down(E1 - 1, 1, 1, 2)
                down(E1 - 1, 1, 1, 3)
                pairs.readers[:] = [(x_new, (s, 1))] * 3
                banks.readers[:] = sums.readers[:] = [(x_new, (s, 1))]

            def state_space(s=6):
                for b in range(B):
                    pe.wait_ge(*xnT_ready.at(s, b))
                    slot = pairs.take(pe, aside_scalar, (s, "h", b), ("h", s, b))
                    for c in range(CH):
                        last = mm(PAIR[:, 2 * slot + c, :], W["inw"][:, col(c)], xnT[:, half(b)], start=True, stop=True)
                    last.then_inc(*aside_psum.tick(s, "h", b))
                slot = pairs.take(pe, aside_ready, (s, "scanned"), ("xp", s))
                slot2 = sums.take(pe, aside_ready, (s, "scanned"), ("hsum", s))
                for b in range(B):
                    pe.wait_ge(*aside_scalar.at(s, "silu", b))
                    rows = slice(ROWS * b, ROWS * b + NSTATE)
                    for c in range(CH):
                        hb = wide4(b * CH + c)
                        for a in range(2):
                            mm(PAIR[rows, 2 * slot + a, :], W["xpw"][:, c, a * NSTATE:(a + 1) * NSTATE], hb,
                               start=c == 0, stop=c == CH - 1, skip_group_check=True)
                        last = mm(BANK[rows, slot2, :], ones[:, 0:NSTATE], hb, start=c == 0, stop=c == CH - 1,
                                  skip_group_check=True)
                    last.then_inc(*aside_psum.tick(s, "xp", b))
                for b in range(B):
                    slot = banks.take(pe, x_new, (s, b), ("out", s, b))
                    if b == 0:
                        pe.wait_ge(*aside_ready.at(s, "scanned"))
                    rows = slice(ROWS * b, ROWS * b + NSTATE)
                    for t in range(TPB):
                        one = slice(ROWS * b, ROWS * b + 1)
                        mm(BANK[:, slot, col(t)], ones[one, :], W["bo_6"][one, :], start=True, stop=False)
                        last = mm(BANK[:, slot, col(t)], tokst[rows, 2, col(t)], W["ssmo"][rows, :],
                                  start=False, stop=True)
                    last.then_inc(*out_psum.tick(s, b))

            def dispatch_experts(s=8):
                slot = pairs.take(pe, gate_scored, (s,), ("gate", s))
                for b in range(B):
                    pe.wait_ge(*xnT_ready.at(s, b))
                    last = tokens_by(PAIR[:, 2 * slot, b * TPB * E2:(b + 1) * TPB * E2], W["wg"][:, :], b)
                last.then_inc(*gate_psum.tick(s))
                slot = pairs.take(pe, aside_ready, (s, "slots"), ("cumsum", s))
                pe.wait_ge(*aside_ready.at(s, "onehot"))
                pe.wait_ge(*aside_pool.at(s, "triangle"))
                for t in range(TILES):
                    for u in range(t + 1):
                        last = mm(PAIR[:, 2 * slot, t * E2:(t + 1) * E2],
                                  (tri if u == t else onesB)[:, :], onehotB[:, u, :],
                                  start=u == 0, stop=u == t)
                last.then_inc(*aside_psum.tick(s, "cumsum"))
                slot = pairs.take(pe, aside_ready, (s, "rows"), ("rows", s))
                pe.wait_ge(*aside_ready.at(s, "diagonal"))
                for t in range(TILES):
                    last = mm(PAIR[:, 2 * slot + t // TPB, col(t % TPB)], ones[:, :], diag2[:, t, :],
                              start=True, stop=True)
                last.then_inc(*aside_psum.tick(s, "rows"))
                outs = [banks.take(pe, x_new, (s, 0), ("out", s, 0)), sums.take(pe, x_new, (s, 1), ("out", s, 1))]

                def gather(e):
                    slot = pairs.take(pe, aside_scalar, (s, "gathered", e), ("gather", s, e))
                    pe.wait_ge(*aside_ready.at(s, "dispatch", e))
                    for t in range(TILES):
                        last = mm(PAIR[:, 2 * slot, 0:CAP], xn[:, t, :], disp2[e % 2][:, t, :],
                                  start=t == 0, stop=t == TILES - 1)
                    last.then_inc(*aside_psum.tick(s, "gathered", e))

                def ffn_up(e):
                    slot = pairs.take(pe, aside_scalar, (s, "hidden", e), ("up", s, e))
                    pe.wait_ge(m2_load[e % 2], 16 * (e // 2 + 1))
                    pe.wait_ge(*aside_scalar.at(s, "gathered", e))
                    for fb in range(F2 // P):
                        last = mm(PAIR[:, 2 * slot, col(fb)], ring2[:, e % 2, 0, col(fb)], tokst[:, e % 2, 0:CAP],
                                  start=True, stop=True)
                    last.then_inc(*aside_psum.tick(s, "hidden", e))

                def ffn_down(e):
                    slot = pairs.take(pe, aside_scalar, (s, "expert", e), ("down", s, e))
                    pe.wait_ge(*aside_scalar.at(s, "hidden", e))
                    for fb in range(F2 // P):
                        last = mm(PAIR[:, 2 * slot, 0:D], hid2[e % 2][:, col(fb)], ring2[:, e % 2, 1, col(fb)],
                                  start=fb == 0, stop=fb == F2 // P - 1)
                    last.then_inc(*aside_psum.tick(s, "expert", e))

                def combine(e):
                    pe.wait_ge(*aside_scalar.at(s, "expert", e))
                    for t in range(TILES):
                        last = mm(BANK[:, outs[t // TPB], col(t % TPB)], combT2[e % 2][:, col(t)],
                                  tokst[:, e % 2, P:P + D],
                                  start=(e == 0 and t % TPB == 0), stop=e == E2 - 1, skip_group_check=True)
                    last.then_inc(*aside_psum.tick(s, "combined", e))

                gather(0)
                for e in range(E2):
                    ffn_up(e)
                    if e:
                        combine(e - 1)
                    if e + 1 < E2:
                        gather(e + 1)
                    ffn_down(e)
                combine(E2 - 1)

            def linear(s, b, step):
                if step == ("ln",):
                    pe.wait_ge(*loaded(s))
                    ln(s, b)
                    return
                pe.wait_ge(*xnT_ready.at(s, b))
                slot = pairs.take(pe, aside_scalar, (s, "xv", b), ("xv", s, b))
                mm(PAIR[0:32, 2 * slot, :], W["vr_11"][:, :], xnT[:, half(b)], start=True, stop=True)\
                    .then_inc(*aside_psum.tick(s, "xv", b))
                slot = banks.take(pe, x_new, (s, b), ("out", s, b))
                for t in range(TPB):
                    dst = BANK[:, slot, col(t)]
                    mm(dst, ones[0:1, :], W["b_11"][:, :], start=t == 0, stop=False, skip_group_check=True)
                    mm(dst, xnT[:, b * SEQ + t * P:b * SEQ + (t + 1) * P], W["w_11"][:, :], start=False, stop=False,
                       skip_group_check=True)
                pe.wait_ge(*aside_scalar.at(s, "xv", b))
                for t in range(TPB):
                    last = mm(BANK[:, slot, col(t)], tokst[0:32, b, col(t)], W["c_11"][:, :], start=False, stop=True,
                              skip_group_check=True)
                last.then_inc(*out_psum.tick(s, b))

            stages = {0: pair_attention, 2: experts0, 5: experts1, 6: state_space, 8: dispatch_experts}
            for kind, s, b, step in order:
                if kind == "stage":
                    stages[s]()
                elif kind == "prepare":
                    prepare(s, b, step)
                elif kind == "linear":
                    linear(s, b, step)
                elif kind == "ln":
                    pe.wait_ge(*loaded(s))
                    ln(s, b)
                else:
                    attend(s, b, step)

        @block.scalar
        def _(act):
            def act_fn(out, in_, func, bias=0.0, scale=1.0):
                return nc.scalar.activation(out, in_, func, bias=bias, scale=scale)

            def ln_copy(s, b):
                act.wait_ge(*xnT_psum.at(s, b))
                act_fn(xnT[:, half(b)], BANK[:, banks.of("xnT", s, b), :], ACT.Copy).then_inc(*xnT_ready.tick(s, b))

            def low_parts(s, b, which, gp):
                n = len(lo_ready.made)
                if n >= 2:
                    act.wait_ge(*stack_ready.at(*list(lo_ready.made)[n - 2]))
                act.wait_ge(*proj_psum.at(s, b, which, gp))
                slot = pairs.of("stack", s, b, which, gp)
                i = 0 if which == "q" else 1
                scale = W["lorows"][:, i:i + 1]
                bias = ATTN[s].get("bias") and not (s == 9 and which == "q")
                if bias and (n == 0 or not any(k[0] == s for k in lo_ready.made)):
                    act.wait_ge(*aside_ready.at(s, "blo"))
                if ATTN[s]["cross"] and which == "k":
                    w = NCTX if ATTN[s].get("heads") else NCTXP
                    src = PAIR[:, 2 * slot, 0:QUADS * NCTXP].rearrange("p (g n) -> p g n", g=QUADS)[:, :, 0:w]
                    dst = lopart[:, n % 2, 0, 0:QUADS * NCTXP].rearrange("p (g n) -> p g n", g=QUADS)[:, :, 0:w]
                    gs = range(QUADS)
                else:
                    src, dst = PAIR[:, 2 * slot:2 * slot + 2, :], lopart[:, n % 2, :, :]
                    gs = range(2 * gp, 2 * gp + 2)
                if bias:
                    for k, g in enumerate(gs):
                        last = act_fn(r32(dst[:, k, :]), src[:, k, :], ACT.Identity,
                                      bias=blo[:, i, g:g + 1], scale=scale)
                else:
                    last = act_fn(r32(dst), src, ACT.Identity, scale=scale)
                last.then_inc(*lo_ready.tick(s, b, which, gp))

            def root(s, b, which):
                act.wait_ge(*tok_square.at(s, b, which))
                if ATTN[s]["cross"]:
                    m, n = (NCTX, H) if which == "k" else (P, TPB * H)
                    out, src = small[0:m, 1, 0:n], small[0:m, 2, 0:n]
                else:
                    out, src = small[:, 1, :], small[:, 0, :]
                act_fn(out, src, ACT.Sqrt).then_inc(*tok_power.tick(s, b, which))

            history = []
            copies = []

            def weighted_copy(s, b, g):
                act.wait_ge(*pv_done.at(s, b, *[u for u in units(s) if u[0] == g][-1]))
                if len(copies) >= 2:
                    act.wait_ge(*pv_psum.at(*copies[-2]))
                act_fn(pvT[:, g % 2, :], BANK[:, sums.of("pv", s, b, g), :], ACT.Copy)\
                    .then_inc(*pvT_ready.tick(s, b, g))
                copies.append((s, b, g))

            def attend(s, b, step):
                cfg = ATTN[s]
                if step == ("finish",):
                    weighted_copy(s, b, QUADS - 1)
                    output(s, b)
                    return
                m = NCTX if cfg["cross"] else P
                func = ACT.Sigmoid if cfg.get("sigmoid") else ACT.Exp
                n = len(history)
                if n >= 4:
                    act.wait_ge(*pv_done.at(*history[n - 4]))
                act.wait_ge(*score_psum.at(s, b, *step))
                slot = pairs.of("score", s, b, *step)
                w = SEQ - step[1] * P
                act_fn(probs[0:m, n % 4, :, 0:w], PAIR[0:m, 2 * slot:2 * slot + 2, 0:w], func, scale=SCALE)\
                    .then_inc(*probs_ready.tick(s, b, *step))
                history.append((s, b, *step))
                if step[0] and step[1:] == (0, 0):
                    weighted_copy(s, b, step[0] - 1)

            def output(s, b):
                act.wait_ge(*headsT_psum.at(s, b))
                act_fn(headsT[:, b, :], BANK[:, banks.of("headsT", s, b), :], ACT.Copy)\
                    .then_inc(*headsT_ready.tick(s, b))

            def prepare(s, b, step):
                kind = step[0]
                if kind == "ln":
                    act.wait_ge(*loaded(-1))
                    act.wait_ge(*loaded(s))
                    if ATTN[s].get("mixed") and b == 0:
                        act_fn(small[:, 0, 0:1], W["gate_9"][:, :], ACT.Sigmoid).then_inc(*aside_scalar.tick(s, "gate"))
                    ln_copy(s, b)
                elif kind == "context":
                    if not ATTN[s].get("heads"):
                        low_parts(s, b, "k", 0)
                elif kind == "mix":
                    act.wait_ge(*proj_psum.at(s, b, "qc"))
                    act_fn(tq[:, b, :], BANK[:, banks.of("qc", s, b), :], ACT.Identity, bias=W["bqc_9"][:, 0:1])\
                        .then_inc(*qc_ready.tick(s, b))
                elif kind == "root":
                    root(s, b, step[1])
                elif kind == "stack":
                    low_parts(s, b, step[1], step[2])
                elif kind == "spread":
                    act.wait_ge(*stack_ready.at(s, b, "k", 0))
                    for j in range(PER):
                        c = SPREAD + j * NCTXP
                        last = act_fn(r32(kst[:, b, :, c:c + NCTXP]), kst[:, b, :, 0:NCTXP], ACT.Identity,
                                      scale=W["headrows"][:, j:j + 1])
                    last.then_inc(*spread_ready.tick(s, b))

            def pair_attention(s=0):
                for b in range(B):
                    ln_copy(s, b)
                act.wait_ge(*aside_ready.at(s, "centred"))
                act_fn(tq[:, 1, 0:256], tq[:, 0, 0:256], ACT.Exp, scale=SCALE).then_inc(*aside_scalar.tick(s, "exp"))
                for b in range(B):
                    output(s, b)

            def experts0(s=2):
                act.wait_ge(*xnT_ready.at(s, 1))
                act_fn(r32(x_high), xnT[:, :], ACT.Copy).then_inc(*aside_scalar.tick(s, "high"))
                act.wait_ge(*gate_psum.at(s))
                act_fn(tq[:, 0, :], PAIR[:, 2, :], ACT.Sigmoid).then_inc(*gate_scored.tick(s))

                def silu(i, k, h):
                    positive_wait(act, m0_hidden, 8 * i + 2 * k + h + 1)
                    act.wait_ge(m0_gu, 8 * i + 2 * k + h + 3)
                    act_fn(silu0[:, h, :], PAIR[:, 3 * h, :], ACT.Silu).then_inc(m0_silu, 1)


                def weights_high(i, k):
                    act.wait_ge(m0_load[k], 16 * i + (32 if k == 3 else 16))
                    positive_wait(act, m0_gu, 8 * i + 2 * k - 4)
                    act_fn(r32(high[:, 2 * k * P:2 * (k + 1) * P]),
                           ring0[:, k, 0:2, :].rearrange("p a n -> p (a n)"), ACT.Copy).then_inc(m0_whigh, 1)

                def four_pairs(i, last=False):
                    for k in range(4):
                        silu(i, k, 0)
                        if k < 3:
                            weights_high(i, k + 1)
                        elif not last:
                            weights_high(i + 1, 0)
                        silu(i, k, 1)

                weights_high(-1, 3)
                weights_high(0, 0)
                silu(-1, 3, 0)
                silu(-1, 3, 1)
                four_pairs(0)
                with act.Fori(1, PAIRS0 // 4 - 1) as i:
                    four_pairs(i)
                four_pairs(PAIRS0 // 4 - 1, True)

            def experts1(s=5):
                act.wait_ge(*aside_ready.at(s, "centred"))
                act_fn(tq[:, 1, 0:TILES * E1], tq[:, 0, 0:TILES * E1], ACT.Exp)\
                    .then_inc(*aside_scalar.tick(s, "exp"))
                act.wait_ge(*xnT_ready.at(s, 1))
                act_fn(r32(x_high), xnT[:, :], ACT.Copy).then_inc(*aside_scalar.tick(s, "high"))

                def silu(e, h, fb):
                    u = 8 * e + 4 * h + fb
                    act.wait_ge(m1_gu, u + 1)
                    positive_wait(act, m1_prod, u - 1)
                    act_fn(silu1[:, fb % 2, :], PAIR[:, 2 * (fb % 2), :], ACT.Silu).then_inc(m1_silu, 1)

                def weights_high(e, k, a, loads, first=False):
                    if a == 0:
                        act.wait_ge(m1_load[k], loads)
                        positive_wait(act, m1_down, 8 * e - 8 if not first else 0)
                    act_fn(r32(w_high(k, a, slice(0, F1))), ring1[:, k, a, :], ACT.Copy).then_inc(m1_whigh, 1)

                def normed(n, h):
                    act.wait_ge(m1_scale, n + 1)
                    for t in range(TPB):
                        k = TPB * h + t
                        last = act_fn(norm1[:, h, col(t)], BANK[:, h, col(t)], ACT.Identity,
                                      bias=shift1[:, k:k + 1], scale=sc1[:, k:k + 1])
                    last.then_inc(m1_norm, 1)

                def expert(e, first=False, prepare=None):
                    for h in range(2):
                        for fb in range(4):
                            silu(e, h, fb)
                            if fb == 1 and not first:
                                normed(2 * e + h - 2, h)
                            if prepare and (h, fb) in ((0, 2), (1, 0)):
                                weights_high(e + 1, prepare[0], h, prepare[1])

                for a in range(2):
                    weights_high(0, 0, a, 16, True)
                expert(0, True, (1, 16))
                with act.Fori(1, E1 // 2) as i:
                    expert(2 * i - 1, prepare=(0, 16 * i + 16))
                    expert(2 * i, prepare=(1, 16 * i + 16))
                expert(E1 - 1)
                for h in range(2):
                    normed(2 * E1 - 2 + h, h)

            def state_space(s=6):
                act.wait_ge(*loaded(s))
                for b in range(B):
                    act.wait_ge(*aside_psum.at(s, "h", b))
                    slot = pairs.of("h", s, b)
                    for c in range(CH):
                        last = act_fn(hpre[:, b * CH + c, LEFT:LEFT + SEQ], PAIR[:, 2 * slot + c, :], ACT.Identity,
                                      bias=W["inb"][:, c:c + 1])
                    last.then_inc(*aside_scalar.tick(s, "h", b))
                for b in range(B):
                    act.wait_ge(*aside_ready.at(s, "conv", b))
                    for c in range(CH):
                        last = act_fn(wide4(b * CH + c), wide[:, b * CH + c, :], ACT.Silu, bias=W["convb"][:, c:c + 1])
                    last.then_inc(*aside_scalar.tick(s, "silu", b))
                for b in range(B):
                    act.wait_ge(*aside_psum.at(s, "xp", b))
                    rows = slice(ROWS * b, ROWS * b + NSTATE)
                    slot = pairs.of("xp", s)
                    last = act_fn(tokst[rows, 1, :], PAIR[rows, 2 * slot + 1, :], ACT.Silu, bias=W["xpb"][rows, 1:2])
                last.then_inc(*aside_scalar.tick(s, "input"))
                for b in range(B):
                    rows = slice(ROWS * b, ROWS * b + NSTATE)
                    last = act_fn(tokst[rows, 0, :], PAIR[rows, 2 * slot, :], ACT.Exp, bias=W["xpb"][rows, 0:1])
                last.then_inc(*aside_scalar.tick(s, "exp"))
                act.wait_ge(*aside_scalar.at(s, "exp"))
                for b in range(B):
                    rows = slice(ROWS * b, ROWS * b + NSTATE)
                    last = act_fn(tokst[rows, 3, :], tokst[rows, 0, :], ACT.Exp, scale=-1.0)
                last.then_inc(*aside_scalar.tick(s, "decay"))

            def dispatch_experts(s=8):
                act.wait_ge(*aside_ready.at(s, "centred"))
                act_fn(tq[:, 1, 0:TILES * E2], tq[:, 0, 0:TILES * E2], ACT.Exp)\
                    .then_inc(*aside_scalar.tick(s, "exp"))

                def gathered(e):
                    act.wait_ge(*aside_psum.at(s, "gathered", e))
                    act_fn(tokst[:, e % 2, 0:CAP], PAIR[:, 2 * pairs.of("gather", s, e), 0:CAP], ACT.Copy)\
                        .then_inc(*aside_scalar.tick(s, "gathered", e))

                gathered(0)
                for e in range(E2):
                    act.wait_ge(*aside_psum.at(s, "hidden", e))
                    act_fn(hid2[e % 2], PAIR[:, 2 * pairs.of("up", s, e), :], ACT.Relu)\
                        .then_inc(*aside_scalar.tick(s, "hidden", e))
                    if e + 1 < E2:
                        gathered(e + 1)
                    act.wait_ge(*aside_psum.at(s, "expert", e))
                    if e >= 2:
                        act.wait_ge(*aside_psum.at(s, "combined", e - 2))
                    act_fn(tokst[:, e % 2, P:P + D], PAIR[:, 2 * pairs.of("down", s, e), 0:D], ACT.Copy)\
                        .then_inc(*aside_scalar.tick(s, "expert", e))

            def linear(s, b, step):
                if step == ("ln",):
                    ln_copy(s, b)
                    return
                act.wait_ge(*aside_psum.at(s, "xv", b))
                act_fn(tokst[0:32, b, :], PAIR[0:32, 2 * pairs.of("xv", s, b), :], ACT.Copy)\
                    .then_inc(*aside_scalar.tick(s, "xv", b))

            stages = {0: pair_attention, 2: experts0, 5: experts1, 6: state_space, 8: dispatch_experts}
            for kind, s, b, step in order:
                if kind == "stage":
                    stages[s]()
                elif kind == "prepare":
                    prepare(s, b, step)
                elif kind == "linear":
                    linear(s, b, step)
                elif kind == "ln":
                    ln_copy(s, b)
                else:
                    attend(s, b, step)

        @block.vector
        def _(v):
            V = nc.vector
            then = chain(vector_step, v)

            def ln(s, b):
                ts = range(TPB * b, TPB * (b + 1))
                if s == 0:
                    v.wait_ge(s_x, 16)
                else:
                    v.wait_ge(*x_new.at(s - 1, b))
                for t in ts:
                    last = V.bn_stats(stats[:, t, :], X[:, t, :])
                then(last)
                for t in ts:
                    last = V.bn_aggr(meanvar[:, t, :], stats[:, t, :])
                last.then_inc(*ln_var.tick(s, b))
                v.wait_ge(*ln_var.at(s, b))
                v.wait_ge(*ln_rstd.at(s, b))
                for t in ts:
                    last = V.tensor_scalar(xn[:, t, :], X[:, t, :], meanvar[:, t, 0:1], rstd[:, t:t + 1],
                                           ALU.subtract, ALU.mult)
                last.then_inc(*xn_ready.tick(s, b))

            def stack(s, b, which, gp):
                v.wait_ge(*lo_ready.at(s, b, which, gp))
                n = (lo_ready.at(s, b, which, gp)[1] - 1) % 2
                slot = pairs.of("stack", s, b, which, gp)
                cfg = ATTN[s]
                if cfg["cross"] and which == "k":
                    w = NCTX if cfg.get("heads") else NCTXP
                    src = PAIR[:, 2 * slot, 0:QUADS * NCTXP].rearrange("p (g n) -> p g n", g=QUADS)[:, :, 0:w]
                    lo = lopart[:, n, 0, 0:QUADS * NCTXP].rearrange("p (g n) -> p g n", g=QUADS)[:, :, 0:w]
                    dst, gs = kst[:, b, :, 0:w], range(QUADS)
                else:
                    src, lo = PAIR[:, 2 * slot:2 * slot + 2, :], lopart[:, n, :, :]
                    dst, gs = (qst if which == "q" else kst)[:, b, 2 * gp:2 * gp + 2, :], range(2 * gp, 2 * gp + 2)
                bias = cfg.get("bias") and not (s == 9 and which == "q")
                if bias:
                    for k, g in enumerate(gs):
                        last = V.scalar_tensor_tensor(r32(dst[:, k, :]), src[:, k, :], W[f"b{which}_{s}"][:, g:g + 1],
                                                      lo[:, k, :], ALU.add, ALU.subtract)
                elif which == "k":
                    last = V.scalar_tensor_tensor(r32(dst), src, W["kone"][:, 0:1], lo, ALU.add, ALU.subtract)
                else:
                    last = V.tensor_tensor(r32(dst), src, lo, ALU.subtract)
                last.then_inc(*stack_ready.tick(s, b, which, gp))

            def values(s, b):
                cfg = ATTN[s]
                v.wait_ge(*proj_psum.at(s, b, "v"))
                slot = banks.of("v", s, b)
                m, nt = (NCTX, 1) if cfg["cross"] else (P, TPB)
                src = BANK[0:m, slot, 0:nt * D].rearrange("p (t h d) -> p t h d", t=nt, h=H)
                dst = vaug[0:m, b, 0:nt, 0:H * (HD + 1)].rearrange("p t (h d) -> p t h d", h=H)[:, :, :, 0:HD]
                if cfg.get("bias"):
                    bv = W[f"bv_{s}"][0:m, :].rearrange("p (h d) -> p h d", h=H)
                    for t in range(nt):
                        last = V.tensor_tensor(dst[:, t], src[:, t], bv, ALU.add)
                else:
                    for t in range(nt):
                        last = V.tensor_copy(dst[:, t], src[:, t])
                last.then_inc(*v_ready.tick(s, b))

            def maxima(s, b, *at):
                v.wait_ge(*max_psum.at(s, b, *at))
                slot = pairs.of("max", s, b, *at)
                t, jp = at[-2:]
                c = 2 * jp * ROWS + AUG
                if ATTN[s]["cross"]:
                    src = PAIR[:, 2 * slot:2 * slot + 2, 0:PER * NCTXP]\
                        .rearrange("p r (j n) -> p r j n", j=PER)[:, :, :, 0:NCTX]
                    dst = negmax[:, t, 2 * jp:2 * jp + 2, AUG::ROWS]
                else:
                    src, dst = PAIR[:, 2 * slot:2 * slot + 2, 0:(t + 1) * P], negmax[:, t, at[0], c:c + ROWS + 1:ROWS]
                V.tensor_reduce(dst, src, AX, ALU.max, negate=True).then_inc(*max_read.tick(s, b, *at))

            def maxima_back(s, b, g):
                v.wait_ge(*negmaxT_psum.at(s, b, g))
                V.tensor_tensor(r32(qst[:, b, g, :]), qst[:, b, g, :], BANK[:, banks.of("aug", s, b, g), :],
                                ALU.add).then_inc(*aug_ready.tick(s, b, g))

            divided = []

            def normalise(s, b, g):
                cfg = ATTN[s]
                v.wait_ge(*pv_psum.at(s, b, g))
                O = PAIR[:, 2 * pairs.of("pv", s, b, g), :].rearrange("p (t j d) -> p t j d", t=TPB, j=PER)
                dst = heads[:, b, :, g * PER * HD:(g + 1) * PER * HD].rearrange("p t (j d) -> p t j d", j=PER)
                if cfg.get("sigmoid"):
                    V.tensor_copy(dst, O[:, :, :, 0:HD]).then_inc(*heads_ready.tick(s, b, g))
                    return
                if divided:
                    v.wait_ge(*heads_ready.at(*divided[-1]))
                divided.append((s, b, g))
                then(V.reciprocal(rden[:, :, :], O[:, :, :, HD:HD + 1].rearrange("p t j d -> p t (j d)")))
                if cfg.get("hscale"):
                    hs = W[f"hs_{s}"][:, PER * g:PER * (g + 1)].unsqueeze(1).to_broadcast([P, TPB, PER])
                    then(V.tensor_tensor(rden[:, :, :], rden[:, :, :], hs, ALU.mult))
                V.tensor_tensor(dst, O[:, :, :, 0:HD], rden[:, :, :].unsqueeze(3).to_broadcast([P, TPB, PER, HD]),
                                ALU.mult).then_inc(*heads_ready.tick(s, b, g))

            def attend(s, b, step):
                if step == ("finish",):
                    normalise(s, b, QUADS - 1)
                    residual(s, b)
                elif step[0] and step[1:] == (0, 1):
                    normalise(s, b, step[0] - 1)

            def residual(s, b):
                v.wait_ge(*out_psum.at(s, b))
                xs = X[:, TPB * b:TPB * (b + 1), :]
                V.tensor_tensor(xs, xs, BANK[:, banks.of("out", s, b), :].rearrange("p (t d) -> p t d", d=D),
                                ALU.add).then_inc(*x_new.tick(s, b))

            def stack_tokens(dst, src, m):
                return dst.rearrange("p (h r) -> p h r", h=H)[0:m, :, 0:3 * HD].rearrange("p h (c d) -> p h c d", d=HD)

            def thrice(ap, m):
                return ap.unsqueeze(2).to_broadcast([m, H, 3, HD])

            def rope(s, b, which):
                v.wait_ge(*tok_psum.at(s, b, which))
                if which == "k":
                    v.wait_ge(*tok_stacked.at(s, b, "q"))
                src = PAIR[:, 2 * pairs.of("tok", s, b, which), :].rearrange("p (t h d) -> p t h d", t=TPB, h=H)
                q4 = lambda i: tq[:, i, :].rearrange("p (t h d) -> p t h d", t=TPB, h=H)
                hh = HD // 2
                for t in range(TPB):
                    cs = W["cos"][:, t, :].unsqueeze(1).to_broadcast([P, H, HD])
                    sn = W["sin"][:, t, :].unsqueeze(1).to_broadcast([P, H, HD])
                    V.tensor_tensor(q4(0)[:, t], src[:, t], cs, ALU.mult)
                    V.tensor_tensor(q4(1)[:, t, :, 0:hh], src[:, t, :, hh:HD], sn[:, :, 0:hh], ALU.mult)
                    last = V.tensor_tensor(q4(1)[:, t, :, hh:HD], src[:, t, :, 0:hh], sn[:, :, hh:HD], ALU.mult)
                last.then_inc(*tok_read.tick(s, b, which))
                v.wait_ge(*tok_read.at(s, b, which))
                then(V.tensor_tensor(tq[:, 2, :], tq[:, 0, :], tq[:, 1, :], ALU.add))
                then(V.tensor_tensor(tq[:, 3, :], tq[:, 2, :], tq[:, 2, :], ALU.mult))
                V.tensor_reduce(small[:, 0, :], tq[:, 3, :].rearrange("p (n d) -> p n d", d=HD), AX, ALU.add)\
                    .then_inc(*tok_square.tick(s, b, which))

            def rope_norm(s, b, which):
                q4 = lambda i: tq[:, i, :].rearrange("p (t h d) -> p t h d", t=TPB, h=H)
                nw = W[f"n{which}_{s}"][:, :].unsqueeze(1).to_broadcast([P, TPB * H, HD])
                then(V.tensor_tensor(tq[:, 0, :].rearrange("p (n d) -> p n d", d=HD),
                                     tq[:, 2, :].rearrange("p (n d) -> p n d", d=HD), nw, ALU.mult))
                v.wait_ge(*tok_power.at(s, b, which))
                then(V.tensor_scalar(small[:, 2, :], small[:, 1, :], float(np.float32(HD ** -0.5)), 1e-6,
                                     ALU.mult, ALU.add))
                then(V.reciprocal(small[:, 3, :], small[:, 2, :]))
                if which == "k":
                    v.wait_ge(*proj_psum.at(s, b, "q", 1))
                elif b:
                    v.wait_ge(*proj_psum.at(s, b - 1, "k", 1))
                for t in range(TPB):
                    r = small[:, 3, t * H:(t + 1) * H].unsqueeze(2).unsqueeze(3).to_broadcast([P, H, 3, HD])
                    last = V.tensor_tensor(stack_tokens(tokst[:, t, :], None, P), thrice(q4(0)[:, t], P), r, ALU.mult)
                last.then_inc(*tok_stacked.tick(s, b, which))

            def head_views(which):
                m, nt = (NCTX, 1) if which == "k" else (P, TPB)
                n = nt * H
                return (m, nt, n, lambda i: tq[0:m, i, 0:nt * D].rearrange("p (n d) -> p n d", d=HD),
                        lambda a: a.unsqueeze(2).to_broadcast([m, n, HD]))

            def head_moments(s, b, which):
                m, nt, n, q, over = head_views(which)
                v.wait_ge(*tok_psum.at(s, b, which))
                src = PAIR[0:m, 2 * pairs.of("tok", s, b, which), 0:nt * D].rearrange("p (n d) -> p n d", d=HD)
                then(V.tensor_reduce(small[0:m, 0, 0:n], src, AX, ALU.add))
                then(V.tensor_scalar(small[0:m, 1, 0:n], small[0:m, 0, 0:n], 1.0 / HD, None, ALU.mult))
                V.tensor_tensor(q(0), src, over(small[0:m, 1, 0:n]), ALU.subtract)\
                    .then_inc(*tok_read.tick(s, b, which))
                v.wait_ge(*tok_read.at(s, b, which))
                then(V.tensor_tensor(q(1), q(0), q(0), ALU.mult))
                then(V.tensor_reduce(small[0:m, 0, 0:n], q(1), AX, ALU.add))
                V.tensor_scalar(small[0:m, 2, 0:n], small[0:m, 0, 0:n], 1.0 / HD, 1e-5, ALU.mult, ALU.add)\
                    .then_inc(*tok_square.tick(s, b, which))

            def head_norm(s, b, which):
                m, nt, n, q, over = head_views(which)
                v.wait_ge(*tok_power.at(s, b, which))
                then(V.reciprocal(small[0:m, 3, 0:n], small[0:m, 1, 0:n]))
                then(V.tensor_tensor(q(2), q(0), over(small[0:m, 3, 0:n]), ALU.mult))
                gm = W[f"g{which}_{s}"][0:m, :].unsqueeze(1).to_broadcast([m, n, HD])
                then(V.tensor_tensor(q(3), q(2), gm, ALU.mult))
                if which == "k" and b:
                    v.wait_ge(*proj_psum.at(s, b - 1, "q", 1))
                elif which == "q":
                    v.wait_ge(*proj_psum.at(s, b, "k", 0))
                bt = W[f"b{which}_{s}"][0:m, :].unsqueeze(1).unsqueeze(2).to_broadcast([m, H, 3, HD])
                for t in range(nt):
                    last = V.tensor_tensor(stack_tokens(tokst[:, t, :], None, m),
                                           thrice(q(3)[:, t * H:(t + 1) * H, :], m), bt, ALU.add)
                last.then_inc(*tok_stacked.tick(s, b, which))

            def added(s):
                cfg = ATTN[s]
                v.wait_ge(*consts.at("all"))
                if cfg["add"] == "mask":
                    V.tensor_scalar(r32(addq[:, 0, :, :]), W["maskq"][:, :, :], 0.0, -BIG, ALU.is_equal, ALU.mult)
                    V.tensor_scalar(r32(addT[:, 0, 0, :]), W["maskT"][:, :], 0.0, -BIG, ALU.is_equal, ALU.mult)\
                        .then_inc(*add_ready.tick(s))
                    return
                root = float(np.float32(HD ** 0.5))
                padT, padq = small[0:NCTX, 0, 0:B], small[:, 1:4, :].rearrange("p a n -> p (a n)")[:, 0:B * NCTXP]
                V.tensor_scalar(padT, W["padT"][:, :], -BIG, None, ALU.mult)
                then(V.tensor_scalar(padq, W["padq"][:, :], -BIG, None, ALU.mult))
                for b in range(B):
                    V.scalar_tensor_tensor(r32(addq[:, b, :, :]), W["biasq"][:, b, :, :], root,
                                           padq[:, b * NCTXP:(b + 1) * NCTXP].unsqueeze(1)
                                           .to_broadcast([P, TPB, NCTXP]), ALU.mult, ALU.add)
                    then(V.tensor_scalar(tq[0:NCTX, 2 + b, :], W["biasT"][:, b, :], root, padT[:, b:b + 1],
                                         ALU.mult, ALU.add))
                    then(V.tensor_copy(r32(addT[:, b, 0, :]), tq[0:NCTX, 2 + b, :]))
                    last = V.tensor_tensor(r32(addT[:, b, 1, :]), tq[0:NCTX, 2 + b, :], addT[:, b, 0, :], ALU.subtract)
                last.then_inc(*add_ready.tick(s))

            def once(s):
                cfg = ATTN[s]
                v.wait_ge(*loaded(-1))
                v.wait_ge(*loaded(s))
                if s == 1:
                    v.wait_ge(*consts.at("all"))
                    then(V.tensor_copy(r32(identR[:, :]), ident[:, :]))
                    then(V.tensor_copy(identB[:, :], ident[:, :]))
                if cfg.get("add"):
                    added(s)
                if cfg.get("bias"):
                    for i, n in enumerate("qk"):
                        if f"b{n}_{s}" in W:
                            last = V.tensor_scalar(blo[:, i, :], W[f"b{n}_{s}"][:, :], W["lorows"][:, i:i + 1], None,
                                                   ALU.mult)
                    last.then_inc(*aside_ready.tick(s, "blo"))
                if cfg.get("mixed"):
                    v.wait_ge(*aside_scalar.at(s, "gate"))
                    A, M = W[f"cross_{s}"], W[f"shift_{s}"]
                    then(V.tensor_tensor(A[:, :, :], A[:, :, :], M[:, :, :], ALU.subtract))
                    V.scalar_tensor_tensor(A[:, :, :].rearrange("p g n -> p (g n)"),
                                           A[:, :, :].rearrange("p g n -> p (g n)"), small[:, 0, 0:1],
                                           M[:, :, :].rearrange("p g n -> p (g n)"), ALU.mult, ALU.add)\
                        .then_inc(*mixed_ready.tick(s))

            def prepare(s, b, step):
                kind, cfg = step[0], ATTN[s]
                if kind == "ln":
                    ln(s, b)
                    if b == 0:
                        once(s)
                elif kind == "context":
                    if cfg.get("heads"):
                        head_moments(s, b, "k")
                        values(s, b)
                    else:
                        values(s, b)
                        stack(s, b, "k", 0)
                elif kind == "values":
                    values(s, b)
                elif kind == "tokens":
                    (head_moments if cfg["cross"] else rope)(s, b, step[1])
                elif kind == "root":
                    (head_norm if cfg["cross"] else rope_norm)(s, b, step[1])
                elif kind == "stack":
                    stack(s, b, step[1], step[2])
                elif kind == "max":
                    maxima(s, b, *step[1:])
                elif kind == "aug":
                    maxima_back(s, b, step[1])

            def pair_attention(s=0):
                v.wait_ge(*loaded(-1))
                v.wait_ge(*loaded(0))
                for i, w in enumerate("qv"):
                    v.wait_ge(*aside_psum.at(0, "V" + w))
                    V.tensor_tensor(W[f"dirT_{w}"][:, :], W[f"dirT_{w}"][:, :], BANK[:, banks.of("V", w), 0:D],
                                    ALU.add).then_inc(*aside_ready.tick(0, "V" + w))
                    v.wait_ge(*aside_ready.at(0, "V" + w))
                    V.tensor_tensor(tq[:, i, 0:D], W[f"dirT_{w}"][:, :], W[f"dirT_{w}"][:, :], ALU.mult)
                then(V.tensor_copy(tq[:, 2, 0:D], W["dirT_v"][:, :]))
                for i in range(2):
                    last = V.tensor_reduce(small[:, 0, i:i + 1], tq[:, i, 0:D], AX, ALU.add)
                last.then_inc(*aside_ready.tick(0, "squares"))
                v.wait_ge(*aside_psum.at(0, "norm"))
                V.tensor_copy(small[:, 1, 0:2], BANK[:, banks.of("norm"), 0:2]).then_inc(*aside_ready.tick(0, "norm"))
                v.wait_ge(*aside_pool.at(0, "norm"))
                then(V.tensor_scalar(small[:, 3, 0:2], small[:, 2, 0:2], 1e-8, None, ALU.add))
                then(V.reciprocal(small[:, 0, 2:4], small[:, 3, 0:2]))
                for i, w in enumerate("qv"):
                    last = V.tensor_tensor(small[:, 0, 4 + i:5 + i], small[:, 0, 2 + i:3 + i], W[f"mag_{w}"][:, :],
                                           ALU.mult)
                then(last)
                for i, w in enumerate("qv"):
                    last = V.tensor_scalar(W[f"dirT_{w}"][:, :], W[f"dirT_{w}"][:, :], small[:, 0, 4 + i:5 + i], None,
                                           ALU.mult)
                last.then_inc(*aside_ready.tick(0, "W"))
                for b in range(B):
                    ln(s, b)
                bias = lambda n: W[f"b{n}_0"][:, :].unsqueeze(1).to_broadcast([P, TPB, D])
                td = lambda ap: ap.rearrange("p (t d) -> p t d", d=D)
                for b in range(B):
                    v.wait_ge(*tok_psum.at(0, b, "q"))
                    slot = pairs.of("tok", 0, b, "q")
                    V.tensor_tensor(td(probs[:, 0, b, :]), td(PAIR[:, 2 * slot, :]), bias("q"), ALU.add)
                    V.tensor_tensor(td(probs[:, 1, b, :]), td(PAIR[:, 2 * slot + 1, :]), bias("k"), ALU.add)\
                        .then_inc(*tok_read.tick(0, b, "k"))
                    v.wait_ge(*proj_psum.at(0, b, "v"))
                    V.tensor_tensor(td(probs[:, 2, b, :]), td(BANK[:, banks.of("v", 0, b), :]), bias("v"), ALU.add)\
                        .then_inc(*v_ready.tick(0, b))
                v.wait_ge(*v_ready.at(0, 1))
                N = TPB * H
                for i in range(B):
                    for j in range(B):
                        then(V.tensor_tensor(tq[:, 2, :], probs[:, 0, i, :], probs[:, 1, j, :], ALU.mult))
                        last = V.tensor_reduce(tq[:, 3, (2 * i + j) * N:(2 * i + j + 1) * N],
                                               tq[:, 2, :].rearrange("p (n d) -> p n d", d=HD), AX, ALU.add)
                        then(last)
                for i in range(B):
                    last = V.tensor_tensor(small[:, i, :], tq[:, 3, 2 * i * N:(2 * i + 1) * N],
                                           tq[:, 3, (2 * i + 1) * N:(2 * i + 2) * N], ALU.max)
                then(last)
                for i in range(B):
                    for j in range(B):
                        c = slice((2 * i + j) * N, (2 * i + j + 1) * N)
                        last = V.tensor_tensor(tq[:, 0, c], tq[:, 3, c], small[:, i, :], ALU.subtract)
                last.then_inc(*aside_ready.tick(0, "centred"))
                v.wait_ge(*aside_scalar.at(0, "exp"))
                for i in range(B):
                    last = V.tensor_tensor(small[:, i, :], tq[:, 1, 2 * i * N:(2 * i + 1) * N],
                                           tq[:, 1, (2 * i + 1) * N:(2 * i + 2) * N], ALU.add)
                then(last)
                then(V.reciprocal(small[:, 2:4, :], small[:, 0:2, :]))
                for i in range(B):
                    for j in range(B):
                        c = slice((2 * i + j) * N, (2 * i + j + 1) * N)
                        last = V.tensor_tensor(tq[:, 2, c], tq[:, 1, c], small[:, 2 + i, :], ALU.mult)
                then(last)
                for i in range(B):
                    for j in range(B):
                        c = slice((2 * i + j) * N, (2 * i + j + 1) * N)
                        last = V.tensor_tensor(tq[:, 3 + j, :].rearrange("p (n d) -> p n d", d=HD),
                                               probs[:, 2, j, :].rearrange("p (n d) -> p n d", d=HD),
                                               tq[:, 2, c].unsqueeze(2).to_broadcast([P, N, HD]), ALU.mult)
                    then(last)
                    V.tensor_tensor(heads[:, i].rearrange("p t d -> p (t d)"), tq[:, 3, :], tq[:, 4, :], ALU.add)\
                        .then_inc(*heads_ready.tick(0, i, QUADS - 1))
                    v.wait_ge(*heads_ready.at(0, i, QUADS - 1))
                for b in range(B):
                    residual(s, b)

            between = []

            def turn():
                if between:
                    between.pop(0)()

            def one_hots(idx, n, upto):
                acc = tq[:, 2, 0:TILES * n].rearrange("p (t e) -> p t e", e=n)
                eq = tq[:, 3, 0:TILES * n].rearrange("p (t e) -> p t e", e=n)
                io = iota[:, 0:n].unsqueeze(1).to_broadcast([P, TILES, n])
                for k in range(upto):
                    i = idx[:, :, k:k + 1].to_broadcast([P, TILES, n])
                    then(V.tensor_tensor(eq if k else acc, io, i, ALU.is_equal))
                    if k:
                        then(V.tensor_tensor(acc, acc, eq, ALU.add))
                    turn()
                return acc

            def best(values8, index8, as_float, src, n):
                for t in range(TILES):
                    last = V.max(values8[:, t, :], src[:, t * n:(t + 1) * n])
                then(last)
                turn()
                for t in range(TILES):
                    last = V.max_index(index8[:, t, :], values8[:, t, :], src[:, t * n:(t + 1) * n])
                then(last)
                turn()
                then(V.tensor_copy(as_float, index8))

            v8 = lambda i: small[:, i, :].rearrange("p (t k) -> p t k", k=8)
            u8 = lambda i: small[:, i, :].bitcast(U32).rearrange("p (t k) -> p t k", k=8)

            def softmax_rows(s, n):
                bank = 4 if s == 5 else 2 * pairs.of("gate", s)
                v.wait_ge(*gate_psum.at(s))
                g = lambda ap: ap.rearrange("p (t e) -> p t e", e=n)
                wide_n = TILES * n
                src = g(PAIR[:, bank, 0:wide_n])
                logits = g(tq[:, 3, 0:wide_n])
                if s == 5:
                    V.tensor_tensor(logits, src, W["br"][:, :].unsqueeze(1).to_broadcast([P, TILES, n]), ALU.add)\
                        .then_inc(*gate_scored.tick(s))
                else:
                    V.tensor_copy(logits, src).then_inc(*gate_scored.tick(s))
                v.wait_ge(*gate_scored.at(s))
                then(V.tensor_reduce(small[:, 0, 0:TILES], logits, AX, ALU.max))
                V.tensor_tensor(g(tq[:, 0, 0:wide_n]), logits,
                                small[:, 0, 0:TILES].unsqueeze(2).to_broadcast([P, TILES, n]), ALU.subtract)\
                    .then_inc(*aside_ready.tick(s, "centred"))
                if s == 5:
                    v.wait_ge(*aside_scalar.at(s, "high"))
                    V.tensor_tensor(r32(x_low), xnT[:, :], x_high, ALU.subtract).then_inc(*aside_ready.tick(s, "low"))
                v.wait_ge(*aside_scalar.at(s, "exp"))
                then(V.tensor_reduce(small[:, 0, 0:TILES], g(tq[:, 1, 0:wide_n]), AX, ALU.add))
                then(V.reciprocal(small[:, 0, 8:8 + TILES], small[:, 0, 0:TILES]))
                then(V.tensor_tensor(g(tq[:, 4, 0:wide_n]), g(tq[:, 1, 0:wide_n]),
                                     small[:, 0, 8:8 + TILES].unsqueeze(2).to_broadcast([P, TILES, n]), ALU.mult))

            def experts0(s=2):
                v.wait_ge(*loaded(s))
                V.memset(combB[0:P // 2, :], 0.0)
                v.wait_ge(*aside_scalar.at(s, "high"))
                V.tensor_tensor(r32(x_low), xnT[:, :], x_high, ALU.subtract).then_inc(*aside_ready.tick(s, "low"))
                def unit(i, k, h, shared=False):
                    v.wait_ge(m0_silu, 8 * i + 2 * k + h + 3)
                    positive_wait(v, m0_down, 8 * i + 2 * k + h + 1)
                    if shared:
                        V.tensor_tensor(hidden0[:, h, :], silu0[:, h, :], PAIR[:, 3 * h + 1, :], ALU.mult)\
                            .then_inc(m0_hidden, 1)
                        return
                    V.tensor_tensor(prod0[:, h, :], silu0[:, h, :], PAIR[:, 3 * h + 1, :], ALU.mult)\
                        .then_inc(m0_prod, 1)
                    v.wait_ge(m0_prod, 8 * i + 2 * k + h + 1)
                    V.tensor_tensor(hidden0[:, h, :], prod0[:, h, :], PAIR[:, 3 * h + 2, :], ALU.mult)\
                        .then_inc(m0_hidden, 1)

                v.wait_ge(*gate_scored.at(s))
                te = lambda ap: ap.rearrange("p (t e) -> p t e", e=E0)
                then(V.tensor_tensor(te(tq[:, 4, :]), te(tq[:, 0, :]),
                                     W["gbias0"][:, :].unsqueeze(1).to_broadcast([P, TILES, E0]), ALU.add))
                then(V.tensor_reduce(small[:, 0, :], tq[:, 4, :].rearrange("p (g e) -> p g e", e=E0 // GROUPS0),
                                     AX, ALU.max))
                best(v8(1), u8(2), v8(3), small[:, 0, :], GROUPS0)
                groups = one_hots(v8(3), GROUPS0, TOPG0)
                masked = tq[:, 1, :]
                ge = lambda ap: ap.rearrange("p (g e) -> p g e", e=E0 // GROUPS0)
                then(V.tensor_tensor(ge(masked), ge(tq[:, 4, :]),
                                     tq[:, 2, 0:TILES * GROUPS0].unsqueeze(2)
                                     .to_broadcast([P, TILES * GROUPS0, E0 // GROUPS0]), ALU.mult))
                best(v8(1), u8(2), v8(3), masked, E0)
                between[:] = [lambda: unit(-1, 3, 0, True), lambda: unit(-1, 3, 1, True)]
                chosen = one_hots(v8(3), E0, TOP0)
                then(V.tensor_reduce(small[:, 0, 0:TILES], v8(1)[:, :, 0:TOP0], AX, ALU.add))
                then(V.tensor_scalar(small[:, 0, 8:8 + TILES], small[:, 0, 0:TILES], 1e-8, None, ALU.add))
                then(V.reciprocal(small[:, 0, 16:16 + TILES], small[:, 0, 8:8 + TILES]))
                then(V.tensor_tensor(te(tq[:, 3, :]), chosen, te(masked), ALU.mult))
                weights = te(tq[:, 3, :])
                over = small[:, 0, 16:16 + TILES].unsqueeze(2).to_broadcast([P, TILES, E0])
                for c in range(2):
                    last = V.tensor_tensor(tq4d[:, :, c * E0:(c + 1) * E0], weights, over, ALU.mult)
                last.then_inc(*aside_ready.tick(s, "doubled"))
                v.wait_ge(*aside_psum.at(s, "comb"))
                src = PAIR[:, 2:6:3, :]
                rest = tq[:, 2:4, :]
                h2 = lambda ap: ap.rearrange("p (a n) -> p a n", a=2)
                up = slice(P // 2, P)
                then(V.tensor_copy(h2(combA[:, :]), src))
                V.tensor_tensor(rest, src, h2(combA[:, :]), ALU.subtract).then_inc(*aside_ready.tick(s, "comb"))
                v.wait_ge(*aside_ready.at(s, "comb"))
                then(V.tensor_copy(h2(combA[up, :]), rest[up]))
                V.tensor_tensor(h2(combB[up, :]), rest[up], h2(combA[up, :]), ALU.subtract)\
                    .then_inc(*aside_ready.tick(s, "parts"))

                for k in range(4):
                    unit(0, k, 0)
                    unit(0, k, 1)
                with v.Fori(1, PAIRS0 // 4) as i:
                    for k in range(4):
                        unit(i, k, 0)
                        unit(i, k, 1)
                v.wait_ge(m0_down, 2 * PAIRS0 + 2)
                for b in range(B):
                    xs = X[:, TPB * b:TPB * (b + 1), :]
                    V.tensor_tensor(xs, xs, BANK[:, b, :].rearrange("p (t d) -> p t d", d=D), ALU.add)\
                        .then_inc(*x_new.tick(s, b))

            def experts1(s=5):
                v.wait_ge(*loaded(s))

                def hidden(e, h, fb):
                    u = 8 * e + 4 * h + fb
                    v.wait_ge(m1_silu, u + 1)
                    positive_wait(v, m1_down, u - 3)
                    V.tensor_tensor(hidden1[:, fb, :], silu1[:, fb % 2, :], PAIR[:, 2 * (fb % 2) + 1, :], ALU.mult)\
                        .then_inc(m1_prod, 1)

                def first_hidden(u):
                    return lambda: hidden(0, u // 4, u % 4)

                between[:] = [first_hidden(u) for u in range(8)]
                softmax_rows(s, E1)
                gates = tq[:, 4, 0:TILES * E1]
                turn()
                best(v8(1), u8(2), v8(3), gates, E1)
                then(V.tensor_tensor(small[:, 0, 0:TILES], v8(1)[:, :, 0], v8(1)[:, :, 1], ALU.add))
                then(V.reciprocal(small[:, 0, 8:8 + TILES], small[:, 0, 0:TILES]))
                turn()
                chosen = one_hots(v8(3), E1, 2)
                te = lambda ap: ap.rearrange("p (t e) -> p t e", e=E1)
                then(V.tensor_tensor(te(tq[:, 3, 0:TILES * E1]), chosen, te(gates), ALU.mult))
                V.tensor_tensor(comb[:, :, 0:E1], te(tq[:, 3, 0:TILES * E1]),
                                small[:, 0, 8:8 + TILES].unsqueeze(2).to_broadcast([P, TILES, E1]), ALU.mult)\
                    .then_inc(*aside_ready.tick(s, "combined"))
                while between:
                    turn()

                def moments(n, h):
                    v.wait_ge(m1_down, 4 * n + 4)
                    for t in range(TPB):
                        last = V.bn_stats(st1[:, TPB * h + t, :], BANK[:, h, col(t)])
                    last.then_inc(m1_stat, 1)

                def aggregate(n, h):
                    for t in range(TPB):
                        last = V.bn_aggr(mv1[:, TPB * h + t, :], st1[:, TPB * h + t, :])
                    last.then_inc(m1_var, 1)

                def scales(n, h, e):
                    hs = slice(TPB * h, TPB * (h + 1))
                    v.wait_ge(m1_rstd, n + 1)
                    V.tensor_tensor(sc1[:, hs], rs1[:, hs], comb[:, hs, e], ALU.mult).then_inc(m1_rescale, 1)
                    v.wait_ge(m1_rescale, n + 1)
                    V.scalar_tensor_tensor(shift1[:, hs], mv1[:, hs, 0], -1.0, sc1[:, hs], ALU.mult, ALU.mult)\
                        .then_inc(m1_scale, 1)

                def expert(e):
                    for h in range(2):
                        n = 2 * e + h
                        for fb in range(4):
                            if fb == 3:
                                v.wait_ge(m1_stat, n)
                            hidden(e, h, fb)
                            if fb == 0:
                                scales(n - 2, h, e - 1)
                            if fb == 2:
                                moments(n - 1, 1 - h)
                            if fb == 3:
                                aggregate(n - 1, 1 - h)

                moments(0, 0)
                v.wait_ge(m1_stat, 1)
                aggregate(0, 0)
                v.wait_ge(*aside_ready.at(s, "combined"))
                with v.Fori(1, E1 // 2) as i:
                    expert(2 * i - 1)
                    expert(2 * i)
                v.wait_ge(*aside_psum.at(s, "comb"))
                V.tensor_copy(combT1[:, :].rearrange("p (a n) -> p a n", a=2), PAIR[0:E1, 4:6, :])\
                    .then_inc(*aside_ready.tick(s, "comb"))
                expert(E1 - 1)
                scales(2 * E1 - 2, 0, E1 - 1)
                moments(2 * E1 - 1, 1)
                v.wait_ge(m1_stat, 2 * E1)
                aggregate(2 * E1 - 1, 1)
                scales(2 * E1 - 1, 1, E1 - 1)
                v.wait_ge(m1_added, 2 * E1)
                v.wait_ge(*aside_psum.at(s, "beta"))
                for b in range(B):
                    xs = X[:, TPB * b:TPB * (b + 1), :].rearrange("p t d -> p (t d)")
                    V.tensor_tensor(xs, xs, PAIR[:, 4 + b, :], ALU.add).then_inc(*x_new.tick(s, b))

            def state_space(s=6):
                v.wait_ge(*x_new.at(s - 1, 1))
                V.memset(hpre[:, :, 0:LEFT], 0.0).then_inc(*aside_ready.tick(s, "padding"))
                v.wait_ge(*loaded(s))
                v.wait_ge(*aside_ready.at(s, "padding"))
                for b in range(B):
                    v.wait_ge(*aside_scalar.at(s, "h", b))
                    for k in range(NCONV):
                        for c in range(CH):
                            src, dst = hpre[:, b * CH + c, k:k + SEQ], wide[:, b * CH + c, :]
                            w = W["convw"][:, c, k:k + 1]
                            if k == 0:
                                last = V.tensor_scalar(dst, src, w, None, ALU.mult)
                            else:
                                last = V.scalar_tensor_tensor(dst, src, w, dst, ALU.mult, ALU.add)
                        if k < NCONV - 1:
                            then(last)
                    last.then_inc(*aside_ready.tick(s, "conv", b))
                v.wait_ge(*aside_psum.at(s, "xp", 1))
                v.wait_ge(*aside_scalar.at(s, "input"))
                slot = sums.of("hsum", s)
                for b in range(B):
                    rows = slice(ROWS * b, ROWS * b + NSTATE)
                    last = V.tensor_tensor(tokst[rows, 1, :], tokst[rows, 1, :], BANK[rows, slot, :], ALU.mult)
                then(last)
                v.wait_ge(*aside_scalar.at(s, "decay"))
                for b in range(B):
                    rows = slice(ROWS * b, ROWS * b + NSTATE)
                    last = V.tensor_tensor_scan(tokst[rows, 2, :], tokst[rows, 3, :], tokst[rows, 1, :], 0.0,
                                                ALU.mult, ALU.add)
                last.then_inc(*aside_ready.tick(s, "scanned"))
                for b in range(B):
                    residual(s, b)

            def dispatch_experts(s=8):
                v.wait_ge(*loaded(s))
                softmax_rows(s, E2)
                gates = tq[:, 4, 0:TILES * E2]
                best(v8(1), u8(2), v8(3), gates, E2)
                onehot = one_hots(v8(3), E2, 1)
                V.tensor_copy(onehotB[:, :, :], onehot).then_inc(*aside_ready.tick(s, "onehot"))
                v.wait_ge(*aside_psum.at(s, "cumsum"))
                slot = pairs.of("cumsum", s)
                counts = PAIR[:, 2 * slot, 0:TILES * E2].rearrange("p (t e) -> p t e", e=E2)
                t3 = tq[:, 3, 0:TILES * E2].rearrange("p (t e) -> p t e", e=E2)
                then(V.tensor_tensor(t3, counts, onehot, ALU.mult))
                then(V.tensor_reduce(small[:, 0, 0:TILES], t3, AX, ALU.add))
                then(V.tensor_scalar(small[:, 0, 8:16], small[:, 0, 0:8], float(CAP), None, ALU.is_le))
                then(V.scalar_tensor_tensor(small[:, 0, 16:24], v8(3)[:, :, 0], float(CAP), small[:, 0, 0:8],
                                            ALU.mult, ALU.add))
                then(V.tensor_tensor(small[:, 0, 24:32], small[:, 0, 16:24], small[:, 0, 8:16], ALU.mult))
                V.tensor_copy(small[:, 0, 40:48], v8(1)[:, :, 0])
                V.tensor_scalar(small[:, 0, 32:40], small[:, 0, 24:32], -1.0, None, ALU.add)\
                    .then_inc(*aside_ready.tick(s, "slots"))
                v.wait_ge(*aside_ready.at(s, "slots"))
                token_slot = small[:, 0, 32:40]
                for t in range(TILES):
                    last = V.tensor_scalar(diag2[:, t, :], ident[:, :], token_slot[:, t:t + 1], None, ALU.mult)
                last.then_inc(*aside_ready.tick(s, "diagonal"))
                places = small[:, 1, :].rearrange("p (e t) -> p e t", e=E2)
                for e in range(E2):
                    last = V.tensor_scalar(places[:, e, :], token_slot, float(CAP * e), None, ALU.subtract)
                then(last)
                v.wait_ge(*aside_pool.at(s, "own"))
                v.wait_ge(*aside_psum.at(s, "rows"))
                slot = pairs.of("rows", s)
                V.tensor_copy(slot_rows.rearrange("p (a n) -> p a n", a=2), PAIR[:, 2 * slot:2 * slot + 2, :])\
                    .then_inc(*aside_ready.tick(s, "rows"))
                v.wait_ge(*aside_ready.at(s, "rows"))
                for e in range(E2):
                    if e >= 2:
                        v.wait_ge(*aside_psum.at(s, "combined", e - 2))
                    V.tensor_tensor(disp2[e % 2], iota[:, :].unsqueeze(1).to_broadcast([P, TILES, CAP]),
                                    places[:, e, :].unsqueeze(2).to_broadcast([P, TILES, CAP]), ALU.is_equal)
                    V.tensor_scalar(combT2[e % 2], slot_rows, own_slot[:, e:e + 1], None, ALU.is_equal)\
                        .then_inc(*aside_ready.tick(s, "dispatch", e))
                v.wait_ge(*aside_psum.at(s, "combined", E2 - 1))
                for b in range(B):
                    slot = (sums if b else banks).of("out", s, b)
                    for t in range(TPB):
                        k = TPB * b + t
                        last = V.scalar_tensor_tensor(X[:, k, :], BANK[:, slot, col(t)], small[:, 0, 40 + k:41 + k],
                                                      X[:, k, :], ALU.mult, ALU.add)
                    last.then_inc(*x_new.tick(s, b))

            def linear(s, b, step):
                (ln if step == ("ln",) else residual)(s, b)

            stages = {0: pair_attention, 2: experts0, 5: experts1, 6: state_space, 8: dispatch_experts}
            for kind, s, b, step in order:
                if kind == "stage":
                    stages[s]()
                elif kind == "prepare":
                    prepare(s, b, step)
                elif kind == "linear":
                    linear(s, b, step)
                elif kind == "ln":
                    ln(s, b)
                else:
                    attend(s, b, step)

        @block.gpsimd
        def _(pool):
            G = nc.gpsimd
            then = chain(pool_step, pool)
            G.memset(ident[:, :], 0.0)
            G.memset(ones[:, :], 1.0)
            G.memset(plushalf[:, :], 0.5)
            then(G.memset(minushalf[:, :], -0.5))
            G.affine_select(out=ident[:, :], in_=ident[:, :], compare_op=ALU.not_equal, fill=1.0, base=0,
                            pattern=[[-1, P]], channel_multiplier=1).then_inc(*consts.tick("ident"))

            def power(out, in_, exponent, tick):
                G.tensor_tensor(out, in_, exponent, ALU.pow).then_inc(*tick)

            def ln(s, b):
                ts = slice(TPB * b, TPB * (b + 1))
                pool.wait_ge(*ln_var.at(s, b))
                then(G.tensor_scalar(vareps[:, ts], meanvar[:, ts, 1], 1e-5, None, ALU.add))
                power(rstd[:, ts], vareps[:, ts], minushalf[:, 0:TPB], ln_rstd.tick(s, b))

            def other_constants():
                if moe1:
                    G.memset(epsilon[:, :], 1e-5)
                G.memset(above[:, :], 0.0)
                G.memset(below[:, :], 0.0)
                G.memset(negmax[:, :, :, :], 0.0)
                G.memset(vaug[:, :, :, :], 1.0)
                then(G.memset(tokst[:, :, :], 0.0))
                G.affine_select(out=above[:, :], in_=above[:, :], compare_op=ALU.is_ge, fill=-BIG, base=0,
                                pattern=[[-1, P]], channel_multiplier=1)
                G.affine_select(out=below[:, :], in_=below[:, :], compare_op=ALU.is_ge, fill=-BIG, base=0,
                                pattern=[[1, P]], channel_multiplier=-1)
                G.iota(iota[:, :], pattern=[[1, P]], base=0, channel_multiplier=0,
                       allow_small_or_imprecise_dtypes=True).then_inc(*consts.tick("all"))

            for s in range(STAGES):
                cfg = ATTN.get(s)
                if s == 0:
                    pool.wait_ge(*aside_ready.at(0, "norm"))
                    power(small[:, 2, 0:2], small[:, 1, 0:2], plushalf[:, 0:2], aside_pool.tick(0, "norm"))
                    for b in range(B):
                        ln(s, b)
                    other_constants()
                    if moe0:
                        then(G.memset(pick0[:, :, :], 0.0))
                        for r in range(2):
                            v4 = pick0[r * E0:(r + 1) * E0, :, :].rearrange("p n (a m) -> p n a m", a=2)
                            G.affine_select(out=v4, in_=v4, compare_op=ALU.not_equal, fill=1.0, base=0,
                                            pattern=[[-2, PAIRS0], [-1, 2], [0, P // 2]], channel_multiplier=1)\
                                .then_inc(*aside_pool.tick(2, "pick", r))
                            pool.wait_ge(*aside_pool.at(2, "pick", r))
                    if STAGES > 8:
                        G.memset(onesB[:, :], 1.0)
                        then(G.memset(tri[:, :], 1.0))
                        G.affine_select(out=tri[:, :], in_=tri[:, :], compare_op=ALU.is_ge, fill=0.0, base=0,
                                        pattern=[[1, P]], channel_multiplier=-1)\
                            .then_inc(*aside_pool.tick(8, "triangle"))
                        G.iota(own_slot[:, :], pattern=[[CAP, E2]], base=0, channel_multiplier=1,
                               allow_small_or_imprecise_dtypes=True).then_inc(*aside_pool.tick(8, "own"))
                    continue
                for b in range(B):
                    ln(s, b)
                    if s == 9 and b == 0 and STAGES > 10:
                        then(G.memset(tokst[:, :, :], 0.0))
                if s == 2:
                    def weights_low(i, k):
                        pool.wait_ge(m0_whigh, 4 * i + k + 2)
                        w = slice(2 * k * P, 2 * (k + 1) * P)
                        G.tensor_tensor(r32(low[:, w]), ring0[:, k, 0:2, :].rearrange("p a n -> p (a n)"), high[:, w],
                                        ALU.subtract).then_inc(m0_wlow, 1)

                    weights_low(-1, 3)
                    with pool.Fori(0, PAIRS0 // 4) as i:
                        for k in range(4):
                            weights_low(i, k)
                if s == 5:
                    pool.wait_ge(*loaded(s))

                    def weights_low(e, k, a):
                        G.tensor_tensor(r32(w_low(k, a, slice(0, F1))), ring1[:, k, a, :],
                                        w_high(k, a, slice(0, F1)), ALU.subtract).then_inc(m1_wlow, 1)

                    def rstd1(n, h):
                        hs = slice(TPB * h, TPB * (h + 1))
                        pool.wait_ge(m1_var, n + 1)
                        positive_wait(pool, m1_added, n)
                        G.tensor_tensor(ve1[:, hs], mv1[:, hs, 1], epsilon[:, 0:TPB], ALU.add).then_inc(m1_eps, 1)
                        pool.wait_ge(m1_eps, n + 1)
                        G.tensor_tensor(rs1[:, hs], ve1[:, hs], minushalf[:, 0:TPB], ALU.pow).then_inc(m1_rstd, 1)

                    def add1(n, k, h, loads):
                        pool.wait_ge(m1_gamma[k], loads)
                        pool.wait_ge(m1_norm, n + 1)
                        y = norm1[:, h, :].rearrange("p (t d) -> p t d", d=D)
                        gm = gammarow[:, k, :].unsqueeze(1).to_broadcast([P, TPB, D])
                        G.tensor_tensor(y, y, gm, ALU.mult).then_inc(m1_scaled, 1)
                        pool.wait_ge(m1_scaled, n + 1)
                        xs = X[:, TPB * h:TPB * (h + 1), :]
                        G.tensor_tensor(xs, xs, y, ALU.add).then_inc(m1_added, 1)

                    def expert(e, k, loads, first=False, last=False):
                        for h in range(2):
                            n = 2 * e + h
                            if not first and h == 0:
                                add1(n - 2, 1 - k, h, loads)
                            if not last:
                                pool.wait_ge(m1_whigh, 2 * e + h + 3)
                                weights_low(e + 1, 1 - k, h)
                            if not first and h:
                                add1(n - 2, 1 - k, h, loads)
                            if not (first and h == 0):
                                rstd1(n - 1, 1 - h)

                    for a in range(2):
                        pool.wait_ge(m1_whigh, a + 1)
                        weights_low(0, 0, a)
                    expert(0, 0, 0, first=True)
                    with pool.Fori(1, E1 // 2) as i:
                        expert(2 * i - 1, 1, 16 * i)
                        expert(2 * i, 0, 16 * i)
                    expert(E1 - 1, 1, 16 * (E1 // 2), last=True)
                    add1(2 * E1 - 2, 1, 0, 16 * (E1 // 2))
                    rstd1(2 * E1 - 1, 1)
                    add1(2 * E1 - 1, 1, 1, 16 * (E1 // 2))
    return made


def kernel(**inputs):
    import concourse.bacc as _bacc
    from concourse.bass_utils import run_bass_kernel_spmd as _run

    given = {k: np.asarray(v) for k, v in inputs.items()}
    tiles = layout(given)
    needed_by = {"stream0": 2, "stream1": 5, "gamma": 5, "stream2": 8}
    more = {k: v for k, v in streams(given).items() if STAGES > needed_by[k]}

    def program(plan):
        nc = _bacc.Bacc("TRN2", target_bir_lowering=False, num_devices=1)
        arrays = {"x": np.ascontiguousarray(given["x"])}
        arrays.update({k: a for k, (a, _, _) in tiles.items()})
        arrays.update(more)
        dram = {k: nc.dram_tensor("in_" + k, a.shape, mybir.dt.from_np(a.dtype), kind="ExternalInput").ap()
                for k, a in arrays.items()}
        out = nc.dram_tensor("out_0", (B, SEQ, D), F32, kind="ExternalOutput").ap()
        made = build(nc, tiles, None, dram, out, plan)
        return nc, made, {"in_" + k: np.ascontiguousarray(a) for k, a in arrays.items()}

    _, plan, _ = program({})
    nc, _, arrays = program(plan)
    r = _run(nc, [arrays], core_ids=[0])
    return r.results[0]["out_0"]
```
